# Optimizing a Trainium2 kernel written in Bass

```python
import numpy as np
import jax
import jax.numpy as jnp

def _softmax(x, axis=-1):
    return jax.nn.softmax(x, axis=axis)

def _gelu(x):
    return jax.nn.gelu(x, approximate=True)

def _silu(x):
    return jax.nn.silu(x)

def _sigmoid(x):
    return jax.nn.sigmoid(x)

def _layernorm(x, axis=-1, eps=1e-05):
    m = jnp.mean(x, axis=axis, keepdims=True)
    v = jnp.var(x, axis=axis, keepdims=True)
    return (x - m) / jnp.sqrt(v + eps)

def _scatter_add(tgt, idx, src, axis=0):
    return tgt.at[idx].add(src)

def _segment_sum(src, seg, n):
    return jax.ops.segment_sum(src, seg, n)
kernel_name = 'mk_flamingo_gated_d1_seqx_r4_1dc17b'

def setup_inputs(seed: int=0):
    np.random.seed(seed)
    _w = jnp.asarray

    def _rec_inputs():
        import jax
        import jax.numpy as jnp
        _rk = jax.random.key(seed)
        x = -0.0002928 + 1 * jax.random.normal(jax.random.fold_in(_rk, 1), (4, 1024, 256), jnp.float32)
        _lenS = 1024 - jax.random.randint(jax.random.fold_in(_rk, 7), (4,), 0, max(1, 1024 // 4) + 1, jnp.int32)
        _lenS2 = 77 - jax.random.randint(jax.random.fold_in(_rk, 8), (4,), 0, max(1, 77 // 4) + 1, jnp.int32)
        _ctx_1024P = jax.random.normal(jax.random.fold_in(_rk, 11), (4, 16, 256), jnp.float32)
        _ctx_1024c = jax.random.dirichlet(jax.random.fold_in(_rk, 511), 0.3 * jnp.ones((16,), jnp.float32), (4, 77))
        _ctx_1024t = jnp.einsum('bsk,bkd->bsd', _ctx_1024c, _ctx_1024P)
        _ctx_1024t = _ctx_1024t * jax.lax.rsqrt(jnp.mean(jnp.square(_ctx_1024t)) + 1e-12) * 0.953939
        ctx_1024 = -1.39393e-06 + 0.999914 * (_ctx_1024t + 0.3 * jax.random.normal(jax.random.fold_in(_rk, 611), (4, 77, 256), jnp.float32))
        _g = jax.random.normal(jax.random.fold_in(_rk, 9001), (2, 1), jnp.float32)
        _g = jnp.sign(_g) * jnp.maximum(jnp.abs(_g), 1.0) + (_g == 0) * 1.0
        g_xattn = _g[0]
        g_ffn = _g[1]
        return (x, ctx_1024, g_xattn, g_ffn)
    x, ctx_1024, g_xattn, g_ffn = _rec_inputs()

    def _L0_xattn_setup():
        import jax, jax.numpy as jnp
        import numpy as np
        import math
        HEADS = 16
        D_MODEL = 256
        D_K = D_MODEL // HEADS
        key = jax.random.key(seed)
        ks = jax.random.split(key, 11)
        B, S = (2, 512)
        s = 1.0 / math.sqrt(D_MODEL)
        return {'q': jax.random.normal(ks[0], (B, S, D_MODEL), jnp.float32), 'k': jax.random.normal(ks[1], (B, S, D_MODEL), jnp.float32), 'v': jax.random.normal(ks[2], (B, S, D_MODEL), jnp.float32), 'Wq': jax.random.normal(ks[3], (D_MODEL, D_MODEL), jnp.float32) * s, 'bq': jax.random.normal(ks[4], (D_MODEL,), jnp.float32) * s, 'Wk': jax.random.normal(ks[5], (D_MODEL, D_MODEL), jnp.float32) * s, 'bk': jax.random.normal(ks[6], (D_MODEL,), jnp.float32) * s, 'Wv': jax.random.normal(ks[7], (D_MODEL, D_MODEL), jnp.float32) * s, 'bv': jax.random.normal(ks[8], (D_MODEL,), jnp.float32) * s, 'Wo': jax.random.normal(ks[9], (D_MODEL, D_MODEL), jnp.float32) * s, 'bo': jax.random.normal(ks[10], (D_MODEL,), jnp.float32) * s}
    _L0_xattn_all = _L0_xattn_setup()
    _L0_xattn_in = {k: v for k, v in _L0_xattn_all.items() if k in ('Wq', 'bq', 'Wk', 'bk', 'Wv', 'bv', 'Wo', 'bo')}
    del _L0_xattn_all

    def _L0_ffn_setup():
        import jax, jax.numpy as jnp
        import numpy as np
        EMBED_DIM = 256
        HIDDEN_DIM = 1024
        NUM_EXPERTS = 8
        TOP_K = 2
        key = jax.random.key(seed)
        ks = jax.random.split(key, 4)
        std1 = float(np.sqrt(2.0 / EMBED_DIM))
        std2 = float(np.sqrt(2.0 / HIDDEN_DIM))
        x = jax.random.normal(ks[0], (1, 512, EMBED_DIM), dtype=jnp.float32)
        w_router = jax.random.normal(ks[1], (EMBED_DIM, NUM_EXPERTS), dtype=jnp.float32) * 0.02
        w1 = jax.random.normal(ks[2], (NUM_EXPERTS, EMBED_DIM, HIDDEN_DIM), dtype=jnp.float32) * std1
        b1 = jnp.zeros((NUM_EXPERTS, HIDDEN_DIM), dtype=jnp.float32)
        w2 = jax.random.normal(ks[3], (NUM_EXPERTS, HIDDEN_DIM, EMBED_DIM), dtype=jnp.float32) * std2
        b2 = jnp.zeros((NUM_EXPERTS, EMBED_DIM), dtype=jnp.float32)
        return {'x': x, 'w_router': w_router, 'w1': w1, 'b1': b1, 'w2': w2, 'b2': b2}
    _L0_ffn_all = _L0_ffn_setup()
    _L0_ffn_in = {k: v for k, v in _L0_ffn_all.items() if k in ('w_router', 'w1', 'b1', 'w2', 'b2')}
    del _L0_ffn_all
    return {'x': x, 'ctx_1024': ctx_1024, 'g_xattn': g_xattn, 'g_ffn': g_ffn, 'L0_xattn_Wq': _L0_xattn_in['Wq'], 'L0_xattn_bq': _L0_xattn_in['bq'], 'L0_xattn_Wk': _L0_xattn_in['Wk'], 'L0_xattn_bk': _L0_xattn_in['bk'], 'L0_xattn_Wv': _L0_xattn_in['Wv'], 'L0_xattn_bv': _L0_xattn_in['bv'], 'L0_xattn_Wo': _L0_xattn_in['Wo'], 'L0_xattn_bo': _L0_xattn_in['bo'], 'L0_ffn_w_router': _L0_ffn_in['w_router'], 'L0_ffn_w1': _L0_ffn_in['w1'], 'L0_ffn_b1': _L0_ffn_in['b1'], 'L0_ffn_w2': _L0_ffn_in['w2'], 'L0_ffn_b2': _L0_ffn_in['b2']}

def reference(x, ctx_1024, g_xattn, g_ffn, L0_xattn_Wq, L0_xattn_bq, L0_xattn_Wk, L0_xattn_bk, L0_xattn_Wv, L0_xattn_bv, L0_xattn_Wo, L0_xattn_bo, L0_ffn_w_router, L0_ffn_w1, L0_ffn_b1, L0_ffn_w2, L0_ffn_b2):
    import jax
    import jax.numpy as jnp

    def _L0_xattn_ref(q, k, v, Wq, bq, Wk, bk, Wv, bv, Wo, bo):
        import jax, jax.numpy as jnp
        import numpy as np
        import math
        HEADS = 16
        D_MODEL = 256
        D_K = D_MODEL // HEADS
        B, S, _ = q.shape

        def proj(x, W, b):
            y = x @ W.T + b
            return y.reshape(B, -1, HEADS, D_K).transpose(0, 2, 1, 3)
        qh, kh, vh = (proj(q, Wq, bq), proj(k, Wk, bk), proj(v, Wv, bv))
        scores = jnp.abs(jnp.einsum('bhsd,bhtd->bhst', qh, kh) / math.sqrt(D_K))
        attn = jax.nn.softmax(scores, axis=-1)
        out = jnp.einsum('bhst,bhtd->bhsd', attn, vh)
        concat = out.transpose(0, 2, 1, 3).reshape(B, S, D_MODEL)
        return concat @ Wo.T + bo

    def _L0_ffn_ref(x, w_router, w1, b1, w2, b2):
        import jax, jax.numpy as jnp
        import numpy as np
        EMBED_DIM = 256
        HIDDEN_DIM = 1024
        NUM_EXPERTS = 8
        TOP_K = 2
        orig_shape = x.shape
        xf = x.reshape(-1, EMBED_DIM)
        logits = xf @ w_router
        probs = jax.nn.softmax(logits, axis=-1)
        topk_w, topk_idx = jax.lax.top_k(probs, TOP_K)
        mask = jax.nn.one_hot(topk_idx, NUM_EXPERTS, dtype=xf.dtype)
        weights = jnp.sum(topk_w[..., None] * mask, axis=1)
        h = jnp.einsum('te,ieh->tih', xf, w1) + b1
        h = jax.nn.gelu(h)
        out = jnp.einsum('tih,ihe->tie', h, w2) + b2
        out = jnp.sum(out * weights[..., None], axis=1)
        return out.reshape(orig_shape)
    x = x + jnp.tanh(g_xattn[0]) * _L0_xattn_ref(_layernorm(x, axis=-1), ctx_1024, ctx_1024, L0_xattn_Wq, L0_xattn_bq, L0_xattn_Wk, L0_xattn_bk, L0_xattn_Wv, L0_xattn_bv, L0_xattn_Wo, L0_xattn_bo)
    x = x + jnp.tanh(g_ffn[0]) * _L0_ffn_ref(_layernorm(x, axis=-1), L0_ffn_w_router, L0_ffn_w1, L0_ffn_b1, L0_ffn_w2, L0_ffn_b2)
    return x

_drawn_inputs = setup_inputs


def setup_inputs(seed=0):
    import zlib

    import numpy as np

    out = dict(_drawn_inputs(seed))
    spreads = {'L0_ffn_b1': (0.0, 0.376), 'L0_ffn_b2': (0.0, 0.384)}
    factors = {}
    for name, (base, spread) in spreads.items():
        noise = np.random.default_rng([zlib.crc32(name.encode()), seed]).standard_normal(out[name].shape)
        drawn = base * np.exp(spread * noise) if base else spread * noise
        out[name] = jnp.asarray(drawn.astype(out[name].dtype))
    for name, factor in factors.items():
        out[name] = (out[name] * factor).astype(out[name].dtype)
    return out
```

```python
from contextlib import ExitStack

import concourse.bass as bass
from concourse import mybir

F32 = mybir.dt.float32
F16 = mybir.dt.float16
BF16 = mybir.dt.bfloat16
I32 = mybir.dt.int32
U32 = mybir.dt.uint32
ALU = mybir.AluOpType
ACT = mybir.ActivationFunctionType
AX = mybir.AxisListType

P = 128
BATCH, SEQ, D = 4, 1024, 256
KEYS = 77
HEADS = 16
DH = D // HEADS
E = 8
HID = 1024
TOKENS = BATCH * SEQ
LN_EPS = 1e-5

KC = D // P
HC = HID // P
PAIR = 2 * P
PAIRS = TOKENS // PAIR
PAIRS_PER_BATCH = SEQ // PAIR
HALF_HEADS = HEADS // KC
SCORES = HEADS * KEYS
QUAD = 4 * KEYS
PCH = -(-SCORES // P)
VW = DH + 1
VCOLS = 3 * VW

SLOTS = 256
SB = SLOTS // P
MAX_TILES = TOKENS * 2 // SLOTS + E - 1
REGION = TOKENS + SLOTS
ROUTED = E * REGION + SLOTS
ROW = D + E + 1
W_SCALE = 64.0


def chunk_heads(c):
    first = P * c // KEYS
    return first, min((P * c + P - 1) // KEYS, HEADS - 1) - first + 1


def chunk_rows(c):
    return min(P, SCORES - P * c)


def ready(eng, sem, item, per=1, part=None):
    value = item * per + (per if part is None else part)
    if isinstance(value, int) and value <= 0:
        return
    eng.wait_ge(sem, value)


def settled(eng, sem, item, per=1, part=None):
    ready(eng, sem, item, per, part)
    eng.nop(nofuse=True)


def exists(pair):
    return not isinstance(pair, int) or 0 <= pair < PAIRS


def pipeline(eng, step):
    for s in range(-2, 4):
        step(s // 2, s % 2)
    with eng.Fori(2, (PAIRS - 2) // 2) as m:
        for par in range(2):
            step(m, par)
    for s in range(PAIRS - 2, PAIRS + 2):
        step(s // 2, s % 2)


def item(m, par, shift):
    return 2 * m + (par + shift), m + (par + shift) // 2, (par + shift) % 2


def batch_of(m, par, shift):
    return (m + (par + shift) // 2) // (PAIRS_PER_BATCH // 2)


def setup_phase(nc, t, k):
    banks = k.banks
    with ExitStack() as ctx:
        def sb(name, shape, dt=F32):
            return ctx.enter_context(nc.sbuf_tensor(name, shape, dt))

        def sem(name):
            return ctx.enter_context(nc.semaphore(name))

        w_raw = sb("w_raw", [P, 4, KC, D])
        wk_t = sb("wk_t", [P, KC, D])
        wv_t = sb("wv_t", [P, KC, D])
        ctx_raw = sb("ctx_raw", [KEYS, BATCH, D])
        ctx_t = sb("ctx_t", [P, KC, BATCH * KEYS])
        key_t = sb("key_t", [P, KC, BATCH * KEYS])
        v_aug = sb("v_aug", [KEYS, BATCH, HEADS, VW])
        bias_rows = sb("bias_rows", [E * HC + 3 * KC, P])
        head_mask = sb("head_mask", [P, HALF_HEADS])
        iota_i = sb("iota_i", [P, E], I32)
        iota_j = sb("iota_j", [P, MAX_TILES + 1], I32)
        bo_b = sb("bo_b", [P, D])
        g_b = sb("g_b", [P, 2])

        ld_w, ld_ctx, ld_bias, ld_g, ld_bo, ld_wr = (
            sem(n) for n in ("ld_w", "ld_ctx", "ld_bias", "ld_g", "ld_bo", "ld_wr"))
        made = sem("made")
        consts = sem("consts")
        wt_done = sem("wt_done")
        wt_sb = sem("wt_sb")
        ctx_done, ctx_sb = sem("ctx_done"), sem("ctx_sb")
        bias_done, bias_sb = sem("bias_done"), sem("bias_sb")
        key_done, key_sb = sem("key_done"), sem("key_sb")
        v_done, v_sb = sem("v_done"), sem("v_sb")
        tanh_sb = sem("tanh_sb")
        spread, v_placed = sem("spread"), sem("v_placed")
        n_bias = E * HC

        pieces = []
        for h in range(HEADS):
            row = h * KEYS
            while row < (h + 1) * KEYS:
                c = row // P
                n = min((c + 1) * P, (h + 1) * KEYS) - row
                pieces.append((h, c, row - h * KEYS, row - c * P, n))
                row += n

        weights = ["Wk", "Wv", "Wq", "Wo"]
        turned = [wk_t, wv_t, k.wq_t, k.wo_t]

        with nc.Block() as block:
            @block.sync
            def _(sp):
                sp.dma_start(ctx_raw[:], t["ctx_1024"].rearrange("b k d -> k b d")).then_inc(ld_ctx, 16)
                for i, w in enumerate(weights):
                    sp.dma_start(w_raw[:, i], t["L0_xattn_" + w].rearrange("(c p) i -> p c i", p=P)).then_inc(ld_w, 16)
                sp.wait_ge(consts, 1)
                sp.wait_ge(v_sb, BATCH // 2)
                for h, c, key, part, n in pieces:
                    col = (h - chunk_heads(c)[0]) * VW
                    sp.dma_start(k.v_rows[part:part + n, :, c, col:col + VW],
                                 v_aug[key:key + n, :, h, :]).then_inc(v_placed, 16)
                sp.wait_ge(v_placed, 16 * len(pieces))

            @block.scalar
            def _(act):
                act.dma_start(bias_rows[0:n_bias, :],
                              t["L0_ffn_b1"].rearrange("e (m p) -> (e m) p", p=P)).then_inc(ld_bias, 16)
                for i, b in enumerate(("bq", "bk", "bv")):
                    act.dma_start(bias_rows[n_bias + KC * i:n_bias + KC * (i + 1), :],
                                  t["L0_xattn_" + b].rearrange("(c p) -> c p", p=P)).then_inc(ld_bias, 16)
                act.dma_start(g_b[:, 0:1], t["g_xattn"].partition_broadcast(P)).then_inc(ld_g, 16)
                act.dma_start(g_b[:, 1:2], t["g_ffn"].partition_broadcast(P)).then_inc(ld_g, 16)
                act.dma_start(bo_b[:], t["L0_xattn_bo"].partition_broadcast(P)).then_inc(ld_bo, 16)
                act.dma_start(k.w_router[:], t["L0_ffn_w_router"].rearrange("(c p) e -> p c e", p=P)).then_inc(ld_wr, 16)
                act.wait_ge(ld_g, 32)
                act.activation(k.gates[:], g_b[:], ACT.Tanh).then_inc(tanh_sb, 1)
                act.wait_ge(ctx_done, 1)
                for c in range(KC):
                    act.activation(ctx_t[:, c], banks[:, c, 0:BATCH * KEYS], ACT.Copy).then_inc(ctx_sb, 1)
                act.wait_ge(bias_done, 1)
                act.activation(k.bias_t[:], banks[:, 2, 0:n_bias + 3 * KC], ACT.Copy).then_inc(bias_sb, 1)
                act.wait_ge(bias_sb, 1)
                for c in range(KC):
                    act.wait_ge(key_done, c + 1)
                    act.activation(key_t[:, c], banks[:, c, 0:BATCH * KEYS], ACT.Identity,
                                   bias=k.bias_t[:, n_bias + KC + c:n_bias + KC + c + 1]).then_inc(key_sb, 1)
                act.wait_ge(ld_wr, 16)

            @block.gpsimd
            def _(pool):
                pool.memset(k.ident[:], 0.0).then_inc(made, 1)
                pool.memset(k.ones[:], 1.0).then_inc(made, 1)
                pool.memset(head_mask[:], 1.0).then_inc(made, 1)
                pool.wait_ge(made, 3)
                pool.affine_select(out=k.ident[:], in_=k.ident[:], compare_op=ALU.not_equal, fill=1.0, base=0,
                                   pattern=[[-1, P]], channel_multiplier=1).then_inc(made, 1)
                pool.affine_select(out=k.before[:], in_=k.ones[:], compare_op=ALU.is_gt, fill=0.0, base=0,
                                   pattern=[[1, P]], channel_multiplier=-1).then_inc(made, 1)
                pool.affine_select(out=head_mask[:], in_=head_mask[:], compare_op=ALU.is_ge, fill=0.0, base=0,
                                   pattern=[[-DH, HALF_HEADS]], channel_multiplier=1).then_inc(made, 1)
                pool.wait_ge(made, 6)
                pool.affine_select(out=head_mask[:], in_=head_mask[:], compare_op=ALU.is_ge, fill=0.0, base=DH - 1,
                                   pattern=[[DH, HALF_HEADS]], channel_multiplier=-1).then_inc(made, 1)
                pool.iota(iota_i[:], pattern=[[1, E]], base=0, channel_multiplier=0).then_inc(made, 1)
                pool.iota(iota_j[:], pattern=[[1, MAX_TILES + 1]], base=0, channel_multiplier=0).then_inc(made, 1)
                pool.iota(k.token_no[:], pattern=[[P, TOKENS // P]], base=0, channel_multiplier=1).then_inc(made, 1)
                pool.memset(k.minus_half[:], -0.5).then_inc(made, 1)
                pool.memset(k.seen[:], 0.0).then_inc(made, 1)
                pool.memset(k.upto[:], 1.0).then_inc(made, 1)
                pool.wait_ge(made, 13)
                pool.affine_select(out=k.upto[:], in_=k.upto[:], compare_op=ALU.is_ge, fill=0.0, base=0,
                                   pattern=[[1, E], [-1, E]], channel_multiplier=0).then_inc(made, 1)
                pool.memset(k.pad_rows[:], 0.0).then_inc(made, 1)
                pool.wait_ge(made, 15)
                pool.iota(k.pad_rows[:, :, ROW - 1:ROW].bitcast(I32), pattern=[[P, SB], [1, 1]], base=TOKENS,
                          channel_multiplier=1).then_inc(made, 1)

            @block.vector
            def _(dve):
                dve.memset(k.v_rows[:], 0.0).then_inc(consts, 1)
                dve.memset(v_aug[:], 1.0).then_inc(consts, 1)
                dve.wait_ge(made, 9)
                dve.tensor_copy(k.expert_no[:], iota_i[:]).then_inc(consts, 1)
                dve.tensor_copy(k.tile_no[:], iota_j[:]).then_inc(consts, 1)
                dve.wait_ge(consts, 4)
                dve.tensor_scalar(k.region_of[:], k.expert_no[:], float(REGION), None, ALU.mult).then_inc(consts, 1)
                dve.wait_ge(tanh_sb, 1)
                dve.wait_ge(ld_bo, 16)
                dve.tensor_scalar(k.gated_bo[:], bo_b[:], k.gates[:, 0:1], None, ALU.mult).then_inc(consts, 1)
                dve.tensor_scalar(k.out_gate[:], k.gates[:, 1:2], 1.0 / W_SCALE, None, ALU.mult).then_inc(consts, 1)
                for i in range(4):
                    dve.wait_ge(wt_done, i + 1)
                    dve.tensor_copy(turned[i][:].rearrange("p c o -> p (c o)"), banks[:, 4 + i, :]).then_inc(wt_sb, 1)
                for pair in range(BATCH // 2):
                    dve.wait_ge(v_done, pair + 1)
                    dve.tensor_copy(v_aug[:, 2 * pair:2 * pair + 2, :, 0:DH].rearrange("k b h d -> k (b h) d"),
                                    banks[0:KEYS, 4 + pair, :].rearrange("k (a d) -> k a d", d=DH)).then_inc(v_sb, 1)
                for c in range(KC):
                    dve.wait_ge(key_sb, c + 1)
                    for b in range(BATCH):
                        dve.tensor_tensor(
                            k.keys_bd[:, b, c * HALF_HEADS * KEYS:(c + 1) * HALF_HEADS * KEYS].rearrange(
                                "p (h k) -> p h k", k=KEYS),
                            key_t[:, c, b * KEYS:(b + 1) * KEYS].unsqueeze(1).to_broadcast([P, HALF_HEADS, KEYS]),
                            head_mask[:].unsqueeze(2).to_broadcast([P, HALF_HEADS, KEYS]),
                            ALU.mult).then_inc(spread, 1)

            @block.tensor
            def _(pe):
                pe.wait_ge(made, 4)
                pe.wait_ge(ld_ctx, 16)
                for c in range(KC):
                    for b in range(BATCH):
                        mm = pe.transpose(banks[:, c, b * KEYS:(b + 1) * KEYS], ctx_raw[:, b, c * P:(c + 1) * P],
                                          k.ident[0:KEYS, 0:KEYS])
                mm.then_inc(ctx_done, 1)
                pe.wait_ge(ld_bias, 64)
                pe.transpose(banks[:, 2, 0:n_bias + 3 * KC], bias_rows[:],
                             k.ident[0:n_bias + 3 * KC, 0:n_bias + 3 * KC]).then_inc(bias_done, 1)
                pe.wait_ge(ld_w, 64)
                for i in range(4):
                    for c in range(KC):
                        for o in range(KC):
                            mm = pe.transpose(banks[:, 4 + i, c * D + o * P:c * D + (o + 1) * P],
                                              w_raw[:, i, o, c * P:(c + 1) * P], k.ident[:])
                    mm.then_inc(wt_done, 1)
                pe.wait_ge(ctx_sb, KC)
                pe.wait_ge(wt_sb, 2)
                for o in range(KC):
                    for c in range(KC):
                        mm = pe.matmul(banks[:, o, 0:BATCH * KEYS], wk_t[:, c, o * P:(o + 1) * P], ctx_t[:, c],
                                       start=(c == 0), stop=(c == KC - 1))
                    mm.then_inc(key_done, 1)
                for pair in range(BATCH // 2):
                    for j in range(2):
                        b = 2 * pair + j
                        for c in range(KC):
                            mm = pe.matmul(banks[0:KEYS, 4 + pair, j * D:(j + 1) * D],
                                           ctx_t[:, c, b * KEYS:(b + 1) * KEYS], wv_t[:, c],
                                           start=(c == 0), stop=(c == KC - 1))
                    mm.then_inc(v_done, 1)


def attention_phase(nc, t, k, out, routed):
    S, A, B, C, DB = k.banks[:, 0:4], k.banks[:, 4], k.banks[:, 5], k.banks[:, 6], k.banks[:, 7]
    n_bias = E * HC
    x_rows = t["x"].rearrange("b s d -> (b s) d").rearrange("(j t p) d -> j p t d", t=2, p=P)
    out_rows = out[0:TOKENS, :].rearrange("(j t p) d -> j p t d", t=2, p=P)

    with ExitStack() as ctx:
        def sb(name, shape, dt=F32):
            return ctx.enter_context(nc.sbuf_tensor(name, shape, dt))

        def sem(name):
            return ctx.enter_context(nc.semaphore(name))

        lent = [w[:, E - 1].rearrange("p c n -> p (c n)").bitcast(F32) for w in (k.w1_hi, k.w1_lo, k.w2_hi, k.w2_lo)]
        x_in = lent[0].rearrange("p (b t d) -> p b t d", b=2, t=2)
        q_t = lent[1].rearrange("p (b c n) -> p b c n", b=2, c=KC)
        x_res = lent[2].rearrange("p (b t d) -> p b t d", b=2, t=2)
        attn_t, x2_t = (lent[3][:, i * KC * PAIR:(i + 1) * KC * PAIR].rearrange("p (c n) -> p c n", c=KC)
                        for i in range(2))
        x_norm = sb("x_norm", [P, 2, D])
        xn_t = sb("xn_t", [P, KC, PAIR])
        prob = sb("prob", [P, 2, SCORES])
        prob_t = sb("prob_t", [P, PCH, P])
        attn = sb("attn", [P, 2, D])
        row = sb("row", [P, 2, 2, ROW])
        pos = sb("pos", [P, 2, 2, 2], U32)
        stage = sb("stage", [P, 2048])
        top = sb("top", [P, 2, HEADS])
        den = sb("den", [P, 2, HEADS])
        stats = sb("stats", [P, 2, 2, 6])
        mv = sb("mv", [P, 2, 2, 2])
        var_eps = sb("var_eps", [P, 2, 2, 1])
        rstd = sb("rstd", [P, 2, 2, 1])
        l_max = sb("l_max", [P, 2])
        l_shift = sb("l_shift", [P, 2, E])
        l_exp = sb("l_exp", [P, 2, E])
        l_sum = sb("l_sum", [P, 2])
        l_rec = sb("l_rec", [P, 2])
        r_prob = sb("r_prob", [P, 2, E])
        best = sb("best", [P, 2, 8])
        best_i = sb("best_i", [P, 2, 8], U32)
        best_f = sb("best_f", [P, 2, 2])
        mask = sb("mask", [P, 2, 2, E])
        weighed = sb("weighed", [P, 2, 2, E])
        chosen = sb("chosen", [P, 2, E], BF16)
        place = sb("place", [P, 2, E])
        placed = sb("placed", [P, 2, 2, E])

        x_in_ld = [sem(f"x_in_ld{i}") for i in range(2)]
        x_res_ld = [sem(f"x_res_ld{i}") for i in range(2)]
        x2_st = [sem(f"x2_st{i}") for i in range(2)]
        scat = [sem(f"scat{i}") for i in range(2)]
        stage_ld = sem("stage_ld")
        pad_st = sem("pad_st")
        score_ps, x2t_ps, pt_ps, av_ps, q_ps, logit_ps, ot_ps, wo_ps, xt_ps, rank_ps = (
            sem(n) for n in ("score_ps", "x2t_ps", "pt_ps", "av_ps", "q_ps", "logit_ps", "ot_ps", "wo_ps",
                             "xt_ps", "rank_ps"))
        x2t_sb, pt_sb, prob_abs, prob_exp, q_sb, ot_sb, xt_sb, router_exp, w_hi = (
            sem(n) for n in ("x2t_sb", "pt_sb", "prob_abs", "prob_exp", "q_sb", "ot_sb", "xt_sb", "router_exp", "w_hi"))
        top_sb, shift_sb, den_sb, attn_sb, ln1, x2_sb, ln2, router, w_scaled = (
            sem(n) for n in ("top_sb", "shift_sb", "den_sb", "attn_sb", "ln1", "x2_sb", "ln2", "router",
                             "w_scaled"))
        rstd1, rstd2, res_bo, token_sb, w_lo = (sem(n) for n in ("rstd1", "rstd2", "res_bo", "token_sb", "w_lo"))
        LN_OPS = 6
        ROUTER_OPS = 19
        STAGED = 2 * (E - 1)

        def staged(m, par):
            return exists(2 * m + par) and (not isinstance(m, int) or m < E - 1)

        def halves(m, par):
            hi, lo = ((k.w1_hi, k.w1_lo), (k.w2_hi, k.w2_lo))[par]
            return [w[:, bass.ds(m, 1)].rearrange("p a c n -> p (a c n)") for w in (hi, lo)]

        with nc.Block() as block:
            @block.sync
            def _(sp):
                def load_x(j, mj, pj):
                    ready(sp, ln1, j - 2, LN_OPS)
                    sp.dma_start(x_in[:, pj], x_rows[bass.ds(j, 1)].rearrange("a p t d -> p (a t) d"))\
                        .then_inc(x_in_ld[pj], 16)

                sp.dma_start(routed[E * REGION:ROUTED, :].rearrange("(t p) r -> p t r", p=P),
                             k.pad_rows[:]).then_inc(pad_st, 16)

                def step(m, par):
                    j, mj, pj = item(m, par, 2)
                    if exists(j):
                        load_x(j, mj, pj)
                    if staged(m, par):
                        ready(sp, w_lo, 2 * m + par - 1, 1)
                        w = t["L0_ffn_w1"] if par == 0 else t["L0_ffn_w2"]
                        sp.dma_start(stage[:].rearrange("p (c n) -> p c n", n=w.shape[2]),
                                     w[bass.ds(m, 1)].rearrange("a (c p) n -> p (a c) n", p=P))\
                            .then_inc(stage_ld, 16)
                    j, mj, pj = item(m, par, 0)
                    if exists(j):
                        ready(sp, ln2, j - 2, LN_OPS)
                        ready(sp, x2_st[pj], mj - 1, 16)
                        sp.dma_start(x_res[:, pj], x_rows[bass.ds(j, 1)].rearrange("a p t d -> p (a t) d"))\
                            .then_inc(x_res_ld[pj], 16)
                    j, mj, pj = item(m, par, -1)
                    if exists(j):
                        ready(sp, x2_sb, j)
                        sp.dma_start(out_rows[bass.ds(j, 1)].rearrange("a p t d -> p (a t) d"), x_res[:, pj])\
                            .then_inc(x2_st[pj], 16)

                pipeline(sp, step)
                for i in range(2):
                    sp.wait_ge(x2_st[i], 16 * PAIRS // 2)
                sp.wait_ge(pad_st, 16)

            @block.gpsimd
            def _(pool):
                def inverse_std(n, ln, rstd_sem, j):
                    settled(pool, ln, j, LN_OPS, 4)
                    pool.tensor_scalar(var_eps[:, n], mv[:, n, :, 1:2], LN_EPS, None, ALU.add)\
                        .then_inc(rstd_sem, 1)
                    ready(pool, rstd_sem, j, 2, 1)
                    pool.tensor_tensor(rstd[:, n], var_eps[:, n],
                                       k.minus_half[:].unsqueeze(2).to_broadcast([P, 2, 1]), ALU.pow)\
                        .then_inc(rstd_sem, 1)

                def step(m, par):
                    j, mj, pj = item(m, par, 2)
                    if exists(j):
                        inverse_std(0, ln1, rstd1, j)
                    j, mj, pj = item(m, par, -1)
                    if exists(j):
                        ready(pool, x_res_ld[pj], mj, 16)
                        pool.tensor_tensor(x_res[:, pj], x_res[:, pj],
                                           k.gated_bo[:].unsqueeze(1).to_broadcast([P, 2, D]), ALU.add)\
                            .then_inc(res_bo, 1)
                        inverse_std(1, ln2, rstd2, j)
                    if staged(m, par):
                        hi, lo = halves(m, par)
                        ready(pool, w_scaled, 2 * m + par)
                        pool.tensor_tensor(lo, stage[:], hi, ALU.subtract).then_inc(w_lo, 1)
                    j, mj, pj = item(m, par, -2)
                    if exists(j):
                        ready(pool, ln2, j, LN_OPS)
                        pool.tensor_copy(row[:, pj, :, ROW - 1:ROW].bitcast(I32),
                                         k.token_no[:, bass.ds(2 * j, 2)].unsqueeze(2)).then_inc(token_sb, 1)
                        ready(pool, token_sb, j)
                        settled(pool, router, j, ROUTER_OPS, 17)
                        for tile in range(2):
                            for choice in range(2):
                                pool.indirect_dma_start(
                                    routed[:, :], bass.IndirectOffsetOnAxis(ap=pos[:, pj, tile, choice:choice + 1], axis=0),
                                    row[:, pj, tile], None).then_inc(scat[pj], 16)

                pipeline(pool, step)
                for i in range(2):
                    pool.wait_ge(scat[i], 64 * PAIRS // 2)

            @block.scalar
            def _(act):
                def copy_prob_t(j, tile):
                    ready(act, av_ps, 2 * j + tile - 1)
                    for g, (first, n) in enumerate(((0, 4), (4, 4), (8, 2))):
                        ready(act, pt_ps, 2 * j + tile, 3, g + 1)
                        bank = (A, B, A)[g]
                        if g < 2:
                            act.activation(prob_t[:, first:first + n, :].rearrange("p c n -> p (c n)"),
                                           bank[:, 0:n * P], ACT.Copy).then_inc(pt_sb, 1)
                        else:
                            act.activation(prob_t[:, first, :], bank[:, 0:P], ACT.Copy).then_inc(pt_sb, 1)
                            r = chunk_rows(first + 1)
                            act.activation(prob_t[0:r, first + 1, :], bank[0:r, P:2 * P], ACT.Copy)\
                                .then_inc(pt_sb, 1)

                def absolute_scores(j, tile):
                    ready(act, score_ps, j, 2, tile + 1)
                    ready(act, pt_ps, 2 * (j - 1) + tile, 3)
                    act.activation(prob[:, tile].rearrange("p (q n) -> p q n", q=4), S[:, :, 0:QUAD], ACT.Abs)\
                        .then_inc(prob_abs, 1)

                def exponentials(j, tile):
                    ready(act, shift_sb, j, 2, tile + 1)
                    act.activation(prob[:, tile], prob[:, tile], ACT.Exp, scale=DH ** -0.5).then_inc(prob_exp, 1)

                def step(m, par):
                    j, mj, pj = item(m, par, 0)
                    if exists(j):
                        absolute_scores(j, 0)
                    j, mj, pj = item(m, par, -2)
                    if exists(j):
                        ready(act, x2t_ps, j)
                        ready(act, logit_ps, j - 1)
                        act.activation(x2_t.rearrange("p c n -> p (c n)"), C, ACT.Copy).then_inc(x2t_sb, 1)
                    j, mj, pj = item(m, par, -1)
                    if exists(j):
                        copy_prob_t(j, 1)
                    j, mj, pj = item(m, par, 0)
                    if exists(j):
                        exponentials(j, 0)
                    j, mj, pj = item(m, par, 1)
                    if exists(j):
                        ready(act, q_ps, j)
                        ready(act, score_ps, j - 2, 2)
                        for c in range(KC):
                            act.activation(q_t[:, pj, c], C[:, c * PAIR:(c + 1) * PAIR], ACT.Identity,
                                           bias=k.bias_t[:, n_bias + c:n_bias + c + 1]).then_inc(q_sb, 1)
                    j, mj, pj = item(m, par, -2)
                    if exists(j):
                        ready(act, router, j, ROUTER_OPS, 2)
                        act.activation(l_exp[:], l_shift[:], ACT.Exp).then_inc(router_exp, 1)
                    j, mj, pj = item(m, par, -1)
                    if exists(j):
                        ready(act, ot_ps, j)
                        ready(act, wo_ps, j - 1)
                        for c in range(KC):
                            act.activation(attn_t[:, c], DB[:, c * PAIR:(c + 1) * PAIR], ACT.Identity,
                                           bias=k.bias_t[:, n_bias + 2 * KC + c:n_bias + 2 * KC + c + 1])\
                                .then_inc(ot_sb, 1)
                    if staged(m, par):
                        hi, lo = halves(m, par)
                        ready(act, stage_ld, 2 * m + par, 16)
                        act.activation(hi, stage[:], ACT.Copy, scale=W_SCALE).then_inc(w_hi, 1)
                    j, mj, pj = item(m, par, 0)
                    if exists(j):
                        absolute_scores(j, 1)
                        copy_prob_t(j, 0)
                    j, mj, pj = item(m, par, 2)
                    if exists(j):
                        ready(act, xt_ps, j)
                        ready(act, q_ps, j - 1)
                        act.activation(xn_t[:].rearrange("p c n -> p (c n)"), B, ACT.Copy).then_inc(xt_sb, 1)
                    j, mj, pj = item(m, par, 0)
                    if exists(j):
                        exponentials(j, 1)

                pipeline(act, step)

            @block.vector
            def _(dve):
                def shift_scores(j, tile):
                    absolute = prob[:, tile].rearrange("p (h k) -> p h k", k=KEYS)
                    ready(dve, prob_abs, j, 2, tile + 1)
                    dve.tensor_reduce(top[:, tile], absolute, AX.X, ALU.max).then_inc(top_sb, 1)
                    ready(dve, top_sb, j, 2, tile + 1)
                    dve.tensor_tensor(absolute, absolute, top[:, tile].unsqueeze(2).to_broadcast([P, HEADS, KEYS]),
                                      ALU.subtract).then_inc(shift_sb, 1)

                def normalise_attn(j, tile):
                    ready(dve, av_ps, j, 2, tile + 1)
                    v = DB[:, 0:HEADS * VW].rearrange("p (h w) -> p h w", w=VW)
                    dve.reciprocal(den[:, tile], v[:, :, DH]).then_inc(den_sb, 1)
                    ready(dve, den_sb, j, 2, tile + 1)
                    ready(dve, ot_ps, j - 1)
                    dve.tensor_tensor(attn[:, tile].rearrange("p (h d) -> p h d", d=DH), v[:, :, 0:DH],
                                      den[:, tile].unsqueeze(2).to_broadcast([P, HEADS, DH]), ALU.mult)\
                        .then_inc(attn_sb, 1)

                def norm_stats(n, ln, x, j):
                    for tile in range(2):
                        dve.bn_stats(stats[:, n, tile], x[:, tile]).then_inc(ln, 1)
                    settled(dve, ln, j, LN_OPS, 2)
                    for tile in range(2):
                        dve.bn_aggr(mv[:, n, tile], stats[:, n, tile]).then_inc(ln, 1)

                def norm_apply(n, ln, x, y):
                    for tile in range(2):
                        dve.tensor_scalar(y[:, tile], x[:, tile], mv[:, n, tile, 0:1], rstd[:, n, tile, 0:1],
                                          ALU.subtract, ALU.mult).then_inc(ln, 1)

                def over_experts(a):
                    return a.unsqueeze(2).to_broadcast([P, 2, E])

                def route_weights(j, pj):
                    def done(part):
                        ready(dve, router, j, ROUTER_OPS, part)

                    logits = B[:, 0:2 * E].rearrange("p (t e) -> p t e", e=E)
                    ready(dve, logit_ps, j)
                    dve.tensor_reduce(l_max[:], logits, AX.X, ALU.max).then_inc(router, 1)
                    done(1)
                    dve.tensor_tensor(l_shift[:], logits, over_experts(l_max[:]), ALU.subtract).then_inc(router, 1)
                    ready(dve, router_exp, j)
                    dve.tensor_reduce(l_sum[:], l_exp[:], AX.X, ALU.add).then_inc(router, 1)
                    done(3)
                    dve.reciprocal(l_rec[:], l_sum[:]).then_inc(router, 1)
                    done(4)
                    dve.tensor_tensor(r_prob[:], l_exp[:], over_experts(l_rec[:]), ALU.mult).then_inc(router, 1)
                    settled(dve, router, j, ROUTER_OPS, 5)
                    for tile in range(2):
                        dve.max(best[:, tile], r_prob[:, tile]).then_inc(router, 1)
                    settled(dve, router, j, ROUTER_OPS, 7)
                    for tile in range(2):
                        dve.max_index(best_i[:, tile], best[:, tile], r_prob[:, tile]).then_inc(router, 1)
                    done(9)
                    dve.tensor_copy(best_f[:], best_i[:, :, 0:2]).then_inc(router, 1)
                    done(10)
                    dve.tensor_tensor(mask[:], k.expert_no[:].unsqueeze(1).unsqueeze(1).to_broadcast([P, 2, 2, E]),
                                      best_f[:].unsqueeze(3).to_broadcast([P, 2, 2, E]), ALU.is_equal)\
                        .then_inc(router, 1)
                    done(11)
                    dve.tensor_tensor(weighed[:], mask[:], best[:, :, 0:2].unsqueeze(3).to_broadcast([P, 2, 2, E]),
                                      ALU.mult).then_inc(router, 1)
                    done(12)
                    dve.tensor_tensor(row[:, pj, :, D:D + E], weighed[:, :, 0], weighed[:, :, 1], ALU.add)\
                        .then_inc(router, 1)
                    dve.tensor_tensor(chosen[:], mask[:, :, 0], mask[:, :, 1], ALU.add).then_inc(router, 1)

                def route_places(j, pj):
                    def done(part):
                        ready(dve, router, j, ROUTER_OPS, part)

                    ready(dve, rank_ps, j)
                    dve.tensor_tensor(place[:], A[:, 0:2 * E].rearrange("p (t e) -> p t e", e=E),
                                      k.region_of[:].unsqueeze(1).to_broadcast([P, 2, E]), ALU.add)\
                        .then_inc(router, 1)
                    done(15)
                    dve.tensor_tensor(placed[:], mask[:], place[:].unsqueeze(2).to_broadcast([P, 2, 2, E]),
                                      ALU.mult).then_inc(router, 1)
                    done(16)
                    with nc.allow_low_precision(reason="whole numbers below 2**24"):
                        dve.tensor_reduce(pos[:, pj], placed[:], AX.X, ALU.add).then_inc(router, 1)
                    for tile in range(2):
                        dve.tensor_tensor(k.seen[:], k.seen[:], chosen[:, tile], ALU.add).then_inc(router, 1)
                        if tile == 0:
                            done(18)

                def step(m, par):
                    j, mj, pj = item(m, par, 0)
                    if exists(j):
                        shift_scores(j, 0)
                    j, mj, pj = item(m, par, -1)
                    if exists(j):
                        normalise_attn(j, 1)
                    j, mj, pj = item(m, par, 2)
                    if exists(j):
                        ready(dve, x_in_ld[pj], mj, 16)
                        norm_stats(0, ln1, x_in[:, pj], j)
                    j, mj, pj = item(m, par, -2)
                    if exists(j):
                        route_weights(j, pj)
                    if staged(m, par):
                        ready(dve, w_hi, 2 * m + par)
                        dve.tensor_scalar(stage[:], stage[:], W_SCALE, None, ALU.mult).then_inc(w_scaled, 1)
                    j, mj, pj = item(m, par, 0)
                    if exists(j):
                        shift_scores(j, 1)
                    j, mj, pj = item(m, par, 2)
                    if exists(j):
                        ready(dve, rstd1, j, 2)
                        ready(dve, xt_ps, j - 1)
                        norm_apply(0, ln1, x_in[:, pj], x_norm[:])
                    j, mj, pj = item(m, par, -1)
                    if exists(j):
                        ready(dve, wo_ps, j)
                        ready(dve, res_bo, j)
                        dve.scalar_tensor_tensor(x_res[:, pj].rearrange("p t d -> p (t d)"), C, k.gates[:, 0:1],
                                                 x_res[:, pj].rearrange("p t d -> p (t d)"), ALU.mult, ALU.add)\
                            .then_inc(x2_sb, 1)
                        ready(dve, x2_sb, j)
                        norm_stats(1, ln2, x_res[:, pj], j)
                    j, mj, pj = item(m, par, 0)
                    if exists(j):
                        normalise_attn(j, 0)
                    j, mj, pj = item(m, par, -1)
                    if exists(j):
                        ready(dve, rstd2, j, 2)
                        ready(dve, scat[pj], mj - 1, 64)
                        norm_apply(1, ln2, x_res[:, pj], row[:, pj, :, 0:D])
                    j, mj, pj = item(m, par, -2)
                    if exists(j):
                        route_places(j, pj)

                pipeline(dve, step)

            @block.tensor
            def _(pe):
                def scores(m, par, tile):
                    j, mj, pj = item(m, par, 0)
                    b = batch_of(m, par, 0)
                    ready(pe, q_sb, j, KC)
                    ready(pe, prob_abs, 2 * j + tile - 1)
                    for q in range(4):
                        c = q // 2
                        mm = pe.matmul(S[:, q, 0:QUAD], q_t[:, pj, c, tile * P:(tile + 1) * P],
                                       k.keys_bd[:, bass.ds(b, 1), q * QUAD:(q + 1) * QUAD].rearrange("p a n -> p (a n)"),
                                       start=True, stop=True)
                    mm.then_inc(score_ps, 1)

                def values(m, par, shift, tile):
                    j, mj, pj = item(m, par, shift)
                    b = batch_of(m, par, shift)
                    ready(pe, prob_exp, j, 2, tile + 1)
                    ready(pe, pt_sb, 2 * j + tile - 1, 4)
                    if tile == 1:
                        ready(pe, router, j - 2, ROUTER_OPS, 17)
                        if exists(j + 2):
                            ready(pe, xt_sb, j + 2)
                    else:
                        ready(pe, router, j - 2, ROUTER_OPS, 2)
                    for g, chunks in enumerate((range(0, 4), range(4, 8), range(8, PCH))):
                        if g == 2:
                            ready(pe, pt_sb, 2 * j + tile, 4, 1)
                        for i, c in enumerate(chunks):
                            r = chunk_rows(c)
                            mm = pe.transpose((A, B, A)[g][0:r, i * P:(i + 1) * P], prob[:, tile, c * P:c * P + r],
                                              k.ident[:])
                        mm.then_inc(pt_ps, 1)
                    if tile == 1:
                        ready(pe, attn_sb, j, 2, 1)
                    else:
                        ready(pe, ot_sb, j - 1, KC)
                    for c in range(PCH):
                        ready(pe, pt_sb, 2 * j + tile, 4, (1, 1, 1, 1, 2, 2, 2, 2, 3, 4)[c])
                        first, n = chunk_heads(c)
                        r = chunk_rows(c)
                        mm = pe.matmul(DB[:, first * VW:(first + n) * VW], prob_t[0:r, c, :],
                                       k.v_rows[0:r, bass.ds(b, 1), c, 0:n * VW].rearrange("p a n -> p (a n)"),
                                       start=(c == 0), stop=(c == PCH - 1), skip_group_check=True)
                    mm.then_inc(av_ps, 1)

                def turn_pair(dst, src, done):
                    for c in range(KC):
                        for tile in range(2):
                            mm = pe.transpose(dst[:, c * PAIR + tile * P:c * PAIR + (tile + 1) * P],
                                              src[:, tile, c * P:(c + 1) * P], k.ident[:])
                    mm.then_inc(done, 1)

                def step(m, par):
                    j, mj, pj = item(m, par, 0)
                    if exists(j):
                        scores(m, par, 0)
                    j, mj, pj = item(m, par, -2)
                    if exists(j):
                        ready(pe, ln2, j, LN_OPS)
                        turn_pair(C, row[:, pj, :, 0:D], x2t_ps)
                    j, mj, pj = item(m, par, -1)
                    if exists(j):
                        values(m, par, -1, 1)
                    j, mj, pj = item(m, par, 1)
                    if exists(j):
                        ready(pe, xt_sb, j)
                        ready(pe, x2t_sb, j - 3)
                        ready(pe, q_sb, j - 1, KC)
                        for o in range(KC):
                            for c in range(KC):
                                mm = pe.matmul(C[:, o * PAIR:(o + 1) * PAIR], k.wq_t[:, c, o * P:(o + 1) * P],
                                               xn_t[:, c], start=(c == 0), stop=(c == KC - 1))
                        mm.then_inc(q_ps, 1)
                    j, mj, pj = item(m, par, -2)
                    if exists(j):
                        ready(pe, x2t_sb, j)
                        ready(pe, pt_sb, min(2 * j + 3, 2 * PAIRS - 1) if isinstance(j, int) else 2 * j + 3, 4, 2)
                        for tile in range(2):
                            for c in range(KC):
                                mm = pe.matmul(B[:, tile * E:(tile + 1) * E], x2_t[:, c, tile * P:(tile + 1) * P],
                                               k.w_router[:, c], start=(c == 0), stop=(c == KC - 1))
                        mm.then_inc(logit_ps, 1)
                    j, mj, pj = item(m, par, -1)
                    if exists(j):
                        ready(pe, attn_sb, j, 2)
                        turn_pair(DB, attn, ot_ps)
                    j, mj, pj = item(m, par, 0)
                    if exists(j):
                        scores(m, par, 1)
                    j, mj, pj = item(m, par, -1)
                    if exists(j):
                        ready(pe, ot_sb, j, KC)
                        if exists(j + 2):
                            ready(pe, q_sb, j + 2, KC)
                        ready(pe, x2t_sb, j - 1)
                        for tile in range(2):
                            for c in range(KC):
                                mm = pe.matmul(C[:, tile * D:(tile + 1) * D], attn_t[:, c, tile * P:(tile + 1) * P],
                                               k.wo_t[:, c], start=(c == 0), stop=(c == KC - 1))
                        mm.then_inc(wo_ps, 1)
                    j, mj, pj = item(m, par, 0)
                    if exists(j):
                        values(m, par, 0, 0)
                    j, mj, pj = item(m, par, 2)
                    if exists(j):
                        ready(pe, ln1, j, LN_OPS)
                        ready(pe, xt_sb, j - 1)
                        turn_pair(B, x_norm, xt_ps)
                    j, mj, pj = item(m, par, -2)
                    if exists(j):
                        ready(pe, router, j, ROUTER_OPS, 14)
                        ready(pe, router, j - 1, ROUTER_OPS)
                        pe.matmul(A[:, 0:E], k.before[:], chosen[:, 0], start=True, stop=False)
                        pe.matmul(A[:, 0:E], k.ones[:], k.seen[:], start=False, stop=True)
                        pe.matmul(A[:, E:2 * E], k.before[:], chosen[:, 1], start=True, stop=False)
                        pe.matmul(A[:, E:2 * E], k.ones[:], k.seen[:], start=False, stop=False)
                        pe.matmul(A[:, E:2 * E], k.ones[:], chosen[:, 0], start=False, stop=True)\
                            .then_inc(rank_ps, 1)

                pipeline(pe, step)


LOOP_TILES = range(4, MAX_TILES - 3 - (MAX_TILES - 3) % 2)


def tile_exists(tile):
    return not isinstance(tile, int) or 0 <= tile < MAX_TILES


def tile_pipeline(eng, step):
    for s in range(-2, LOOP_TILES.start):
        step(s // 2, s % 2)
    with eng.Fori(LOOP_TILES.start // 2, LOOP_TILES.stop // 2) as m:
        for par in range(2):
            step(m, par)
    for s in range(LOOP_TILES.stop, MAX_TILES + 2):
        step(s // 2, s % 2)


def expert_phase(nc, t, k, out, routed):
    S, A = k.banks[:, 0:4], k.banks[:, 4]
    Y = [k.banks[:, 6], k.banks[:, 7]]
    BANKS = 4
    PER = HC // BANKS

    with ExitStack() as ctx:
        def sb(name, shape, dt=F32):
            return ctx.enter_context(nc.sbuf_tensor(name, shape, dt))

        def sem(name):
            return ctx.enter_context(nc.semaphore(name))

        x_row = sb("x_row", [P, 2, SB, ROW])
        meta = sb("meta", [P, 2, SB, E + 1])
        x_hi = sb("x_hi", [P, KC, SLOTS], F16)
        x_lo = sb("x_lo", [P, KC, SLOTS], F16)
        hid = sb("hid", [P, HC, SLOTS])
        h_hi = sb("h_hi", [P, 2, HC, SLOTS], F16)
        h_lo = sb("h_lo", [P, 2, HC, SLOTS], F16)
        y = sb("y", [P, 2, SB, D])
        b2_b = sb("b2_b", [P, E, D])
        last_w = sb("last_w", [P, 2, 2048])
        NT = MAX_TILES + 1
        count = sb("count", [P, E])
        pad_at = sb("pad_at", [P, E], I32)
        count_i = sb("count_i", [P, E], I32)
        tiles_i = sb("tiles_i", [P, E], I32)
        tiles = sb("tiles", [P, E])
        upto_tiles = sb("upto_tiles", [P, E, E])
        end_of = sb("end_of", [P, E])
        past = sb("past", [P, NT, E])
        past_tiles = sb("past_tiles", [P, NT, E])
        expert_f = sb("expert_f", [P, NT])
        start_f = sb("start_f", [P, NT])
        row_f = sb("row_f", [P, NT])
        expert_of = sb("expert_of", [P, NT], I32)
        row_of = sb("row_of", [P, NT], I32)

        b2_ld, b2_scaled = sem("b2_ld"), sem("b2_scaled")
        last_ld, last_hi, last_scaled, last_lo = (sem(n) for n in ("last_ld", "last_hi", "last_scaled", "last_lo"))
        count_ps, plan, pads, tile_row = (sem(n) for n in ("count_ps", "plan", "pads", "tile_row"))
        row_ld = [sem(f"row_ld{i}") for i in range(2)]
        added = [sem(f"added{i}") for i in range(2)]
        xt_done, x_hi_sb, x_lo_sb = sem("xt_done"), sem("x_hi_sb"), sem("x_lo_sb")
        hid_ps, hid_sb, h_hi_sb, h_lo_sb = (sem(n) for n in ("hid_ps", "hid_sb", "h_hi_sb", "h_lo_sb"))
        y_ps, y_bias, y_sb, meta_sb = (sem(n) for n in ("y_ps", "y_bias", "y_sb", "meta_sb"))
        PLAN_OPS = 13
        last = [(k.w1_hi, k.w1_lo), (k.w2_hi, k.w2_lo)]

        def flat(w):
            return w[:, E - 1].rearrange("p c n -> p (c n)")

        def expert(eng, tile):
            return eng.value_load(expert_of[0:1, bass.ds(tile, 1)], min_val=0, max_val=E - 1)

        with nc.Block() as block:
            @block.sync
            def _(sp):
                sp.dma_start(last_w[:, 0].rearrange("p (c n) -> p c n", n=HID),
                             t["L0_ffn_w1"][E - 1].rearrange("(c p) n -> p c n", p=P)).then_inc(last_ld, 16)
                sp.dma_start(last_w[:, 1].rearrange("p (c n) -> p c n", n=D),
                             t["L0_ffn_w2"][E - 1].rearrange("(c p) n -> p c n", p=P)).then_inc(last_ld, 16)
                sp.wait_ge(plan, 1)
                for e in range(E):
                    at = sp.value_load(pad_at[0:1, e:e + 1], min_val=0, max_val=E * REGION - SLOTS)
                    sp.dma_start(routed[bass.ds(at, SLOTS), :].rearrange("(t p) r -> p t r", p=P), k.pad_rows[:])\
                        .then_inc(pads, 16)
                sp.wait_ge(pads, 16 * E)
                sp.wait_ge(plan, PLAN_OPS)

                def step(m, par):
                    j, mj, pj = item(m, par, 2)
                    if tile_exists(j):
                        ready(sp, xt_done, j - 2)
                        ready(sp, meta_sb, j - 2)
                        at = sp.value_load(row_of[0:1, bass.ds(j, 1)], min_val=0, max_val=E * REGION)
                        sp.dma_start(x_row[:, pj], routed[bass.ds(at, SLOTS), :].rearrange("(t p) r -> p t r", p=P))\
                            .then_inc(row_ld[pj], 16)

                tile_pipeline(sp, step)

            @block.gpsimd
            def _(pool):
                pool.dma_start(b2_b[:].rearrange("p e d -> p (e d)"),
                               t["L0_ffn_b2"].rearrange("e d -> (e d)").partition_broadcast(P)).then_inc(b2_ld, 16)
                pool.wait_ge(b2_ld, 16)
                pool.tensor_scalar(b2_b[:], b2_b[:], W_SCALE, None, ALU.mult).then_inc(b2_scaled, 1)
                for i, (hi, lo) in enumerate(last):
                    pool.wait_ge(last_scaled, i + 1)
                    pool.tensor_tensor(flat(lo), last_w[:, i], flat(hi), ALU.subtract).then_inc(last_lo, 1)

                def step(m, par):
                    j, mj, pj = item(m, par, -2)
                    if tile_exists(j):
                        ready(pool, y_sb, j, SB)
                        settled(pool, added[1 - pj], mj - (pj == 0), 16 * SB)
                        for b in range(SB):
                            pool.indirect_dma_start(
                                out[:, :], bass.IndirectOffsetOnAxis(ap=meta[:, pj, b, E:E + 1].bitcast(U32), axis=0),
                                y[:, pj, b], None, compute_op=ALU.add).then_inc(added[pj], 16)
                    j, mj, pj = item(m, par, 0)
                    if tile_exists(j):
                        ready(pool, added[pj], mj - 1, 16 * SB)
                        ready(pool, y_sb, j - 2, SB)
                        settled(pool, row_ld[pj], mj, 16)
                        pool.tensor_copy(meta[:, pj], x_row[:, pj, :, D:ROW]).then_inc(meta_sb, 1)

                tile_pipeline(pool, step)
                for i in range(2):
                    pool.wait_ge(added[i], 16 * SB * ((MAX_TILES + 1 - i) // 2))

            @block.scalar
            def _(act):
                for i, (hi, lo) in enumerate(last):
                    act.wait_ge(last_ld, 32)
                    act.activation(flat(hi), last_w[:, i], ACT.Copy, scale=W_SCALE).then_inc(last_hi, 1)
                act.wait_ge(plan, PLAN_OPS)

                def step(m, par):
                    j, mj, pj = item(m, par, 0)
                    if tile_exists(j):
                        e = expert(act, j)
                        for q in range(BANKS):
                            ready(act, hid_ps, j, BANKS, q + 1)
                            ready(act, h_lo_sb, j - 1, BANKS, q + 1)
                            for c in range(q * PER, (q + 1) * PER):
                                ins = act.activation(hid[:, c], S[:, q, c % PER * SLOTS:(c % PER + 1) * SLOTS],
                                                     ACT.Gelu_apprx_tanh, bias=k.bias_t[:, bass.ds(e * HC + c, 1)],
                                                     scale=1.0 / W_SCALE)
                            ins.then_inc(hid_sb, 1)
                    j, mj, pj = item(m, par, 1)
                    if tile_exists(j):
                        ready(act, xt_done, j)
                        ready(act, hid_ps, j - 1, BANKS)
                        ready(act, x_lo_sb, j - 1)
                        act.activation(x_hi[:].rearrange("p c n -> p (c n)"), A, ACT.Copy).then_inc(x_hi_sb, 1)

                tile_pipeline(act, step)

            @block.vector
            def _(dve):
                def done(part):
                    dve.wait_ge(plan, part)

                dve.wait_ge(count_ps, 1)
                dve.tensor_tensor(pad_at[:], A[:, 0:E], k.region_of[:], ALU.add).then_inc(plan, 1)
                dve.tensor_scalar(count[:], A[:, 0:E], float(SLOTS - 1), None, ALU.add).then_inc(plan, 1)
                done(2)
                dve.tensor_copy(count_i[:], count[:]).then_inc(plan, 1)
                done(3)
                dve.tensor_scalar(tiles_i[:], count_i[:], SLOTS.bit_length() - 1, None, ALU.logical_shift_right)\
                    .then_inc(plan, 1)
                done(4)
                dve.tensor_copy(tiles[:], tiles_i[:]).then_inc(plan, 1)
                done(5)
                dve.tensor_tensor(upto_tiles[:], k.upto[:], tiles[:].unsqueeze(1).to_broadcast([P, E, E]), ALU.mult)\
                    .then_inc(plan, 1)
                done(6)
                dve.tensor_reduce(end_of[:], upto_tiles[:], AX.X, ALU.add).then_inc(plan, 1)
                done(7)
                dve.tensor_tensor(past[:], k.tile_no[:].unsqueeze(2).to_broadcast([P, NT, E]),
                                  end_of[:].unsqueeze(1).to_broadcast([P, NT, E]), ALU.is_ge).then_inc(plan, 1)
                done(8)
                dve.tensor_tensor(past_tiles[:], past[:], tiles[:].unsqueeze(1).to_broadcast([P, NT, E]), ALU.mult)\
                    .then_inc(plan, 1)
                dve.tensor_reduce(expert_f[:], past[:], AX.X, ALU.add).then_inc(plan, 1)
                done(9)
                dve.tensor_reduce(start_f[:], past_tiles[:], AX.X, ALU.add).then_inc(plan, 1)
                done(11)
                dve.tensor_tensor(row_f[:], k.tile_no[:], start_f[:], ALU.subtract).then_inc(tile_row, 1)
                dve.tensor_scalar(expert_of[:], expert_f[:], float(E - 1), None, ALU.min).then_inc(plan, 1)
                done(12)
                dve.tensor_scalar(expert_f[:], expert_f[:], float(REGION), None, ALU.mult).then_inc(tile_row, 1)
                dve.wait_ge(tile_row, 2)
                dve.scalar_tensor_tensor(row_f[:], row_f[:], float(SLOTS), expert_f[:], ALU.mult, ALU.add)\
                    .then_inc(tile_row, 1)
                dve.wait_ge(tile_row, 3)
                dve.tensor_scalar(row_of[:], row_f[:], float(E * REGION), None, ALU.min).then_inc(plan, 1)
                for i in range(2):
                    dve.wait_ge(last_hi, i + 1)
                    dve.tensor_scalar(last_w[:, i], last_w[:, i], W_SCALE, None, ALU.mult).then_inc(last_scaled, 1)

                def step(m, par):
                    j, mj, pj = item(m, par, 0)
                    if tile_exists(j):
                        for q in range(BANKS):
                            part = slice(q * PER, (q + 1) * PER)
                            ready(dve, hid_sb, j, BANKS, q + 1)
                            ready(dve, y_ps, j - 2)
                            dve.tensor_copy(h_hi[:, pj, part], hid[:, part]).then_inc(h_hi_sb, 1)
                            ready(dve, h_hi_sb, j, BANKS, q + 1)
                            dve.tensor_tensor(h_lo[:, pj, part], hid[:, part], h_hi[:, pj, part], ALU.subtract)\
                                .then_inc(h_lo_sb, 1)
                    j, mj, pj = item(m, par, 1)
                    if tile_exists(j):
                        ready(dve, x_hi_sb, j)
                        dve.tensor_tensor(x_lo[:].rearrange("p c n -> p (c n)"), A,
                                          x_hi[:].rearrange("p c n -> p (c n)"), ALU.subtract).then_inc(x_lo_sb, 1)
                    j, mj, pj = item(m, par, -1)
                    if tile_exists(j):
                        e = expert(dve, j)
                        ready(dve, y_ps, j)
                        if isinstance(j, int) and j == 0:
                            dve.wait_ge(b2_scaled, 1)
                        ready(dve, added[pj], mj - 1, 16 * SB)
                        dve.tensor_tensor(y[:, pj], Y[pj].rearrange("p (b d) -> p b d", d=D),
                                          b2_b[:, bass.ds(e, 1), :].to_broadcast([P, SB, D]), ALU.add)\
                            .then_inc(y_bias, 1)
                        ready(dve, y_bias, j)
                        ready(dve, meta_sb, j)
                        for b in range(SB):
                            dve.tensor_scalar(y[:, pj, b], y[:, pj, b],
                                              meta[:, pj, b, bass.ds(e, 1)], k.out_gate[:, 0:1],
                                              ALU.mult, ALU.mult).then_inc(y_sb, 1)

                tile_pipeline(dve, step)

            @block.tensor
            def _(pe):
                pe.matmul(A[:, 0:E], k.ones[:], k.seen[:], start=True, stop=True).then_inc(count_ps, 1)
                pe.wait_ge(last_lo, 2)
                pe.wait_ge(plan, PLAN_OPS)

                def step(m, par):
                    j, mj, pj = item(m, par, 0)
                    if tile_exists(j):
                        e = expert(pe, j)
                        ready(pe, x_lo_sb, j)
                        for q in range(BANKS):
                            ready(pe, hid_sb, j - 1, BANKS, q + 1)
                            for c in range(q * PER, (q + 1) * PER):
                                n = 0
                                for i in range(KC):
                                    for w, x in ((k.w1_hi, x_hi), (k.w1_hi, x_lo), (k.w1_lo, x_hi)):
                                        mm = pe.matmul(
                                            S[:, q, c % PER * SLOTS:(c % PER + 1) * SLOTS],
                                            w[:, bass.ds(e, 1), i, c * P:(c + 1) * P].rearrange("p a n -> p (a n)"),
                                            x[:, i], start=(n == 0), stop=(n == 3 * KC - 1))
                                        n += 1
                            mm.then_inc(hid_ps, 1)
                    j, mj, pj = item(m, par, 1)
                    if tile_exists(j):
                        ready(pe, row_ld[pj], mj, 16)
                        ready(pe, x_lo_sb, j - 1)
                        for i in range(KC):
                            for b in range(SB):
                                mm = pe.transpose(A[:, i * SLOTS + b * P:i * SLOTS + (b + 1) * P],
                                                  x_row[:, pj, b, i * P:(i + 1) * P], k.ident[:])
                        mm.then_inc(xt_done, 1)
                    j, mj, pj = item(m, par, -1)
                    if tile_exists(j):
                        e = expert(pe, j)
                        ready(pe, h_lo_sb, j, BANKS)
                        ready(pe, y_bias, j - 2)
                        for b in range(SB):
                            n = 0
                            for c in range(HC):
                                for h, w in ((h_hi, k.w2_hi), (h_hi, k.w2_lo), (h_lo, k.w2_hi)):
                                    mm = pe.matmul(Y[pj][:, b * D:(b + 1) * D], h[:, pj, c, b * P:(b + 1) * P],
                                                   w[:, bass.ds(e, 1), c, :].rearrange("p a n -> p (a n)"),
                                                   start=(n == 0), stop=(n == 3 * HC - 1))
                                    n += 1
                        mm.then_inc(y_ps, 1)

                tile_pipeline(pe, step)


class Kept:
    pass


def gated_cross_attention_and_experts(nc, t, out):
    k = Kept()
    with ExitStack() as ctx:
        def sb(name, shape, dt=F32):
            return ctx.enter_context(nc.sbuf_tensor(name, shape, dt))

        k.banks = ctx.enter_context(nc.psum_tensor("banks", [P, 8, 512], F32))
        k.w1_hi, k.w1_lo = (sb(n, [P, E, KC, HID], F16) for n in ("w1_hi", "w1_lo"))
        k.w2_hi, k.w2_lo = (sb(n, [P, E, HC, D], F16) for n in ("w2_hi", "w2_lo"))
        k.ident = sb("ident", [P, P])
        k.ones = sb("ones", [P, P], BF16)
        k.before = sb("before", [P, P], BF16)
        k.bias_t = sb("bias_t", [P, E * HC + 3 * KC])
        k.gates = sb("gates", [P, 2])
        k.out_gate = sb("out_gate", [P, 1])
        k.expert_no = sb("expert_no", [P, E])
        k.tile_no = sb("tile_no", [P, MAX_TILES + 1])
        k.region_of = sb("region_of", [P, E])
        k.upto = sb("upto", [P, E, E])
        k.seen = sb("seen", [P, E], BF16)
        k.pad_rows = sb("pad_rows", [P, SB, ROW])
        routed = nc.dram_tensor("routed", [ROUTED, ROW], F32, kind="Internal").ap()

        with ExitStack() as attn_ctx:
            def sba(name, shape, dt=F32):
                return attn_ctx.enter_context(nc.sbuf_tensor(name, shape, dt))

            k.wq_t = sba("wq_t", [P, KC, D])
            k.wo_t = sba("wo_t", [P, KC, D])
            k.keys_bd = sba("keys_bd", [P, BATCH, SCORES])
            k.v_rows = sba("v_rows", [P, BATCH, PCH, VCOLS])
            k.w_router = sba("w_router", [P, KC, E])
            k.gated_bo = sba("gated_bo", [P, D])
            k.token_no = sba("token_no", [P, TOKENS // P], I32)
            k.minus_half = sba("minus_half", [P, 1])
            setup_phase(nc, t, k)
            attention_phase(nc, t, k, out, routed)
        expert_phase(nc, t, k, out, routed)


_INS = ["x", "ctx_1024", "g_xattn", "g_ffn", "L0_xattn_Wq", "L0_xattn_bq", "L0_xattn_Wk", "L0_xattn_bk",
        "L0_xattn_Wv", "L0_xattn_bv", "L0_xattn_Wo", "L0_xattn_bo", "L0_ffn_w_router", "L0_ffn_w1", "L0_ffn_b1",
        "L0_ffn_w2", "L0_ffn_b2"]


def kernel(**inputs):
    import numpy as _np
    import concourse.bacc as _bacc
    from concourse import mybir as _mybir
    from concourse.bass_utils import run_bass_kernel_spmd as _run

    nc = _bacc.Bacc("TRN2", target_bir_lowering=False, num_devices=1)
    arrays, args = {}, {}
    for name in _INS:
        a = _np.ascontiguousarray(inputs[name])
        arrays[f"in_{name}_dram"] = a
        args[name] = nc.dram_tensor(f"in_{name}_dram", a.shape, _mybir.dt.from_np(a.dtype), kind="ExternalInput").ap()
    out = nc.dram_tensor("out_0_dram", (TOKENS + SLOTS, D), F32, kind="ExternalOutput").ap()
    gated_cross_attention_and_experts(nc, args, out)
    r = _run(nc, [arrays], core_ids=[0])
    return r.results[0]["out_0_dram"][0:TOKENS].reshape(BATCH, SEQ, D)
```

```python
from contextlib import ExitStack

import concourse.bass as bass
from concourse import mybir

F32 = mybir.dt.float32
F16 = mybir.dt.float16
BF16 = mybir.dt.bfloat16
I32 = mybir.dt.int32
U32 = mybir.dt.uint32
ALU = mybir.AluOpType
ACT = mybir.ActivationFunctionType
AX = mybir.AxisListType

P = 128
BATCH, SEQ, D = 4, 1024, 256
KEYS = 77
HEADS = 16
DH = D // HEADS
E = 8
HID = 1024
TOKENS = BATCH * SEQ
LN_EPS = 1e-5

KC = D // P
HC = HID // P
PAIR = 2 * P
PAIRS = TOKENS // PAIR
PAIRS_PER_BATCH = SEQ // PAIR
HALF_HEADS = HEADS // KC
SCORES = HEADS * KEYS
QUAD = 4 * KEYS
PCH = -(-SCORES // P)
VW = DH + 1
POOL_PIECES = 4
EARLY_PIECES = 9
LATE_PIECES = 14
VCOLS = 3 * VW

SLOTS = 256
SB = SLOTS // P
MAX_TILES = TOKENS * 2 // SLOTS + E - 1
REGION = TOKENS + SLOTS
ROUTED = E * REGION + SLOTS
ROW = D + E + 1
W_SCALE = 64.0


def chunk_heads(c):
    first = P * c // KEYS
    return first, min((P * c + P - 1) // KEYS, HEADS - 1) - first + 1


def chunk_rows(c):
    return min(P, SCORES - P * c)


def value_pieces():
    pieces = []
    for h in range(HEADS):
        row = h * KEYS
        while row < (h + 1) * KEYS:
            c = row // P
            n = min((c + 1) * P, (h + 1) * KEYS) - row
            pieces.append((h, c, row - h * KEYS, row - c * P, n))
            row += n
    return pieces


def values_with_ones(k):
    return k.prob[0:KEYS, 1, 0:BATCH * HEADS * VW].rearrange("k (b h w) -> k b h w", b=BATCH, h=HEADS)


def place_values(eng, k, pieces, placed):
    for h, c, key, part, n in pieces:
        col = (h - chunk_heads(c)[0]) * VW
        eng.dma_start(k.v_rows[part:part + n, :, c, col:col + VW],
                      values_with_ones(k)[key:key + n, :, h, :]).then_inc(placed, 16)


def values_placed(eng, k):
    eng.wait_ge(k.v_placed[0], 16 * (len(value_pieces()) - POOL_PIECES))
    eng.wait_ge(k.v_placed[1], 16 * POOL_PIECES)


def ready(eng, sem, item, per=1, part=None):
    value = item * per + (per if part is None else part)
    if isinstance(value, int) and value <= 0:
        return
    eng.wait_ge(sem, value)


def settled(eng, sem, item, per=1, part=None):
    ready(eng, sem, item, per, part)
    eng.nop(nofuse=True)


def exists(pair):
    return not isinstance(pair, int) or 0 <= pair < PAIRS


def pipeline(eng, step):
    for s in range(-2, 4):
        step(s // 2, s % 2)
    with eng.Fori(2, (PAIRS - 2) // 2) as m:
        for par in range(2):
            step(m, par)
    for s in range(PAIRS - 2, PAIRS + 3):
        step(s // 2, s % 2)


def item(m, par, shift):
    return 2 * m + (par + shift), m + (par + shift) // 2, (par + shift) % 2


def batch_of(m, par, shift):
    return (m + (par + shift) // 2) // (PAIRS_PER_BATCH // 2)


def setup_phase(nc, t, k):
    banks = k.banks
    with ExitStack() as ctx:
        def sb(name, shape, dt=F32):
            return ctx.enter_context(nc.sbuf_tensor(name, shape, dt))

        def sem(name):
            return ctx.enter_context(nc.semaphore(name))

        w_raw = sb("w_raw", [P, 4, KC, D])
        wk_t = sb("wk_t", [P, KC, D])
        wv_t = sb("wv_t", [P, KC, D])
        ctx_raw = sb("ctx_raw", [KEYS, BATCH, D])
        ctx_t = sb("ctx_t", [P, KC, BATCH * KEYS])
        key_hi, key_lo = (sb(n, [P, KC, BATCH * KEYS], F16) for n in ("key_hi", "key_lo"))
        bias_rows = sb("bias_rows", [E * HC + 3 * KC, P])
        head_mask = sb("head_mask", [P, HALF_HEADS], F16)
        iota_i = sb("iota_i", [P, E], I32)
        iota_j = sb("iota_j", [P, MAX_TILES + 1], I32)
        bo_b = sb("bo_b", [P, D])
        g_b = sb("g_b", [P, 2])

        v_aug = values_with_ones(k)
        x_rows = t["x"].rearrange("b s d -> (b s) d").rearrange("(j t p) d -> j p t d", t=2, p=P)

        ld_w = [sem(f"ld_w{i}") for i in range(4)]
        ld_ctx, ld_bias, ld_g, ld_bo, ld_wr = (
            sem(n) for n in ("ld_ctx", "ld_bias", "ld_g", "ld_bo", "ld_wr"))
        made = sem("made")
        consts = sem("consts")
        wt_done = sem("wt_done")
        wt_sb = sem("wt_sb")
        ctx_done, ctx_sb = sem("ctx_done"), sem("ctx_sb")
        bias_done, bias_sb = sem("bias_done"), sem("bias_sb")
        key_done, key_sb = sem("key_done"), sem("key_sb")
        v_done, v_sb = sem("v_done"), sem("v_sb")
        tanh_sb = sem("tanh_sb")
        spread, key_lo_sb = sem("spread"), sem("key_lo_sb")
        n_bias = E * HC

        weights = ["Wk", "Wv", "Wq", "Wo"]
        turned = [wk_t, wv_t, k.wq_t, k.wo_t]

        def spread_keys(eng, half, out, c, batches):
            for b in batches:
                eng.tensor_tensor(
                    out[:, b, c * HALF_HEADS * KEYS:(c + 1) * HALF_HEADS * KEYS].rearrange("p (h k) -> p h k", k=KEYS),
                    half[:, c, b * KEYS:(b + 1) * KEYS].unsqueeze(1).to_broadcast([P, HALF_HEADS, KEYS]),
                    head_mask[:].unsqueeze(2).to_broadcast([P, HALF_HEADS, KEYS]),
                    ALU.mult).then_inc(spread, 1)

        POOL_BATCHES = BATCH // 2

        with nc.Block() as block:
            @block.sync
            def _(sp):
                sp.dma_start(ctx_raw[:], t["ctx_1024"].rearrange("b k d -> k b d")).then_inc(ld_ctx, 16)
                for i, w in enumerate(weights):
                    sp.dma_start(w_raw[:, i], t["L0_xattn_" + w].rearrange("(c p) i -> p c i", p=P)).then_inc(ld_w[i], 16)
                for j in range(2):
                    sp.dma_start(k.x_in[:, j], x_rows[j]).then_inc(k.x_in_ld[j], 16)
                sp.wait_ge(consts, 2)
                sp.wait_ge(v_sb, BATCH // 2)
                place_values(sp, k, value_pieces()[POOL_PIECES:EARLY_PIECES], k.v_placed[0])

            @block.scalar
            def _(act):
                act.dma_start(bias_rows[0:n_bias, :],
                              t["L0_ffn_b1"].rearrange("e (m p) -> (e m) p", p=P)).then_inc(ld_bias, 16)
                for i, b in enumerate(("bq", "bk", "bv")):
                    act.dma_start(bias_rows[n_bias + KC * i:n_bias + KC * (i + 1), :],
                                  t["L0_xattn_" + b].rearrange("(c p) -> c p", p=P)).then_inc(ld_bias, 16)
                act.wait_ge(ctx_done, 1)
                for c in range(KC):
                    act.activation(ctx_t[:, c], banks[:, c, 0:BATCH * KEYS], ACT.Copy).then_inc(ctx_sb, 1)
                act.wait_ge(bias_done, 1)
                act.activation(k.bias_t[:], banks[:, 2, 0:n_bias + 3 * KC], ACT.Copy).then_inc(bias_sb, 1)
                act.wait_ge(bias_sb, 1)
                for c in range(KC):
                    act.wait_ge(key_done, c + 1)
                    act.activation(key_hi[:, c], banks[:, c, 0:BATCH * KEYS], ACT.Identity,
                                   bias=k.bias_t[:, n_bias + KC + c:n_bias + KC + c + 1]).then_inc(key_sb, 1)
                act.wait_ge(ld_g, 32)
                act.activation(k.gates[:], g_b[:], ACT.Tanh).then_inc(tanh_sb, 1)
                act.wait_ge(ld_wr, 16)

            @block.gpsimd
            def _(pool):
                pool.memset(k.ident[:], 0.0).then_inc(made, 1)
                pool.memset(k.ones[:], 1.0).then_inc(made, 1)
                pool.memset(head_mask[:], 1.0).then_inc(made, 1)
                pool.wait_ge(made, 3)
                pool.affine_select(out=k.ident[:], in_=k.ident[:], compare_op=ALU.not_equal, fill=1.0, base=0,
                                   pattern=[[-1, P]], channel_multiplier=1).then_inc(made, 1)
                pool.affine_select(out=k.before[:], in_=k.ones[:], compare_op=ALU.is_gt, fill=0.0, base=0,
                                   pattern=[[1, P]], channel_multiplier=-1).then_inc(made, 1)
                pool.affine_select(out=head_mask[:], in_=head_mask[:], compare_op=ALU.is_ge, fill=0.0, base=0,
                                   pattern=[[-DH, HALF_HEADS]], channel_multiplier=1).then_inc(made, 1)
                pool.dma_start(g_b[:, 0:1], t["g_xattn"].partition_broadcast(P)).then_inc(ld_g, 16)
                pool.dma_start(g_b[:, 1:2], t["g_ffn"].partition_broadcast(P)).then_inc(ld_g, 16)
                pool.dma_start(bo_b[:], t["L0_xattn_bo"].partition_broadcast(P)).then_inc(ld_bo, 16)
                pool.dma_start(k.w_router[:], t["L0_ffn_w_router"].rearrange("(c p) e -> p c e", p=P)).then_inc(ld_wr, 16)
                pool.wait_ge(made, 6)
                pool.affine_select(out=head_mask[:], in_=head_mask[:], compare_op=ALU.is_ge, fill=0.0, base=DH - 1,
                                   pattern=[[DH, HALF_HEADS]], channel_multiplier=-1).then_inc(made, 1)
                pool.iota(iota_i[:], pattern=[[1, E]], base=0, channel_multiplier=0).then_inc(made, 1)
                pool.iota(iota_j[:], pattern=[[1, MAX_TILES + 1]], base=0, channel_multiplier=0).then_inc(made, 1)
                pool.iota(k.token_no[:], pattern=[[P, TOKENS // P]], base=0, channel_multiplier=1).then_inc(made, 1)
                pool.memset(k.minus_half[:], -0.5).then_inc(made, 1)
                pool.memset(k.seen[:], 0.0).then_inc(made, 1)
                pool.memset(k.upto[:], 1.0).then_inc(made, 1)
                pool.wait_ge(made, 13)
                pool.affine_select(out=k.upto[:], in_=k.upto[:], compare_op=ALU.is_ge, fill=0.0, base=0,
                                   pattern=[[1, E], [-1, E]], channel_multiplier=0).then_inc(made, 1)
                pool.memset(k.pad_rows[:], 0.0).then_inc(made, 1)
                pool.wait_ge(made, 15)
                pool.iota(k.pad_rows[:, :, ROW - 1:ROW].bitcast(I32), pattern=[[P, SB], [1, 1]], base=TOKENS,
                          channel_multiplier=1).then_inc(made, 1)
                for c in range(KC):
                    pool.wait_ge(key_lo_sb, c + 1)
                    spread_keys(pool, key_lo, k.keys_lo, c, range(POOL_BATCHES, BATCH))
                pool.wait_ge(consts, 2)
                pool.wait_ge(v_sb, BATCH // 2)
                place_values(pool, k, value_pieces()[0:POOL_PIECES], k.v_placed[1])

            @block.vector
            def _(dve):
                dve.memset(k.v_rows[:], 0.0).then_inc(consts, 1)
                dve.memset(v_aug, 1.0).then_inc(consts, 1)
                dve.wait_ge(made, 9)
                dve.tensor_copy(k.expert_no[:], iota_i[:]).then_inc(consts, 1)
                dve.tensor_copy(k.tile_no[:], iota_j[:]).then_inc(consts, 1)
                dve.wait_ge(consts, 4)
                dve.tensor_scalar(k.region_of[:], k.expert_no[:], float(REGION), None, ALU.mult).then_inc(consts, 1)

                def copy_turned(i):
                    dve.wait_ge(wt_done, i + 1)
                    dve.tensor_copy(turned[i][:].rearrange("p c o -> p (c o)"), banks[:, 4 + i, :]).then_inc(wt_sb, 1)

                def key_low_half(c):
                    dve.wait_ge(key_sb, c + 1)
                    dve.scalar_tensor_tensor(key_lo[:, c], banks[:, c, 0:BATCH * KEYS],
                                             k.bias_t[:, n_bias + KC + c:n_bias + KC + c + 1], key_hi[:, c],
                                             ALU.add, ALU.subtract).then_inc(key_lo_sb, 1)

                for i in range(2):
                    copy_turned(i)
                key_low_half(0)
                spread_keys(dve, key_hi, k.keys_hi, 0, range(0, 2))
                key_low_half(1)
                spread_keys(dve, key_hi, k.keys_hi, 0, range(2, BATCH))
                for pair in range(BATCH // 2):
                    dve.wait_ge(v_done, pair + 1)
                    dve.tensor_copy(v_aug[:, 2 * pair:2 * pair + 2, :, 0:DH].rearrange("k b h d -> k (b h) d"),
                                    banks[0:KEYS, 4 + pair, :].rearrange("k (a d) -> k a d", d=DH)).then_inc(v_sb, 1)
                    spread_keys(dve, key_hi, k.keys_hi, 1, range(2 * pair, 2 * pair + 2))
                for i in range(2, 4):
                    copy_turned(i)
                for c in range(KC):
                    dve.wait_ge(key_lo_sb, c + 1)
                    spread_keys(dve, key_lo, k.keys_lo, c, range(0, POOL_BATCHES))
                dve.wait_ge(tanh_sb, 1)
                dve.wait_ge(ld_bo, 16)
                dve.tensor_scalar(k.gated_bo[:], bo_b[:], k.gates[:, 0:1], None, ALU.mult).then_inc(consts, 1)

            @block.tensor
            def _(pe):
                pe.wait_ge(made, 4)
                pe.wait_ge(ld_ctx, 16)
                for c in range(KC):
                    for b in range(BATCH):
                        mm = pe.transpose(banks[:, c, b * KEYS:(b + 1) * KEYS], ctx_raw[:, b, c * P:(c + 1) * P],
                                          k.ident[0:KEYS, 0:KEYS])
                mm.then_inc(ctx_done, 1)

                def turn_weight(i):
                    pe.wait_ge(ld_w[i], 16)
                    for c in range(KC):
                        for o in range(KC):
                            mm = pe.transpose(banks[:, 4 + i, c * D + o * P:c * D + (o + 1) * P],
                                              w_raw[:, i, o, c * P:(c + 1) * P], k.ident[:])
                    mm.then_inc(wt_done, 1)

                for i in range(2):
                    turn_weight(i)
                pe.wait_ge(ld_bias, 64)
                pe.transpose(banks[:, 2, 0:n_bias + 3 * KC], bias_rows[:],
                             k.ident[0:n_bias + 3 * KC, 0:n_bias + 3 * KC]).then_inc(bias_done, 1)
                pe.wait_ge(ctx_sb, KC)
                pe.wait_ge(wt_sb, 1)
                for o in range(KC):
                    for c in range(KC):
                        mm = pe.matmul(banks[:, o, 0:BATCH * KEYS], wk_t[:, c, o * P:(o + 1) * P], ctx_t[:, c],
                                       start=(c == 0), stop=(c == KC - 1))
                    mm.then_inc(key_done, 1)
                pe.wait_ge(wt_sb, 2)
                for pair in range(BATCH // 2):
                    for j in range(2):
                        b = 2 * pair + j
                        for c in range(KC):
                            mm = pe.matmul(banks[0:KEYS, 4 + pair, j * D:(j + 1) * D],
                                           ctx_t[:, c, b * KEYS:(b + 1) * KEYS], wv_t[:, c],
                                           start=(c == 0), stop=(c == KC - 1))
                    mm.then_inc(v_done, 1)
                for i in range(2, 4):
                    turn_weight(i)


def attention_phase(nc, t, k, out, routed):
    S, A, B, C, DB = k.banks[:, 0:4], k.banks[:, 4], k.banks[:, 5], k.banks[:, 6], k.banks[:, 7]
    n_bias = E * HC
    HALF_LAYER = KC * HID // 2
    NT = MAX_TILES + 1
    x_rows = t["x"].rearrange("b s d -> (b s) d").rearrange("(j t p) d -> j p t d", t=2, p=P)
    out_rows = out[0:TOKENS, :].rearrange("(j t p) d -> j p t d", t=2, p=P)

    with ExitStack() as ctx:
        def sb(name, shape, dt=F32):
            return ctx.enter_context(nc.sbuf_tensor(name, shape, dt))

        def sem(name):
            return ctx.enter_context(nc.semaphore(name))

        lent = [w[:, E - 1].rearrange("p c n -> p (c n)").bitcast(F32) for w in (k.w2_hi, k.w2_lo)]
        x_res = lent[0].rearrange("p (b t d) -> p b t d", b=2, t=2)
        attn_t, x2_t = (lent[1][:, i * KC * PAIR:(i + 1) * KC * PAIR].rearrange("p (c n) -> p c n", c=KC)
                        for i in range(2))
        x_in, prob, row, pos, scat, x_in_ld = k.x_in, k.prob, k.row, k.pos, k.scat, k.x_in_ld
        q_hi, q_lo = (sb(n, [P, 2, KC, PAIR], F16) for n in ("q_hi", "q_lo"))
        x_norm = sb("x_norm", [P, 2, D])
        xn_t = sb("xn_t", [P, KC, PAIR])
        prob_t = sb("prob_t", [P, PCH, P])
        attn = sb("attn", [P, 2, D])
        stage = sb("stage", [P, 2, HALF_LAYER])
        top = sb("top", [P, 2, HEADS])
        den = sb("den", [P, 2, HEADS])
        stats = sb("stats", [P, 2, 2, 6])
        mv = sb("mv", [P, 2, 2, 2])
        var_eps = sb("var_eps", [P, 2, 2, 1])
        rstd = sb("rstd", [P, 2, 2, 1])
        neg_mean = sb("neg_mean", [P, 2, 1])
        offset = sb("offset", [P, 2, 1])
        logits = sb("logits", [P, 2, E])
        best = sb("best", [P, 2, E])
        best_i = sb("best_i", [P, 2, E], U32)
        l_shift = sb("l_shift", [P, 2, E])
        l_exp = sb("l_exp", [P, 2, E])
        l_sum = sb("l_sum", [P, 2])
        l_rec = sb("l_rec", [P, 2])
        share = sb("share", [P, 2, 2])
        best_f = sb("best_f", [P, 2, 2])
        mask = sb("mask", [P, 2, 2, E])
        weighed = sb("weighed", [P, 2, 2, E])
        chosen = sb("chosen", [P, 2, E], BF16)
        count = sb("count", [P, E])
        pad_at = sb("pad_at", [P, E], I32)
        count_i = sb("count_i", [P, E], I32)
        tiles_i = sb("tiles_i", [P, E], I32)
        tiles = sb("tiles", [P, E])
        upto_tiles = sb("upto_tiles", [P, E, E])
        end_of = sb("end_of", [P, E])
        expert_f = sb("expert_f", [P, NT])
        start_f = sb("start_f", [P, NT])
        row_f = sb("row_f", [P, NT])
        past = x_norm[:].rearrange("p t d -> p (t d)")[:, 0:NT * E].rearrange("p (n e) -> p n e", e=E)
        past_tiles = xn_t[:].rearrange("p c n -> p (c n)")[:, 0:NT * E].rearrange("p (n e) -> p n e", e=E)
        place = sb("place", [P, 2, E])
        placed = sb("placed", [P, 2, 2, E])

        x_res_ld = [sem(f"x_res_ld{i}") for i in range(2)]
        x2_st = [sem(f"x2_st{i}") for i in range(2)]
        stage_ld = [sem(f"stage_ld{i}") for i in range(2)]
        pad_st = sem("pad_st")
        score_ps, x2t_ps, pt_ps, av_ps, q_ps, logit_ps, ot_ps, wo_ps, xt_ps, rank_ps = (
            sem(n) for n in ("score_ps", "x2t_ps", "pt_ps", "av_ps", "q_ps", "logit_ps", "ot_ps", "wo_ps",
                             "xt_ps", "rank_ps"))
        x2t_sb, pt_sb, prob_abs, prob_exp, q_sb, ot_sb, xt_sb, router_exp, w_hi, norm2 = (
            sem(n) for n in ("x2t_sb", "pt_sb", "prob_abs", "prob_exp", "q_sb", "ot_sb", "xt_sb", "router_exp", "w_hi", "norm2"))
        q_lo_sb, top_sb, shift_sb, den_sb, attn_sb, stats1, norm1, x2_sb, stats2, router, places, w_scaled = (
            sem(n) for n in ("q_lo_sb", "top_sb", "shift_sb", "den_sb", "attn_sb", "stats1", "norm1", "x2_sb", "stats2",
                             "router", "places", "w_scaled"))
        factors1, factors2, res_bo, row_sb, w_lo = (
            sem(n) for n in ("factors1", "factors2", "res_bo", "row_sb", "w_lo"))
        FACTOR_OPS = (2, 4)
        ROUTER_OPS = 12
        PLACE_OPS = 5
        count_ps, plan, pads = sem("count_ps"), sem("plan"), sem("pads")
        PLAN_OPS = 16

        def staged(m, par):
            return exists(2 * m + par)

        def converted(m, par):
            return staged(m, par) and (not isinstance(m, int) or (m, par) != (E - 1, 1))

        def halves(m, par):
            hi, lo = ((k.w1_hi, k.w1_lo), (k.w2_hi, k.w2_lo))[par]
            return [w[:, bass.ds(m, 1)].rearrange("p a c n -> p (a c n)") for w in (hi, lo)]

        def write_padding(eng, experts):
            eng.wait_ge(plan, 1)
            for e in experts:
                at = eng.value_load(pad_at[0:1, e:e + 1], min_val=0, max_val=E * REGION - SLOTS)
                eng.dma_start(routed[bass.ds(at, SLOTS), :].rearrange("(t p) r -> p t r", p=P), k.pad_rows[:])\
                    .then_inc(pads, 16)

        with nc.Block() as block:
            @block.sync
            def _(sp):
                place_values(sp, k, value_pieces()[EARLY_PIECES:LATE_PIECES], k.v_placed[0])

                def step(m, par):
                    j, mj, pj = item(m, par, 2)
                    if exists(j) and exists(j - 2):
                        ready(sp, norm1, j - 2, 2)
                        sp.dma_start(x_in[:, pj], x_rows[bass.ds(j, 1)].rearrange("a p t d -> p (a t) d"))\
                            .then_inc(x_in_ld[pj], 16)
                    if staged(m, par):
                        w = t["L0_ffn_w1"] if par == 0 else t["L0_ffn_w2"]
                        rows = w.shape[1] // 2
                        for half in range(2):
                            ready(sp, w_lo, 2 * m + par - 1, 2, half + 1)
                            sp.dma_start(stage[:, half].rearrange("p (c n) -> p c n", n=w.shape[2]),
                                         w[bass.ds(m, 1), half * rows:(half + 1) * rows].rearrange(
                                             "a (c p) n -> p (a c) n", p=P)).then_inc(stage_ld[half], 16)
                    j, mj, pj = item(m, par, -2)
                    if exists(j):
                        ready(sp, x2_sb, j)
                        sp.dma_start(out_rows[bass.ds(j, 1)].rearrange("a p t d -> p (a t) d"), x_res[:, pj])\
                            .then_inc(x2_st[pj], 16)
                    j, mj, pj = item(m, par, 0)
                    if exists(j):
                        ready(sp, norm2, j - 2, 2)
                        ready(sp, x2_st[pj], mj - 1, 16)
                        sp.dma_start(x_res[:, pj], x_rows[bass.ds(j, 1)].rearrange("a p t d -> p (a t) d"))\
                            .then_inc(x_res_ld[pj], 16)
                    if isinstance(j, int) and j == 0:
                        place_values(sp, k, value_pieces()[LATE_PIECES:], k.v_placed[0])

                pipeline(sp, step)
                sp.dma_start(routed[E * REGION:ROUTED, :].rearrange("(t p) r -> p t r", p=P),
                             k.pad_rows[:]).then_inc(pad_st, 16)
                write_padding(sp, range(0, E // 2))
                for i in range(2):
                    sp.wait_ge(x2_st[i], 16 * PAIRS // 2)
                sp.wait_ge(pad_st, 16)
                sp.wait_ge(pads, 16 * E)

            @block.gpsimd
            def _(pool):
                def norm_factors(n, stat, factors, used, j):
                    ready(pool, used, j - 1, 2)
                    settled(pool, stat, j, 4)
                    pool.tensor_scalar(var_eps[:, n], mv[:, n, :, 1:2], LN_EPS, None, ALU.add)\
                        .then_inc(factors, 1)
                    if n == 1:
                        pool.tensor_scalar(neg_mean[:], mv[:, n, :, 0:1], -1.0, None, ALU.mult)\
                            .then_inc(factors, 1)
                    ready(pool, factors, j, FACTOR_OPS[n], FACTOR_OPS[n] // 2)
                    pool.tensor_tensor(rstd[:, n], var_eps[:, n],
                                       k.minus_half[:].unsqueeze(2).to_broadcast([P, 2, 1]), ALU.pow)\
                        .then_inc(factors, 1)
                    if n == 1:
                        ready(pool, factors, j, 4, 3)
                        pool.tensor_tensor(offset[:], neg_mean[:], rstd[:, n], ALU.mult).then_inc(factors, 1)

                def step(m, par):
                    j, mj, pj = item(m, par, -2)
                    if exists(j):
                        norm_factors(1, stats2, factors2, norm2, j)
                    j, mj, pj = item(m, par, -3)
                    if exists(j):
                        ready(pool, router, j, ROUTER_OPS)
                        pool.tensor_tensor(weighed[:], mask[:], share[:].unsqueeze(3).to_broadcast([P, 2, 2, E]),
                                           ALU.mult).then_inc(row_sb, 1)
                        pool.tensor_copy(row[:, pj, :, ROW - 1:ROW].bitcast(I32),
                                         k.token_no[:, bass.ds(2 * j, 2)].unsqueeze(2)).then_inc(row_sb, 1)
                        ready(pool, row_sb, j, 3, 1)
                        pool.tensor_tensor(row[:, pj, :, D:D + E], weighed[:, :, 0], weighed[:, :, 1], ALU.add)\
                            .then_inc(row_sb, 1)
                    j, mj, pj = item(m, par, -3)
                    if exists(j):
                        ready(pool, row_sb, j, 3)
                        settled(pool, places, j, PLACE_OPS, 4)
                        for tile in range(2):
                            for choice in range(2):
                                pool.indirect_dma_start(
                                    routed[:, :], bass.IndirectOffsetOnAxis(ap=pos[:, pj, tile, choice:choice + 1], axis=0),
                                    row[:, pj, tile], None).then_inc(scat[pj], 16)
                    j, mj, pj = item(m, par, 2)
                    if exists(j):
                        norm_factors(0, stats1, factors1, norm1, j)
                    j, mj, pj = item(m, par, -1)
                    if exists(j):
                        ready(pool, x_res_ld[pj], mj, 16)
                        pool.tensor_tensor(x_res[:, pj], x_res[:, pj],
                                           k.gated_bo[:].unsqueeze(1).to_broadcast([P, 2, D]), ALU.add)\
                            .then_inc(res_bo, 1)
                    if converted(m, par):
                        hi, lo = halves(m, par)
                        for half in range(2):
                            cols = slice(half * HALF_LAYER, (half + 1) * HALF_LAYER)
                            ready(pool, w_hi, 2 * m + par, 2, half + 1)
                            pool.tensor_tensor(lo[:, cols], stage[:, half], hi[:, cols], ALU.subtract).then_inc(w_lo, 1)

                pipeline(pool, step)

            @block.scalar
            def _(act):
                def copy_prob_t(j, tile, groups):
                    for g in groups:
                        first, n = ((0, 4), (4, 4), (8, 2))[g]
                        ready(act, pt_ps, 2 * j + tile, 3, g + 1)
                        bank = (A, B, A)[g]
                        if g < 2:
                            act.activation(prob_t[:, first:first + n, :].rearrange("p c n -> p (c n)"),
                                           bank[:, 0:n * P], ACT.Copy).then_inc(pt_sb, 1)
                        else:
                            act.activation(prob_t[:, first, :], bank[:, 0:P], ACT.Copy).then_inc(pt_sb, 1)
                            r = chunk_rows(first + 1)
                            act.activation(prob_t[0:r, first + 1, :], bank[0:r, P:2 * P], ACT.Copy)\
                                .then_inc(pt_sb, 1)

                def absolute_scores(j, tile):
                    ready(act, score_ps, j, 2, tile + 1)
                    ready(act, pt_ps, 2 * (j - 1) + tile, 3)
                    if isinstance(j, int) and 2 * j + tile == 1:
                        values_placed(act, k)
                    act.activation(prob[:, tile].rearrange("p (q n) -> p q n", q=4), S[:, :, 0:QUAD], ACT.Abs)\
                        .then_inc(prob_abs, 1)

                def exponentials(j, tile):
                    ready(act, shift_sb, j, 2, tile + 1)
                    act.activation(prob[:, tile], prob[:, tile], ACT.Exp, scale=DH ** -0.5).then_inc(prob_exp, 1)

                def high_half(m, par, half):
                    hi, lo = halves(m, par)
                    ready(act, w_scaled, 2 * m + par, 2, half + 1)
                    act.activation(hi[:, half * HALF_LAYER:(half + 1) * HALF_LAYER], stage[:, half], ACT.Copy)\
                        .then_inc(w_hi, 1)

                def step(m, par):
                    j, mj, pj = item(m, par, 0)
                    if exists(j):
                        absolute_scores(j, 0)
                    j, mj, pj = item(m, par, -1)
                    if exists(j):
                        ready(act, av_ps, 2 * j)
                        copy_prob_t(j, 1, (0, 1))
                    j, mj, pj = item(m, par, -2)
                    if exists(j):
                        ready(act, factors2, j, FACTOR_OPS[1])
                        ready(act, scat[pj], mj - 1, 64)
                        for tile in range(2):
                            act.activation(row[:, pj, tile, 0:D], x_res[:, pj, tile], ACT.Identity,
                                           scale=rstd[:, 1, tile, 0:1], bias=offset[:, tile, 0:1]).then_inc(norm2, 1)
                    j, mj, pj = item(m, par, 1)
                    if exists(j):
                        ready(act, q_ps, j)
                        ready(act, score_ps, j - 2, 2)
                        for c in range(KC):
                            act.activation(q_hi[:, pj, c], C[:, c * PAIR:(c + 1) * PAIR], ACT.Identity,
                                           bias=k.bias_t[:, n_bias + c:n_bias + c + 1]).then_inc(q_sb, 1)
                    j, mj, pj = item(m, par, -1)
                    if exists(j):
                        copy_prob_t(j, 1, (2,))
                    j, mj, pj = item(m, par, 0)
                    if exists(j):
                        exponentials(j, 0)
                    if converted(m, par):
                        high_half(m, par, 0)
                    j, mj, pj = item(m, par, 0)
                    if exists(j):
                        absolute_scores(j, 1)
                    j, mj, pj = item(m, par, -2)
                    if exists(j):
                        ready(act, x2t_ps, j)
                        ready(act, logit_ps, j - 1)
                        act.activation(x2_t.rearrange("p c n -> p (c n)"), C, ACT.Copy).then_inc(x2t_sb, 1)
                    j, mj, pj = item(m, par, -1)
                    if exists(j):
                        ready(act, ot_ps, j)
                        ready(act, wo_ps, j - 1)
                        for c in range(KC):
                            act.activation(attn_t[:, c], DB[:, c * PAIR:(c + 1) * PAIR], ACT.Identity,
                                           bias=k.bias_t[:, n_bias + 2 * KC + c:n_bias + 2 * KC + c + 1])\
                                .then_inc(ot_sb, 1)
                    j, mj, pj = item(m, par, 0)
                    if exists(j):
                        ready(act, av_ps, 2 * j - 1)
                        copy_prob_t(j, 0, (0, 1))
                    if converted(m, par):
                        high_half(m, par, 1)
                    if exists(j):
                        copy_prob_t(j, 0, (2,))
                    j, mj, pj = item(m, par, -2)
                    if exists(j):
                        ready(act, router, j, ROUTER_OPS, 4)
                        act.activation(l_exp[:], l_shift[:], ACT.Exp).then_inc(router_exp, 1)
                    j, mj, pj = item(m, par, 0)
                    if exists(j):
                        exponentials(j, 1)
                    j, mj, pj = item(m, par, 2)
                    if exists(j):
                        ready(act, xt_ps, j)
                        ready(act, q_ps, j - 1)
                        act.activation(xn_t[:].rearrange("p c n -> p (c n)"), B, ACT.Copy).then_inc(xt_sb, 1)

                pipeline(act, step)
                act.wait_ge(logit_ps, PAIRS)
                act.wait_ge(norm2, 2 * PAIRS)
                for i in range(2):
                    act.wait_ge(x2_st[i], 16 * PAIRS // 2)
                for half in range(2):
                    high_half(E - 1, 1, half)
                write_padding(act, range(E // 2, E))

            @block.vector
            def _(dve):
                def heads_of(tile):
                    return prob[:, tile].rearrange("p (h k) -> p h k", k=KEYS)

                def top_scores(j, tile):
                    ready(dve, prob_abs, j, 2, tile + 1)
                    dve.tensor_reduce(top[:, tile], heads_of(tile), AX.X, ALU.max).then_inc(top_sb, 1)

                def shift_scores(j, tile):
                    ready(dve, top_sb, j, 2, tile + 1)
                    dve.tensor_tensor(heads_of(tile), heads_of(tile),
                                      top[:, tile].unsqueeze(2).to_broadcast([P, HEADS, KEYS]),
                                      ALU.subtract).then_inc(shift_sb, 1)

                values = DB[:, 0:HEADS * VW].rearrange("p (h w) -> p h w", w=VW)

                def inverse_sums(j, tile):
                    ready(dve, av_ps, j, 2, tile + 1)
                    dve.reciprocal(den[:, tile], values[:, :, DH]).then_inc(den_sb, 1)

                def normalise_attn(j, tile):
                    ready(dve, den_sb, j, 2, tile + 1)
                    ready(dve, ot_ps, j - 1)
                    dve.tensor_tensor(attn[:, tile].rearrange("p (h d) -> p h d", d=DH), values[:, :, 0:DH],
                                      den[:, tile].unsqueeze(2).to_broadcast([P, HEADS, DH]), ALU.mult)\
                        .then_inc(attn_sb, 1)

                def statistics(n, stat, x, j, tile):
                    if tile == 0:
                        ready(dve, stat, j - 1, 4)
                    dve.bn_stats(stats[:, n, tile], x[:, tile]).then_inc(stat, 1)

                def aggregate(n, stat, factors, j):
                    ready(dve, factors, j - 1, FACTOR_OPS[n])
                    settled(dve, stat, j, 4, 2)
                    for tile in range(2):
                        dve.bn_aggr(mv[:, n, tile], stats[:, n, tile]).then_inc(stat, 1)

                def scale_weights(layer, half):
                    ready(dve, stage_ld[half], layer, 16)
                    dve.tensor_scalar(stage[:, half], stage[:, half], W_SCALE, None, ALU.mult).then_inc(w_scaled, 1)

                def route(j, part, wait=None):
                    if part == 1:
                        ready(dve, logit_ps, j)
                    if part == 10:
                        ready(dve, router_exp, j)
                    if wait:
                        (settled if part in (2, 5) else ready)(dve, router, j, ROUTER_OPS, wait)
                    if part == 1:
                        dve.tensor_copy(logits[:].rearrange("p t e -> p (t e)"), C[:, 0:2 * E]).then_inc(router, 1)
                    if part == 2:
                        for tile in range(2):
                            dve.max(best[:, tile], logits[:, tile]).then_inc(router, 1)
                    if part == 4:
                        dve.tensor_tensor(l_shift[:], best[:], best[:, :, 0:1].to_broadcast([P, 2, E]), ALU.subtract)\
                            .then_inc(router, 1)
                    if part == 5:
                        for tile in range(2):
                            dve.max_index(best_i[:, tile], best[:, tile], logits[:, tile]).then_inc(router, 1)
                    if part == 7:
                        dve.tensor_copy(best_f[:], best_i[:, :, 0:2]).then_inc(router, 1)
                    if part == 8:
                        ready(dve, row_sb, j - 1, 3)
                        dve.tensor_tensor(mask[:], k.expert_no[:].unsqueeze(1).unsqueeze(1).to_broadcast([P, 2, 2, E]),
                                          best_f[:].unsqueeze(3).to_broadcast([P, 2, 2, E]), ALU.is_equal)\
                            .then_inc(router, 1)
                    if part == 9:
                        dve.tensor_tensor(chosen[:], mask[:, :, 0], mask[:, :, 1], ALU.add).then_inc(router, 1)
                    if part == 10:
                        dve.tensor_reduce(l_sum[:], l_exp[:], AX.X, ALU.add).then_inc(router, 1)
                    if part == 11:
                        dve.reciprocal(l_rec[:], l_sum[:]).then_inc(router, 1)
                    if part == 12:
                        dve.tensor_tensor(share[:], l_exp[:, :, 0:2], l_rec[:].unsqueeze(2).to_broadcast([P, 2, 2]),
                                          ALU.mult).then_inc(router, 1)

                def step(m, par):
                    here, last, before_last, placed_pair, coming = (
                        exists(2 * m + par + shift) for shift in (0, -1, -2, -3, 2))
                    i0, i1, i2, i3, n1, n2 = (item(m, par, shift)[0] for shift in (0, -1, -2, -3, 1, 2))
                    x_coming, x_last = x_in[:, par], x_res[:, 1 - par]

                    if staged(m, par):
                        scale_weights(2 * m + par, 0)
                    if placed_pair:
                        ready(dve, rank_ps, i3)
                        dve.tensor_tensor(place[:], C[:, 0:2 * E].rearrange("p (t e) -> p t e", e=E),
                                          k.region_of[:].unsqueeze(1).to_broadcast([P, 2, E]), ALU.add)\
                            .then_inc(places, 1)
                        dve.tensor_tensor(k.seen[:], k.seen[:], chosen[:, 0], ALU.add).then_inc(places, 1)
                        ready(dve, places, i3, PLACE_OPS, 1)
                        dve.tensor_tensor(placed[:], mask[:], place[:].unsqueeze(2).to_broadcast([P, 2, 2, E]),
                                          ALU.mult).then_inc(places, 1)
                        ready(dve, places, i3, PLACE_OPS, 3)
                        with nc.allow_low_precision(reason="whole numbers below 2**24"):
                            dve.tensor_reduce(pos[:, 1 - par], placed[:], AX.X, ALU.add).then_inc(places, 1)
                        dve.tensor_tensor(k.seen[:], k.seen[:], chosen[:, 1], ALU.add).then_inc(places, 1)
                    if here:
                        top_scores(i0, 0)
                        shift_scores(i0, 0)
                    if coming:
                        ready(dve, x_in_ld[par], item(m, par, 2)[1], 16)
                        statistics(0, stats1, x_coming, n2, 0)
                        statistics(0, stats1, x_coming, n2, 1)
                    if last:
                        inverse_sums(i1, 1)
                    if coming:
                        aggregate(0, stats1, factors1, n2)
                    if exists(n1):
                        ready(dve, q_sb, n1, KC)
                        for c in range(KC):
                            dve.scalar_tensor_tensor(q_lo[:, 1 - par, c], C[:, c * PAIR:(c + 1) * PAIR],
                                                     k.bias_t[:, n_bias + c:n_bias + c + 1], q_hi[:, 1 - par, c],
                                                     ALU.add, ALU.subtract).then_inc(q_lo_sb, 1)
                    if last:
                        normalise_attn(i1, 1)
                    if coming:
                        ready(dve, factors1, n2, FACTOR_OPS[0])
                        ready(dve, xt_ps, n2 - 1)
                        for tile in range(2):
                            dve.tensor_scalar(x_norm[:, tile], x_coming[:, tile], mv[:, 0, tile, 0:1],
                                              rstd[:, 0, tile, 0:1], ALU.subtract, ALU.mult).then_inc(norm1, 1)
                    if staged(m, par):
                        scale_weights(2 * m + par, 1)
                    if here:
                        top_scores(i0, 1)
                    if before_last:
                        route(i2, 1)
                    if here:
                        shift_scores(i0, 1)
                    if before_last:
                        route(i2, 2, 1)
                    if before_last:
                        route(i2, 4, 3)
                        route(i2, 5)
                    if last:
                        ready(dve, wo_ps, i1)
                        ready(dve, res_bo, i1)
                        dve.scalar_tensor_tensor(x_last.rearrange("p t d -> p (t d)"), C, k.gates[:, 0:1],
                                                 x_last.rearrange("p t d -> p (t d)"), ALU.mult, ALU.add)\
                            .then_inc(x2_sb, 1)
                    if before_last:
                        route(i2, 7, 6)
                    if last:
                        ready(dve, x2_sb, i1)
                        statistics(1, stats2, x_last, i1, 0)
                    if before_last:
                        route(i2, 8, 7)
                    if last:
                        statistics(1, stats2, x_last, i1, 1)
                    if here:
                        inverse_sums(i0, 0)
                    if before_last:
                        route(i2, 9, 8)
                    if here:
                        normalise_attn(i0, 0)
                    if last:
                        aggregate(1, stats2, factors2, i1)
                    if before_last:
                        route(i2, 10)
                        route(i2, 11, 10)
                        route(i2, 12, 11)

                pipeline(dve, step)

                def done(part):
                    dve.wait_ge(plan, part)

                dve.wait_ge(count_ps, 1)
                dve.tensor_tensor(pad_at[:], C[:, 0:E], k.region_of[:], ALU.add).then_inc(plan, 1)
                dve.tensor_scalar(count[:], C[:, 0:E], float(SLOTS - 1), None, ALU.add).then_inc(plan, 1)
                done(2)
                dve.tensor_copy(count_i[:], count[:]).then_inc(plan, 1)
                done(3)
                dve.tensor_scalar(tiles_i[:], count_i[:], SLOTS.bit_length() - 1, None, ALU.logical_shift_right)\
                    .then_inc(plan, 1)
                done(4)
                dve.tensor_copy(tiles[:], tiles_i[:]).then_inc(plan, 1)
                done(5)
                dve.tensor_tensor(upto_tiles[:], k.upto[:], tiles[:].unsqueeze(1).to_broadcast([P, E, E]), ALU.mult)\
                    .then_inc(plan, 1)
                done(6)
                dve.tensor_reduce(end_of[:], upto_tiles[:], AX.X, ALU.add).then_inc(plan, 1)
                done(7)
                dve.wait_ge(xt_ps, PAIRS)
                dve.wait_ge(q_ps, PAIRS)
                dve.tensor_tensor(past[:], k.tile_no[:].unsqueeze(2).to_broadcast([P, NT, E]),
                                  end_of[:].unsqueeze(1).to_broadcast([P, NT, E]), ALU.is_ge).then_inc(plan, 1)
                done(8)
                dve.tensor_tensor(past_tiles[:], past[:], tiles[:].unsqueeze(1).to_broadcast([P, NT, E]), ALU.mult)\
                    .then_inc(plan, 1)
                dve.tensor_reduce(expert_f[:], past[:], AX.X, ALU.add).then_inc(plan, 1)
                done(9)
                dve.tensor_reduce(start_f[:], past_tiles[:], AX.X, ALU.add).then_inc(plan, 1)
                done(11)
                dve.tensor_tensor(row_f[:], k.tile_no[:], start_f[:], ALU.subtract).then_inc(plan, 1)
                dve.tensor_scalar(k.expert_of[:], expert_f[:], float(E - 1), None, ALU.min).then_inc(plan, 1)
                done(13)
                dve.tensor_scalar(expert_f[:], expert_f[:], float(REGION), None, ALU.mult).then_inc(plan, 1)
                done(14)
                dve.scalar_tensor_tensor(row_f[:], row_f[:], float(SLOTS), expert_f[:], ALU.mult, ALU.add)\
                    .then_inc(plan, 1)
                done(15)
                dve.tensor_scalar(k.row_of[:], row_f[:], float(E * REGION), None, ALU.min).then_inc(plan, 1)
                hi, lo = halves(E - 1, 1)
                for half in range(2):
                    cols = slice(half * HALF_LAYER, (half + 1) * HALF_LAYER)
                    ready(dve, w_hi, 2 * E - 1, 2, half + 1)
                    dve.tensor_tensor(lo[:, cols], stage[:, half], hi[:, cols], ALU.subtract).then_inc(w_lo, 1)

            @block.tensor
            def _(pe):
                def scores(m, par, tile):
                    j, mj, pj = item(m, par, 0)
                    b = batch_of(m, par, 0)
                    ready(pe, q_lo_sb, j, KC)
                    ready(pe, prob_abs, 2 * j + tile - 1)
                    for q in range(4):
                        c = q // 2
                        for n, (rows, keys) in enumerate(((q_hi, k.keys_hi), (q_hi, k.keys_lo), (q_lo, k.keys_hi))):
                            mm = pe.matmul(S[:, q, 0:QUAD], rows[:, pj, c, tile * P:(tile + 1) * P],
                                           keys[:, bass.ds(b, 1), q * QUAD:(q + 1) * QUAD].rearrange("p a n -> p (a n)"),
                                           start=(n == 0), stop=(n == 2))
                    mm.then_inc(score_ps, 1)

                def turn_probs(j, tile, groups):
                    for g in groups:
                        if g == 2:
                            ready(pe, pt_sb, 2 * j + tile, 4, 1)
                        for i, c in enumerate((range(0, 4), range(4, 8), range(8, PCH))[g]):
                            r = chunk_rows(c)
                            mm = pe.transpose((A, B, A)[g][0:r, i * P:(i + 1) * P], prob[:, tile, c * P:c * P + r],
                                              k.ident[:])
                        mm.then_inc(pt_ps, 1)

                def values(m, par, shift, tile):
                    j, mj, pj = item(m, par, shift)
                    b = batch_of(m, par, shift)
                    if isinstance(j, int) and 2 * j + tile == 0:
                        values_placed(pe, k)
                    for c in range(PCH):
                        ready(pe, pt_sb, 2 * j + tile, 4, (1, 1, 1, 1, 2, 2, 2, 2, 3, 4)[c])
                        first, n = chunk_heads(c)
                        r = chunk_rows(c)
                        mm = pe.matmul(DB[:, first * VW:(first + n) * VW], prob_t[0:r, c, :],
                                       k.v_rows[0:r, bass.ds(b, 1), c, 0:n * VW].rearrange("p a n -> p (a n)"),
                                       start=(c == 0), stop=(c == PCH - 1), skip_group_check=True)
                    mm.then_inc(av_ps, 1)

                def turn_pair(dst, src, done):
                    for c in range(KC):
                        for tile in range(2):
                            mm = pe.transpose(dst[:, c * PAIR + tile * P:c * PAIR + (tile + 1) * P],
                                              src[:, tile, c * P:(c + 1) * P], k.ident[:])
                    mm.then_inc(done, 1)

                def step(m, par):
                    here, last, before_last, placed_pair, next_pair, coming = (
                        exists(2 * m + par + shift) for shift in (0, -1, -2, -3, 1, 2))
                    i0, i1, i2, i3, n1, n2 = (item(m, par, shift)[0] for shift in (0, -1, -2, -3, 1, 2))
                    if here:
                        scores(m, par, 0)
                    if placed_pair:
                        ready(pe, router, i3, ROUTER_OPS, 9)
                        ready(pe, places, i3 - 1, PLACE_OPS)
                        if exists(i3 + 1):
                            ready(pe, x2_sb, i3 + 1)
                        pe.matmul(C[:, 0:E], k.before[:], chosen[:, 0], start=True, stop=False)
                        pe.matmul(C[:, 0:E], k.ones[:], k.seen[:], start=False, stop=True)
                        pe.matmul(C[:, E:2 * E], k.before[:], chosen[:, 1], start=True, stop=False)
                        pe.matmul(C[:, E:2 * E], k.ones[:], k.seen[:], start=False, stop=False)
                        pe.matmul(C[:, E:2 * E], k.ones[:], chosen[:, 0], start=False, stop=True)\
                            .then_inc(rank_ps, 1)
                    if last:
                        ready(pe, prob_exp, i1, 2, 2)
                        ready(pe, pt_sb, 2 * i1, 4)
                        if exists(i1 + 2):
                            ready(pe, xt_sb, i1 + 2)
                        turn_probs(i1, 1, (0, 1))
                    if next_pair:
                        ready(pe, xt_sb, n1)
                        ready(pe, x2_sb, n1 - 3)
                        ready(pe, places, n1 - 4, PLACE_OPS, 1)
                        for o in range(KC):
                            for c in range(KC):
                                mm = pe.matmul(C[:, o * PAIR:(o + 1) * PAIR], k.wq_t[:, c, o * P:(o + 1) * P],
                                               xn_t[:, c], start=(c == 0), stop=(c == KC - 1))
                        mm.then_inc(q_ps, 1)
                    if last:
                        turn_probs(i1, 1, (2,))
                        ready(pe, attn_sb, i1, 2, 1)
                        values(m, par, -1, 1)
                    if here:
                        scores(m, par, 1)
                    if before_last:
                        ready(pe, norm2, i2, 2)
                        if exists(i2 + 3):
                            ready(pe, q_lo_sb, i2 + 3, KC)
                        ready(pe, places, i2 - 1, PLACE_OPS, 1)
                        turn_pair(C, row[:, par, :, 0:D], x2t_ps)
                    if last:
                        ready(pe, attn_sb, i1, 2)
                        turn_pair(DB, attn, ot_ps)
                    if here:
                        ready(pe, prob_exp, i0, 2, 1)
                        ready(pe, pt_sb, 2 * i0 - 1, 4)
                        ready(pe, xt_sb, n1 if exists(n1) else PAIRS - 1)
                        turn_probs(i0, 0, (0,))
                    if before_last:
                        ready(pe, x2t_sb, i2)
                        for tile in range(2):
                            for c in range(KC):
                                mm = pe.matmul(C[:, tile * E:(tile + 1) * E], x2_t[:, c, tile * P:(tile + 1) * P],
                                               k.w_router[:, c], start=(c == 0), stop=(c == KC - 1))
                        mm.then_inc(logit_ps, 1)
                    if here:
                        turn_probs(i0, 0, (1,))
                    if last:
                        ready(pe, ot_sb, i1, KC)
                        if next_pair:
                            ready(pe, q_lo_sb, n1, KC)
                        ready(pe, router, i2, ROUTER_OPS, 1)
                        for tile in range(2):
                            for c in range(KC):
                                mm = pe.matmul(C[:, tile * D:(tile + 1) * D], attn_t[:, c, tile * P:(tile + 1) * P],
                                               k.wo_t[:, c], start=(c == 0), stop=(c == KC - 1))
                        mm.then_inc(wo_ps, 1)
                    if here:
                        turn_probs(i0, 0, (2,))
                        ready(pe, ot_sb, i0 - 1, KC)
                        values(m, par, 0, 0)
                    if coming:
                        ready(pe, norm1, n2, 2)
                        ready(pe, xt_sb, n2 - 1)
                        ready(pe, pt_sb, 2 * (n2 - 2), 4, 2)
                        turn_pair(B, x_norm, xt_ps)

                pipeline(pe, step)
                pe.wait_ge(places, PLACE_OPS * PAIRS)
                pe.matmul(C[:, 0:E], k.ones[:], k.seen[:], start=True, stop=True).then_inc(count_ps, 1)


LOOP_TILES = range(4, MAX_TILES - 3 - (MAX_TILES - 3) % 2)


def tile_exists(tile):
    return not isinstance(tile, int) or 0 <= tile < MAX_TILES


def tile_pipeline(eng, step):
    for s in range(-2, LOOP_TILES.start):
        step(s // 2, s % 2)
    with eng.Fori(LOOP_TILES.start // 2, LOOP_TILES.stop // 2) as m:
        for par in range(2):
            step(m, par)
    for s in range(LOOP_TILES.stop, MAX_TILES + 2):
        step(s // 2, s % 2)


def expert_phase(nc, t, k, out, routed):
    S, A = k.banks[:, 0:4], k.banks[:, 4]
    Y = [k.banks[:, 6], k.banks[:, 7]]
    BANKS = 4
    PER = HC // BANKS

    with ExitStack() as ctx:
        def sb(name, shape, dt=F32):
            return ctx.enter_context(nc.sbuf_tensor(name, shape, dt))

        def sem(name):
            return ctx.enter_context(nc.semaphore(name))

        x_row = sb("x_row", [P, 2, SB, ROW])
        meta = sb("meta", [P, 2, SB, E + 1])
        x_hi = sb("x_hi", [P, KC, SLOTS], F16)
        x_lo = sb("x_lo", [P, KC, SLOTS], F16)
        hid = sb("hid", [P, HC, SLOTS])
        h_hi = sb("h_hi", [P, 2, HC, SLOTS], F16)
        h_lo = sb("h_lo", [P, 2, HC, SLOTS], F16)
        y = sb("y", [P, 2, SB, D])
        b2_b = sb("b2_b", [P, E, D])
        b2_ld = sem("b2_ld")
        row_ld = [sem(f"row_ld{i}") for i in range(2)]
        added = [sem(f"added{i}") for i in range(2)]
        xt_done, x_hi_sb, x_lo_sb = sem("xt_done"), sem("x_hi_sb"), sem("x_lo_sb")
        hid_ps, hid_sb, h_hi_sb, h_lo_sb = (sem(n) for n in ("hid_ps", "hid_sb", "h_hi_sb", "h_lo_sb"))
        y_ps, y_bias, y_sb, meta_sb = (sem(n) for n in ("y_ps", "y_bias", "y_sb", "meta_sb"))

        def expert(eng, tile):
            return eng.value_load(k.expert_of[0:1, bass.ds(tile, 1)], min_val=0, max_val=E - 1)

        with nc.Block() as block:
            @block.sync
            def _(sp):
                for i in range(2):
                    sp.wait_ge(k.scat[i], 64 * PAIRS // 2)

                def step(m, par):
                    j, mj, pj = item(m, par, 2)
                    if tile_exists(j):
                        ready(sp, xt_done, j - 2)
                        ready(sp, meta_sb, j - 2)
                        at = sp.value_load(k.row_of[0:1, bass.ds(j, 1)], min_val=0, max_val=E * REGION)
                        sp.dma_start(x_row[:, pj], routed[bass.ds(at, SLOTS), :].rearrange("(t p) r -> p t r", p=P))\
                            .then_inc(row_ld[pj], 16)
                    if isinstance(m, int) and 2 * m + par == -1:
                        sp.dma_start(b2_b[:].rearrange("p e d -> p (e d)"),
                                     t["L0_ffn_b2"].rearrange("e d -> (e d)").partition_broadcast(P)).then_inc(b2_ld, 16)

                tile_pipeline(sp, step)

            @block.gpsimd
            def _(pool):
                def step(m, par):
                    j, mj, pj = item(m, par, -2)
                    if tile_exists(j):
                        ready(pool, y_sb, j, SB)
                        settled(pool, added[1 - pj], mj - (pj == 0), 16 * SB)
                        for b in range(SB):
                            pool.indirect_dma_start(
                                out[:, :], bass.IndirectOffsetOnAxis(ap=meta[:, pj, b, E:E + 1].bitcast(U32), axis=0),
                                y[:, pj, b], None, compute_op=ALU.add).then_inc(added[pj], 16)
                    j, mj, pj = item(m, par, 0)
                    if tile_exists(j):
                        ready(pool, added[pj], mj - 1, 16 * SB)
                        ready(pool, y_sb, j - 2, SB)
                        settled(pool, row_ld[pj], mj, 16)
                        pool.tensor_copy(meta[:, pj], x_row[:, pj, :, D:ROW]).then_inc(meta_sb, 1)

                tile_pipeline(pool, step)
                for i in range(2):
                    pool.wait_ge(added[i], 16 * SB * ((MAX_TILES + 1 - i) // 2))

            @block.scalar
            def _(act):
                def step(m, par):
                    j, mj, pj = item(m, par, 0)
                    if tile_exists(j):
                        e = expert(act, j)
                        for q in range(BANKS):
                            ready(act, hid_ps, j, BANKS, q + 1)
                            ready(act, h_lo_sb, j - 1, BANKS, q + 1)
                            for c in range(q * PER, (q + 1) * PER):
                                ins = act.activation(hid[:, c], S[:, q, c % PER * SLOTS:(c % PER + 1) * SLOTS],
                                                     ACT.Gelu_apprx_tanh, bias=k.bias_t[:, bass.ds(e * HC + c, 1)],
                                                     scale=1.0 / W_SCALE)
                            ins.then_inc(hid_sb, 1)
                    j, mj, pj = item(m, par, 1)
                    if tile_exists(j):
                        ready(act, xt_done, j)
                        ready(act, hid_ps, j - 1, BANKS)
                        ready(act, x_lo_sb, j - 1)
                        act.activation(x_hi[:].rearrange("p c n -> p (c n)"), A, ACT.Copy).then_inc(x_hi_sb, 1)

                tile_pipeline(act, step)

            @block.vector
            def _(dve):
                def step(m, par):
                    j, mj, pj = item(m, par, 0)
                    if tile_exists(j):
                        for q in range(BANKS):
                            part = slice(q * PER, (q + 1) * PER)
                            ready(dve, hid_sb, j, BANKS, q + 1)
                            ready(dve, y_ps, j - 2)
                            dve.tensor_copy(h_hi[:, pj, part], hid[:, part]).then_inc(h_hi_sb, 1)
                            ready(dve, h_hi_sb, j, BANKS, q + 1)
                            dve.tensor_tensor(h_lo[:, pj, part], hid[:, part], h_hi[:, pj, part], ALU.subtract)\
                                .then_inc(h_lo_sb, 1)
                    j, mj, pj = item(m, par, 1)
                    if tile_exists(j):
                        ready(dve, x_hi_sb, j)
                        dve.tensor_tensor(x_lo[:].rearrange("p c n -> p (c n)"), A,
                                          x_hi[:].rearrange("p c n -> p (c n)"), ALU.subtract).then_inc(x_lo_sb, 1)
                    j, mj, pj = item(m, par, -1)
                    if tile_exists(j):
                        e = expert(dve, j)
                        ready(dve, y_ps, j)
                        if isinstance(j, int) and j == 0:
                            dve.wait_ge(b2_ld, 16)
                        ready(dve, added[pj], mj - 1, 16 * SB)
                        dve.scalar_tensor_tensor(y[:, pj], Y[pj].rearrange("p (b d) -> p b d", d=D), 1.0 / W_SCALE,
                                                 b2_b[:, bass.ds(e, 1), :].to_broadcast([P, SB, D]),
                                                 ALU.mult, ALU.add)\
                            .then_inc(y_bias, 1)
                        ready(dve, y_bias, j)
                        ready(dve, meta_sb, j)
                        for b in range(SB):
                            dve.tensor_scalar(y[:, pj, b], y[:, pj, b],
                                              meta[:, pj, b, bass.ds(e, 1)], k.gates[:, 1:2],
                                              ALU.mult, ALU.mult).then_inc(y_sb, 1)

                tile_pipeline(dve, step)

            @block.tensor
            def _(pe):
                def step(m, par):
                    j, mj, pj = item(m, par, 0)
                    if tile_exists(j):
                        e = expert(pe, j)
                        ready(pe, x_lo_sb, j)
                        for q in range(BANKS):
                            ready(pe, hid_sb, j - 1, BANKS, q + 1)
                            for c in range(q * PER, (q + 1) * PER):
                                n = 0
                                for i in range(KC):
                                    for w, x in ((k.w1_hi, x_hi), (k.w1_hi, x_lo), (k.w1_lo, x_hi)):
                                        mm = pe.matmul(
                                            S[:, q, c % PER * SLOTS:(c % PER + 1) * SLOTS],
                                            w[:, bass.ds(e, 1), i, c * P:(c + 1) * P].rearrange("p a n -> p (a n)"),
                                            x[:, i], start=(n == 0), stop=(n == 3 * KC - 1))
                                        n += 1
                            mm.then_inc(hid_ps, 1)
                    j, mj, pj = item(m, par, 1)
                    if tile_exists(j):
                        ready(pe, row_ld[pj], mj, 16)
                        ready(pe, x_lo_sb, j - 1)
                        for i in range(KC):
                            for b in range(SB):
                                mm = pe.transpose(A[:, i * SLOTS + b * P:i * SLOTS + (b + 1) * P],
                                                  x_row[:, pj, b, i * P:(i + 1) * P], k.ident[:])
                        mm.then_inc(xt_done, 1)
                    j, mj, pj = item(m, par, -1)
                    if tile_exists(j):
                        e = expert(pe, j)
                        ready(pe, h_lo_sb, j, BANKS)
                        ready(pe, y_bias, j - 2)
                        for b in range(SB):
                            n = 0
                            for c in range(HC):
                                for h, w in ((h_hi, k.w2_hi), (h_hi, k.w2_lo), (h_lo, k.w2_hi)):
                                    mm = pe.matmul(Y[pj][:, b * D:(b + 1) * D], h[:, pj, c, b * P:(b + 1) * P],
                                                   w[:, bass.ds(e, 1), c, :].rearrange("p a n -> p (a n)"),
                                                   start=(n == 0), stop=(n == 3 * HC - 1))
                                    n += 1
                        mm.then_inc(y_ps, 1)

                tile_pipeline(pe, step)


class Kept:
    pass


def gated_cross_attention_and_experts(nc, t, out):
    k = Kept()
    with ExitStack() as ctx:
        def sb(name, shape, dt=F32):
            return ctx.enter_context(nc.sbuf_tensor(name, shape, dt))

        k.banks = ctx.enter_context(nc.psum_tensor("banks", [P, 8, 512], F32))
        k.w1_hi, k.w1_lo = (sb(n, [P, E, KC, HID], F16) for n in ("w1_hi", "w1_lo"))
        k.w2_hi, k.w2_lo = (sb(n, [P, E, HC, D], F16) for n in ("w2_hi", "w2_lo"))
        k.ident = sb("ident", [P, P])
        k.ones = sb("ones", [P, P], BF16)
        k.before = sb("before", [P, P], BF16)
        k.bias_t = sb("bias_t", [P, E * HC + 3 * KC])
        k.gates = sb("gates", [P, 2])
        k.expert_no = sb("expert_no", [P, E])
        k.tile_no = sb("tile_no", [P, MAX_TILES + 1])
        k.region_of = sb("region_of", [P, E])
        k.upto = sb("upto", [P, E, E])
        k.seen = sb("seen", [P, E], BF16)
        k.pad_rows = sb("pad_rows", [P, SB, ROW])
        k.row = sb("row", [P, 2, 2, ROW])
        k.pos = sb("pos", [P, 2, 2, 2], U32)
        k.expert_of = sb("expert_of", [P, MAX_TILES + 1], I32)
        k.row_of = sb("row_of", [P, MAX_TILES + 1], I32)
        k.scat = [ctx.enter_context(nc.semaphore(f"scat{i}")) for i in range(2)]
        k.x_in_ld = [ctx.enter_context(nc.semaphore(f"x_in_ld{i}")) for i in range(2)]
        k.v_placed = [ctx.enter_context(nc.semaphore(f"v_placed{i}")) for i in range(2)]
        routed = nc.dram_tensor("routed", [ROUTED, ROW], F32, kind="Internal").ap()

        with ExitStack() as attn_ctx:
            def sba(name, shape, dt=F32):
                return attn_ctx.enter_context(nc.sbuf_tensor(name, shape, dt))

            k.wq_t = sba("wq_t", [P, KC, D])
            k.wo_t = sba("wo_t", [P, KC, D])
            k.keys_hi, k.keys_lo = (sba(n, [P, BATCH, SCORES], F16) for n in ("keys_hi", "keys_lo"))
            k.v_rows = sba("v_rows", [P, BATCH, PCH, VCOLS])
            k.w_router = sba("w_router", [P, KC, E])
            k.gated_bo = sba("gated_bo", [P, D])
            k.token_no = sba("token_no", [P, TOKENS // P], I32)
            k.x_in = sba("x_in", [P, 2, 2, D])
            k.prob = sba("prob", [P, 2, SCORES])
            k.minus_half = sba("minus_half", [P, 1])
            setup_phase(nc, t, k)
            attention_phase(nc, t, k, out, routed)
        expert_phase(nc, t, k, out, routed)


_INS = ["x", "ctx_1024", "g_xattn", "g_ffn", "L0_xattn_Wq", "L0_xattn_bq", "L0_xattn_Wk", "L0_xattn_bk",
        "L0_xattn_Wv", "L0_xattn_bv", "L0_xattn_Wo", "L0_xattn_bo", "L0_ffn_w_router", "L0_ffn_w1", "L0_ffn_b1",
        "L0_ffn_w2", "L0_ffn_b2"]


def kernel(**inputs):
    import numpy as _np
    import concourse.bacc as _bacc
    from concourse import mybir as _mybir
    from concourse.bass_utils import run_bass_kernel_spmd as _run

    nc = _bacc.Bacc("TRN2", target_bir_lowering=False, num_devices=1)
    arrays, args = {}, {}
    for name in _INS:
        a = _np.ascontiguousarray(inputs[name])
        arrays[f"in_{name}_dram"] = a
        args[name] = nc.dram_tensor(f"in_{name}_dram", a.shape, _mybir.dt.from_np(a.dtype), kind="ExternalInput").ap()
    out = nc.dram_tensor("out_0_dram", (TOKENS + SLOTS, D), F32, kind="ExternalOutput").ap()
    gated_cross_attention_and_experts(nc, args, out)
    r = _run(nc, [arrays], core_ids=[0])
    return r.results[0]["out_0_dram"][0:TOKENS].reshape(BATCH, SEQ, D)
```

```python
from contextlib import ExitStack

import concourse.bass as bass
from concourse import mybir

F32 = mybir.dt.float32
F16 = mybir.dt.float16
BF16 = mybir.dt.bfloat16
I32 = mybir.dt.int32
U32 = mybir.dt.uint32
ALU = mybir.AluOpType
ACT = mybir.ActivationFunctionType
AX = mybir.AxisListType

P = 128
BATCH, SEQ, D = 4, 1024, 256
KEYS = 77
HEADS = 16
DH = D // HEADS
E = 8
HID = 1024
TOKENS = BATCH * SEQ
LN_EPS = 1e-5

KC = D // P
HC = HID // P
PAIR = 2 * P
PAIRS = TOKENS // PAIR
PAIRS_PER_BATCH = SEQ // PAIR
HALF_HEADS = HEADS // KC
SCORES = HEADS * KEYS
QUAD = 4 * KEYS
PCH = -(-SCORES // P)
VW = DH + 1
POOL_PIECES = 4
EARLY_PIECES = 13
LATE_PIECES = 17
VCOLS = 3 * VW

SLOTS = 256
SB = SLOTS // P
MAX_TILES = TOKENS * 2 // SLOTS + E - 1
FULL_TILES = MAX_TILES - 2 * (E - 1)
RUNS = 2 * E
REGION = TOKENS + SLOTS
ROUTED = E * REGION + SLOTS
ROW = D + E + 1
W_SCALE = 64.0


def chunk_heads(c):
    first = P * c // KEYS
    return first, min((P * c + P - 1) // KEYS, HEADS - 1) - first + 1


def chunk_rows(c):
    return min(P, SCORES - P * c)


def value_pieces():
    pieces = []
    for h in range(HEADS):
        row = h * KEYS
        while row < (h + 1) * KEYS:
            c = row // P
            n = min((c + 1) * P, (h + 1) * KEYS) - row
            pieces.append((h, c, row - h * KEYS, row - c * P, n))
            row += n
    return pieces


def values_with_ones(k):
    return k.prob[0:KEYS, 1, 0:BATCH * HEADS * VW].rearrange("k (b h w) -> k b h w", b=BATCH, h=HEADS)


def place_values(eng, k, pieces, placed):
    for h, c, key, part, n in pieces:
        col = (h - chunk_heads(c)[0]) * VW
        eng.dma_start(k.v_rows[part:part + n, :, c, col:col + VW],
                      values_with_ones(k)[key:key + n, :, h, :]).then_inc(placed, 16)


def values_placed(eng, k):
    eng.wait_ge(k.v_placed[0], 16 * (len(value_pieces()) - POOL_PIECES))
    eng.wait_ge(k.v_placed[1], 16 * POOL_PIECES)


def ready(eng, sem, item, per=1, part=None):
    value = item * per + (per if part is None else part)
    if isinstance(value, int) and value <= 0:
        return
    eng.wait_ge(sem, value)


def settled(eng, sem, item, per=1, part=None):
    ready(eng, sem, item, per, part)
    eng.nop(nofuse=True)


def exists(pair):
    return not isinstance(pair, int) or 0 <= pair < PAIRS


def follows(pair):
    return not isinstance(pair, int) or 0 < pair < PAIRS


def before_pairs(m, par):
    return isinstance(m, int) and 2 * m + par == -1


def pipeline(eng, step):
    for s in range(-1, 4):
        step(s // 2, s % 2)
    with eng.Fori(2, (PAIRS - 2) // 2) as m:
        for par in range(2):
            step(m, par)
    for s in range(PAIRS - 2, PAIRS + 3):
        step(s // 2, s % 2)


def item(m, par, shift):
    return 2 * m + (par + shift), m + (par + shift) // 2, (par + shift) % 2


def batch_of(m, par, shift):
    return (m + (par + shift) // 2) // (PAIRS_PER_BATCH // 2)


def setup_phase(nc, t, k):
    banks = k.banks
    with ExitStack() as ctx:
        def sb(name, shape, dt=F32):
            return ctx.enter_context(nc.sbuf_tensor(name, shape, dt))

        def sem(name):
            return ctx.enter_context(nc.semaphore(name))

        lent = k.w1_lo[:].rearrange("p e c n -> p (e c n)").bitcast(F32)
        w_raw = lent[:, 0:4 * KC * D].rearrange("p (w c d) -> p w c d", w=4, c=KC)
        wk_t, wv_t = (lent[:, i * KC * D:(i + 1) * KC * D].rearrange("p (c d) -> p c d", c=KC) for i in (4, 5))
        ctx_raw = sb("ctx_raw", [KEYS, BATCH, D])
        ctx_t = sb("ctx_t", [P, KC, BATCH * KEYS])
        key_hi, key_lo = (sb(n, [P, KC, BATCH * KEYS], F16) for n in ("key_hi", "key_lo"))
        bias_rows = sb("bias_rows", [E * HC + 3 * KC, P])
        head_mask = sb("head_mask", [P, HALF_HEADS], F16)
        iota_i = sb("iota_i", [P, E], I32)
        iota_j = sb("iota_j", [P, MAX_TILES + 1], I32)
        bo_b = sb("bo_b", [P, D])
        g_b = sb("g_b", [P, 2])

        v_aug = values_with_ones(k)
        x_rows = t["x"].rearrange("b s d -> (b s) d").rearrange("(j t p) d -> j p t d", t=2, p=P)

        ld_w = [sem(f"ld_w{i}") for i in range(4)]
        ld_ctx, ld_bias, ld_g, ld_bo, ld_wr = (
            sem(n) for n in ("ld_ctx", "ld_bias", "ld_g", "ld_bo", "ld_wr"))
        made = sem("made")
        consts = sem("consts")
        wt_done = sem("wt_done")
        wt_sb = sem("wt_sb")
        ctx_done, ctx_sb = sem("ctx_done"), sem("ctx_sb")
        bias_done, bias_sb = sem("bias_done"), sem("bias_sb")
        key_done, key_sb = sem("key_done"), sem("key_sb")
        v_done, v_sb = sem("v_done"), sem("v_sb")
        tanh_sb = sem("tanh_sb")
        spread, key_lo_sb = sem("spread"), sem("key_lo_sb")
        n_bias = E * HC

        weights = ["Wk", "Wv", "Wq", "Wo"]
        turned = [wk_t, wv_t, k.wq_t, k.wo_t]

        def spread_keys(eng, half, out, c, batches):
            for b in batches:
                eng.tensor_tensor(
                    out[:, b, c * HALF_HEADS * KEYS:(c + 1) * HALF_HEADS * KEYS].rearrange("p (h k) -> p h k", k=KEYS),
                    half[:, c, b * KEYS:(b + 1) * KEYS].unsqueeze(1).to_broadcast([P, HALF_HEADS, KEYS]),
                    head_mask[:].unsqueeze(2).to_broadcast([P, HALF_HEADS, KEYS]),
                    ALU.mult).then_inc(spread, 1)

        POOL_BATCHES = BATCH // 2

        with nc.Block() as block:
            @block.sync
            def _(sp):
                sp.dma_start(ctx_raw[:], t["ctx_1024"].rearrange("b k d -> k b d")).then_inc(ld_ctx, 16)
                for i, w in enumerate(weights):
                    sp.dma_start(w_raw[:, i], t["L0_xattn_" + w].rearrange("(c p) i -> p c i", p=P)).then_inc(ld_w[i], 16)
                for j in range(2):
                    sp.dma_start(k.x_in[:, j], x_rows[j]).then_inc(k.x_in_ld[j], 16)
                sp.wait_ge(consts, 2)
                sp.wait_ge(v_sb, BATCH // 2)
                place_values(sp, k, value_pieces()[POOL_PIECES:EARLY_PIECES], k.v_placed[0])

            @block.scalar
            def _(act):
                act.dma_start(bias_rows[0:n_bias, :],
                              t["L0_ffn_b1"].rearrange("e (m p) -> (e m) p", p=P)).then_inc(ld_bias, 16)
                for i, b in enumerate(("bq", "bk", "bv")):
                    act.dma_start(bias_rows[n_bias + KC * i:n_bias + KC * (i + 1), :],
                                  t["L0_xattn_" + b].rearrange("(c p) -> c p", p=P)).then_inc(ld_bias, 16)
                act.wait_ge(ctx_done, 1)
                for c in range(KC):
                    act.activation(ctx_t[:, c], banks[:, c, 0:BATCH * KEYS], ACT.Copy).then_inc(ctx_sb, 1)
                act.wait_ge(bias_done, 1)
                act.activation(k.bias_t[:], banks[:, 2, 0:n_bias + 3 * KC], ACT.Copy).then_inc(bias_sb, 1)
                act.wait_ge(bias_sb, 1)
                for c in range(KC):
                    act.wait_ge(key_done, c + 1)
                    act.activation(key_hi[:, c], banks[:, c, 0:BATCH * KEYS], ACT.Identity,
                                   bias=k.bias_t[:, n_bias + KC + c:n_bias + KC + c + 1]).then_inc(key_sb, 1)
                act.wait_ge(ld_g, 32)
                act.activation(k.gates[:], g_b[:], ACT.Tanh).then_inc(tanh_sb, 1)
                act.wait_ge(ld_wr, 16)
                act.wait_ge(k.xt_ps, 1)
                act.activation(k.xn_t[:].rearrange("p c n -> p (c n)"), banks[:, 3], ACT.Copy).then_inc(k.xt_sb, 1)
                act.wait_ge(k.q_ps, 1)
                for c in range(KC):
                    act.activation(k.q_hi[:, 0, c], banks[:, 2, c * PAIR:(c + 1) * PAIR], ACT.Identity,
                                   bias=k.bias_t[:, n_bias + c:n_bias + c + 1]).then_inc(k.q_sb, 1)

            @block.gpsimd
            def _(pool):
                pool.memset(k.ident[:], 0.0).then_inc(made, 1)
                pool.memset(k.ones[:], 1.0).then_inc(made, 1)
                pool.memset(head_mask[:], 1.0).then_inc(made, 1)
                pool.wait_ge(made, 3)
                pool.affine_select(out=k.ident[:], in_=k.ident[:], compare_op=ALU.not_equal, fill=1.0, base=0,
                                   pattern=[[-1, P]], channel_multiplier=1).then_inc(made, 1)
                pool.affine_select(out=k.before[:], in_=k.ones[:], compare_op=ALU.is_gt, fill=0.0, base=0,
                                   pattern=[[1, P]], channel_multiplier=-1).then_inc(made, 1)
                pool.affine_select(out=head_mask[:], in_=head_mask[:], compare_op=ALU.is_ge, fill=0.0, base=0,
                                   pattern=[[-DH, HALF_HEADS]], channel_multiplier=1).then_inc(made, 1)
                pool.dma_start(g_b[:, 0:1], t["g_xattn"].partition_broadcast(P)).then_inc(ld_g, 16)
                pool.dma_start(g_b[:, 1:2], t["g_ffn"].partition_broadcast(P)).then_inc(ld_g, 16)
                pool.dma_start(bo_b[:], t["L0_xattn_bo"].partition_broadcast(P)).then_inc(ld_bo, 16)
                pool.dma_start(k.w_router[:], t["L0_ffn_w_router"].rearrange("(c p) e -> p c e", p=P)).then_inc(ld_wr, 16)
                pool.wait_ge(made, 6)
                pool.affine_select(out=head_mask[:], in_=head_mask[:], compare_op=ALU.is_ge, fill=0.0, base=DH - 1,
                                   pattern=[[DH, HALF_HEADS]], channel_multiplier=-1).then_inc(made, 1)
                pool.iota(iota_i[:], pattern=[[1, E]], base=0, channel_multiplier=0).then_inc(made, 1)
                pool.iota(iota_j[:], pattern=[[1, MAX_TILES + 1]], base=0, channel_multiplier=0).then_inc(made, 1)
                pool.iota(k.token_no[:], pattern=[[P, TOKENS // P]], base=0, channel_multiplier=1).then_inc(made, 1)
                pool.memset(k.minus_half[:], -0.5).then_inc(made, 1)
                pool.memset(k.seen[:], 0.0).then_inc(made, 1)
                pool.memset(k.pad_rows[:], 0.0).then_inc(made, 1)
                pool.wait_ge(made, 13)
                pool.iota(k.pad_rows[:, :, ROW - 1:ROW].bitcast(I32), pattern=[[P, SB], [1, 1]], base=TOKENS,
                          channel_multiplier=1).then_inc(made, 1)
                pool.wait_ge(made, 14)
                pool.wait_ge(k.stats1, 4)
                pool.tensor_scalar(k.var_eps[:, 0], k.mv[:, 0, :, 1:2], LN_EPS, None, ALU.add).then_inc(k.factors1, 1)
                pool.wait_ge(k.factors1, 1)
                pool.tensor_tensor(k.rstd[:, 0], k.var_eps[:, 0],
                                   k.minus_half[:].unsqueeze(2).to_broadcast([P, 2, 1]), ALU.pow)\
                    .then_inc(k.factors1, 1)
                for c in range(KC):
                    pool.wait_ge(key_lo_sb, c + 1)
                    spread_keys(pool, key_lo, k.keys_lo, c, range(POOL_BATCHES, BATCH))
                pool.wait_ge(consts, 2)
                pool.wait_ge(v_sb, BATCH // 2)
                place_values(pool, k, value_pieces()[0:POOL_PIECES], k.v_placed[1])

            @block.vector
            def _(dve):
                dve.memset(k.v_rows[:], 0.0).then_inc(consts, 1)
                dve.memset(v_aug, 1.0).then_inc(consts, 1)
                dve.wait_ge(made, 9)
                dve.tensor_copy(k.expert_no[:], iota_i[:]).then_inc(consts, 1)
                dve.tensor_copy(k.tile_no[:], iota_j[:]).then_inc(consts, 1)
                dve.wait_ge(consts, 4)
                dve.tensor_scalar(k.region_of[:], k.expert_no[:], float(REGION), None, ALU.mult).then_inc(consts, 1)

                def copy_turned(i):
                    dve.wait_ge(wt_done, i + 1)
                    dve.tensor_copy(turned[i][:].rearrange("p c o -> p (c o)"), banks[:, 4 + i, :]).then_inc(wt_sb, 1)

                def key_low_half(c):
                    dve.wait_ge(key_sb, c + 1)
                    dve.scalar_tensor_tensor(key_lo[:, c], banks[:, c, 0:BATCH * KEYS],
                                             k.bias_t[:, n_bias + KC + c:n_bias + KC + c + 1], key_hi[:, c],
                                             ALU.add, ALU.subtract).then_inc(key_lo_sb, 1)

                for i in range(2):
                    copy_turned(i)
                dve.wait_ge(k.x_in_ld[0], 16)
                for tile in range(2):
                    dve.bn_stats(k.stats[:, 0, tile], k.x_in[:, 0, tile]).then_inc(k.stats1, 1)
                dve.wait_ge(k.stats1, 2)
                for tile in range(2):
                    dve.bn_aggr(k.mv[:, 0, tile], k.stats[:, 0, tile]).then_inc(k.stats1, 1)
                key_low_half(0)
                spread_keys(dve, key_hi, k.keys_hi, 0, range(0, 2))
                dve.wait_ge(k.factors1, 2)
                for tile in range(2):
                    dve.tensor_scalar(k.x_norm[:, tile], k.x_in[:, 0, tile], k.mv[:, 0, tile, 0:1],
                                      k.rstd[:, 0, tile, 0:1], ALU.subtract, ALU.mult).then_inc(k.norm1, 1)
                key_low_half(1)
                copy_turned(2)
                spread_keys(dve, key_hi, k.keys_hi, 0, range(2, BATCH))
                for pair in range(BATCH // 2):
                    dve.wait_ge(v_done, pair + 1)
                    dve.tensor_copy(v_aug[:, 2 * pair:2 * pair + 2, :, 0:DH].rearrange("k b h d -> k (b h) d"),
                                    banks[0:KEYS, 4 + pair, :].rearrange("k (a d) -> k a d", d=DH)).then_inc(v_sb, 1)
                    spread_keys(dve, key_hi, k.keys_hi, 1, range(2 * pair, 2 * pair + 2))
                copy_turned(3)
                for c in range(KC):
                    dve.wait_ge(key_lo_sb, c + 1)
                    spread_keys(dve, key_lo, k.keys_lo, c, range(0, POOL_BATCHES))
                dve.wait_ge(k.q_sb, KC)
                for c in range(KC):
                    dve.scalar_tensor_tensor(k.q_lo[:, 0, c], banks[:, 2, c * PAIR:(c + 1) * PAIR],
                                             k.bias_t[:, n_bias + c:n_bias + c + 1], k.q_hi[:, 0, c],
                                             ALU.add, ALU.subtract).then_inc(k.q_lo_sb, 1)
                dve.wait_ge(tanh_sb, 1)
                dve.wait_ge(ld_bo, 16)
                dve.tensor_scalar(k.gated_bo[:], bo_b[:], k.gates[:, 0:1], None, ALU.mult).then_inc(consts, 1)

            @block.tensor
            def _(pe):
                pe.wait_ge(made, 4)
                pe.wait_ge(ld_ctx, 16)
                for c in range(KC):
                    for b in range(BATCH):
                        mm = pe.transpose(banks[:, c, b * KEYS:(b + 1) * KEYS], ctx_raw[:, b, c * P:(c + 1) * P],
                                          k.ident[0:KEYS, 0:KEYS])
                mm.then_inc(ctx_done, 1)

                def turn_weight(i):
                    pe.wait_ge(ld_w[i], 16)
                    for c in range(KC):
                        for o in range(KC):
                            mm = pe.transpose(banks[:, 4 + i, c * D + o * P:c * D + (o + 1) * P],
                                              w_raw[:, i, o, c * P:(c + 1) * P], k.ident[:])
                    mm.then_inc(wt_done, 1)

                for i in range(2):
                    turn_weight(i)
                pe.wait_ge(ld_bias, 64)
                pe.transpose(banks[:, 2, 0:n_bias + 3 * KC], bias_rows[:],
                             k.ident[0:n_bias + 3 * KC, 0:n_bias + 3 * KC]).then_inc(bias_done, 1)
                pe.wait_ge(ctx_sb, KC)
                pe.wait_ge(wt_sb, 1)
                for o in range(KC):
                    for c in range(KC):
                        mm = pe.matmul(banks[:, o, 0:BATCH * KEYS], wk_t[:, c, o * P:(o + 1) * P], ctx_t[:, c],
                                       start=(c == 0), stop=(c == KC - 1))
                    mm.then_inc(key_done, 1)
                turn_weight(2)
                pe.wait_ge(k.norm1, 2)
                for c in range(KC):
                    for tile in range(2):
                        mm = pe.transpose(banks[:, 3, c * PAIR + tile * P:c * PAIR + (tile + 1) * P],
                                          k.x_norm[:, tile, c * P:(c + 1) * P], k.ident[:])
                mm.then_inc(k.xt_ps, 1)
                pe.wait_ge(wt_sb, 2)
                for pair in range(BATCH // 2):
                    for j in range(2):
                        b = 2 * pair + j
                        for c in range(KC):
                            mm = pe.matmul(banks[0:KEYS, 4 + pair, j * D:(j + 1) * D],
                                           ctx_t[:, c, b * KEYS:(b + 1) * KEYS], wv_t[:, c],
                                           start=(c == 0), stop=(c == KC - 1))
                    mm.then_inc(v_done, 1)
                turn_weight(3)
                pe.wait_ge(k.xt_sb, 1)
                pe.wait_ge(wt_sb, 3)
                pe.wait_ge(bias_sb, 1)
                for o in range(KC):
                    for c in range(KC):
                        mm = pe.matmul(banks[:, 2, o * PAIR:(o + 1) * PAIR], k.wq_t[:, c, o * P:(o + 1) * P],
                                       k.xn_t[:, c], start=(c == 0), stop=(c == KC - 1))
                mm.then_inc(k.q_ps, 1)


def attention_phase(nc, t, k, out, routed):
    S, A, B, C, DB = k.banks[:, 0:4], k.banks[:, 4], k.banks[:, 5], k.banks[:, 6], k.banks[:, 7]
    n_bias = E * HC
    HALF_LAYER = KC * HID // 2
    NT = MAX_TILES + 1
    x_rows = t["x"].rearrange("b s d -> (b s) d").rearrange("(j t p) d -> j p t d", t=2, p=P)
    out_rows = out[0:TOKENS, :].rearrange("(j t p) d -> j p t d", t=2, p=P)

    with ExitStack() as ctx:
        def sb(name, shape, dt=F32):
            return ctx.enter_context(nc.sbuf_tensor(name, shape, dt))

        def sem(name):
            return ctx.enter_context(nc.semaphore(name))

        lent = [w[:, E - 1].rearrange("p c n -> p (c n)").bitcast(F32) for w in (k.w2_hi, k.w2_lo)]
        x_res = lent[0].rearrange("p (b t d) -> p b t d", b=2, t=2)
        attn_t, x2_t = (lent[1][:, i * KC * PAIR:(i + 1) * KC * PAIR].rearrange("p (c n) -> p c n", c=KC)
                        for i in range(2))
        x_in, prob, row, pos, scat, x_in_ld = k.x_in, k.prob, k.row, k.pos, k.scat, k.x_in_ld
        q_hi, q_lo, x_norm, xn_t = k.q_hi, k.q_lo, k.x_norm, k.xn_t
        stats, mv, var_eps, rstd = k.stats, k.mv, k.var_eps, k.rstd
        prob_t = sb("prob_t", [P, PCH, P])
        attn = sb("attn", [P, 2, D])
        stage = sb("stage", [P, 2, HALF_LAYER])
        top = sb("top", [P, 2, HEADS])
        den = sb("den", [P, 2, HEADS])
        neg_mean = sb("neg_mean", [P, 2, 1])
        offset = sb("offset", [P, 2, 1])
        logits = sb("logits", [P, 2, E])
        best = sb("best", [P, 2, E])
        best_i = sb("best_i", [P, 2, E], U32)
        l_shift = sb("l_shift", [P, 2, E])
        l_exp = sb("l_exp", [P, 2, E])
        l_sum = sb("l_sum", [P, 2])
        l_rec = sb("l_rec", [P, 2])
        share = sb("share", [P, 2, 2])
        best_f = sb("best_f", [P, 2, 2])
        mask = sb("mask", [P, 2, 2, E])
        weighed = sb("weighed", [P, 2, 2, E])
        chosen = sb("chosen", [P, 2, E], BF16)
        count_i = sb("count_i", [P, 2, E], I32)
        tiles_i = sb("tiles_i", [P, 2, E], I32)
        run_length = sb("run_length", [P, 2, E])
        lengths = run_length[:].rearrange("p a e -> p (a e)")
        run_end = sb("run_end", [P, RUNS])
        run_base = sb("run_base", [P, RUNS + 1])
        jump = sb("jump", [P, RUNS])
        skip = sb("skip", [P, RUNS])
        plan_place = attn_t.rearrange("p c n -> p (c n)")
        packed_row, run_of, skipped, late, row_f, expert_f = (
            plan_place[:, i * NT:(i + 1) * NT] for i in range(6))
        upto, upto_runs = (x_norm[:, i].rearrange("p (n r) -> p n r", r=RUNS) for i in range(2))
        past, past_skip = (prob[:, i, 0:NT * RUNS].rearrange("p (n r) -> p n r", r=RUNS) for i in range(2))
        place = sb("place", [P, 2, E])
        placed = sb("placed", [P, 2, 2, E])

        x_res_ld = [sem(f"x_res_ld{i}") for i in range(2)]
        x2_st = [sem(f"x2_st{i}") for i in range(2)]
        stage_ld = [sem(f"stage_ld{i}") for i in range(2)]
        stats1, factors1, norm1, xt_ps, xt_sb, q_ps, q_sb, q_lo_sb = (
            k.stats1, k.factors1, k.norm1, k.xt_ps, k.xt_sb, k.q_ps, k.q_sb, k.q_lo_sb)
        score_ps, x2t_ps, pt_ps, av_ps, logit_ps, ot_ps, wo_ps, rank_ps = (
            sem(n) for n in ("score_ps", "x2t_ps", "pt_ps", "av_ps", "logit_ps", "ot_ps", "wo_ps", "rank_ps"))
        x2t_sb, pt_sb, prob_abs, prob_exp, ot_sb, router_exp, w_hi, norm2 = (
            sem(n) for n in ("x2t_sb", "pt_sb", "prob_abs", "prob_exp", "ot_sb", "router_exp", "w_hi", "norm2"))
        top_sb, shift_sb, den_sb, attn_sb, x2_sb, stats2, router, places, w_scaled = (
            sem(n) for n in ("top_sb", "shift_sb", "den_sb", "attn_sb", "x2_sb", "stats2", "router", "places",
                             "w_scaled"))
        factors2, res_bo, row_sb, w_lo = (sem(n) for n in ("factors2", "res_bo", "row_sb", "w_lo"))
        FACTOR_OPS = (2, 4)
        ROUTER_OPS = 12
        PLACE_OPS = 5
        count_ps, plan_consts, plan = (sem(n) for n in ("count_ps", "plan_consts", "plan"))
        PLAN_OPS = 20

        def staged(m, par):
            return exists(2 * m + par)

        def converted(m, par):
            return staged(m, par) and (not isinstance(m, int) or (m, par) != (E - 1, 1))

        def halves(m, par):
            hi, lo = ((k.w1_hi, k.w1_lo), (k.w2_hi, k.w2_lo))[par]
            return [w[:, bass.ds(m, 1)].rearrange("p a c n -> p (a c n)") for w in (hi, lo)]

        with nc.Block() as block:
            @block.sync
            def _(sp):
                place_values(sp, k, value_pieces()[EARLY_PIECES:LATE_PIECES], k.v_placed[0])

                def step(m, par):
                    j, mj, pj = item(m, par, 2)
                    if exists(j) and exists(j - 2):
                        ready(sp, norm1, j - 2, 2)
                        sp.dma_start(x_in[:, pj], x_rows[bass.ds(j, 1)].rearrange("a p t d -> p (a t) d"))\
                            .then_inc(x_in_ld[pj], 16)
                    if staged(m, par):
                        w = t["L0_ffn_w1"] if par == 0 else t["L0_ffn_w2"]
                        rows = w.shape[1] // 2
                        for half in range(2):
                            ready(sp, w_lo, 2 * m + par - 1, 2, half + 1)
                            sp.dma_start(stage[:, half].rearrange("p (c n) -> p c n", n=w.shape[2]),
                                         w[bass.ds(m, 1), half * rows:(half + 1) * rows].rearrange(
                                             "a (c p) n -> p (a c) n", p=P)).then_inc(stage_ld[half], 16)
                    j, mj, pj = item(m, par, -2)
                    if exists(j):
                        ready(sp, x2_sb, j)
                        sp.dma_start(out_rows[bass.ds(j, 1)].rearrange("a p t d -> p (a t) d"), x_res[:, pj])\
                            .then_inc(x2_st[pj], 16)
                    j, mj, pj = item(m, par, 0)
                    if exists(j):
                        ready(sp, norm2, j - 2, 2)
                        ready(sp, x2_st[pj], mj - 1, 16)
                        sp.dma_start(x_res[:, pj], x_rows[bass.ds(j, 1)].rearrange("a p t d -> p (a t) d"))\
                            .then_inc(x_res_ld[pj], 16)
                    if isinstance(j, int) and j == 0:
                        place_values(sp, k, value_pieces()[LATE_PIECES:], k.v_placed[0])

                pipeline(sp, step)
                sp.dma_start(routed[E * REGION:ROUTED, :].rearrange("(t p) r -> p t r", p=P),
                             k.pad_rows[:]).then_inc(k.pads, 16)
                for i in range(2):
                    sp.wait_ge(x2_st[i], 16 * PAIRS // 2)
                for i in range(2):
                    sp.wait_ge(scat[i], 64 * PAIRS // 2)
                sp.wait_ge(plan, PLAN_OPS)
                sp.wait_ge(wo_ps, PAIRS)
                for tile in range(2):
                    load_rows(sp, k, routed, tile, tile)

            @block.gpsimd
            def _(pool):
                def norm_factors(n, stat, factors, used, j):
                    ready(pool, used, j - 1, 2)
                    settled(pool, stat, j, 4)
                    pool.tensor_scalar(var_eps[:, n], mv[:, n, :, 1:2], LN_EPS, None, ALU.add)\
                        .then_inc(factors, 1)
                    if n == 1:
                        pool.tensor_scalar(neg_mean[:], mv[:, n, :, 0:1], -1.0, None, ALU.mult)\
                            .then_inc(factors, 1)
                    ready(pool, factors, j, FACTOR_OPS[n], FACTOR_OPS[n] // 2)
                    pool.tensor_tensor(rstd[:, n], var_eps[:, n],
                                       k.minus_half[:].unsqueeze(2).to_broadcast([P, 2, 1]), ALU.pow)\
                        .then_inc(factors, 1)
                    if n == 1:
                        ready(pool, factors, j, 4, 3)
                        pool.tensor_tensor(offset[:], neg_mean[:], rstd[:, n], ALU.mult).then_inc(factors, 1)

                def step(m, par):
                    j, mj, pj = item(m, par, -2)
                    if exists(j):
                        norm_factors(1, stats2, factors2, norm2, j)
                    j, mj, pj = item(m, par, -3)
                    if exists(j):
                        ready(pool, router, j, ROUTER_OPS)
                        pool.tensor_tensor(weighed[:], mask[:], share[:].unsqueeze(3).to_broadcast([P, 2, 2, E]),
                                           ALU.mult).then_inc(row_sb, 1)
                        pool.tensor_copy(row[:, pj, :, ROW - 1:ROW].bitcast(I32),
                                         k.token_no[:, bass.ds(2 * j, 2)].unsqueeze(2)).then_inc(row_sb, 1)
                        ready(pool, row_sb, j, 3, 1)
                        pool.tensor_tensor(row[:, pj, :, D:D + E], weighed[:, :, 0], weighed[:, :, 1], ALU.add)\
                            .then_inc(row_sb, 1)
                    j, mj, pj = item(m, par, -3)
                    if exists(j):
                        ready(pool, row_sb, j, 3)
                        settled(pool, places, j, PLACE_OPS, 4)
                        for tile in range(2):
                            for choice in range(2):
                                pool.indirect_dma_start(
                                    routed[:, :], bass.IndirectOffsetOnAxis(ap=pos[:, pj, tile, choice:choice + 1], axis=0),
                                    row[:, pj, tile], None).then_inc(scat[pj], 16)
                    j, mj, pj = item(m, par, 2)
                    if follows(j):
                        norm_factors(0, stats1, factors1, norm1, j)
                    j, mj, pj = item(m, par, -1)
                    if exists(j):
                        ready(pool, x_res_ld[pj], mj, 16)
                        pool.tensor_tensor(x_res[:, pj], x_res[:, pj],
                                           k.gated_bo[:].unsqueeze(1).to_broadcast([P, 2, D]), ALU.add)\
                            .then_inc(res_bo, 1)
                    if converted(m, par):
                        hi, lo = halves(m, par)
                        for half in range(2):
                            cols = slice(half * HALF_LAYER, (half + 1) * HALF_LAYER)
                            ready(pool, w_hi, 2 * m + par, 2, half + 1)
                            pool.tensor_tensor(lo[:, cols], stage[:, half], hi[:, cols], ALU.subtract).then_inc(w_lo, 1)

                pipeline(pool, step)

            @block.scalar
            def _(act):
                def copy_prob_t(j, tile, groups):
                    for g in groups:
                        first, n = ((0, 4), (4, 4), (8, 2))[g]
                        ready(act, pt_ps, 2 * j + tile, 3, g + 1)
                        bank = (A, B, A)[g]
                        if g < 2:
                            act.activation(prob_t[:, first:first + n, :].rearrange("p c n -> p (c n)"),
                                           bank[:, 0:n * P], ACT.Copy).then_inc(pt_sb, 1)
                        else:
                            act.activation(prob_t[:, first, :], bank[:, 0:P], ACT.Copy).then_inc(pt_sb, 1)
                            r = chunk_rows(first + 1)
                            act.activation(prob_t[0:r, first + 1, :], bank[0:r, P:2 * P], ACT.Copy)\
                                .then_inc(pt_sb, 1)

                def absolute_scores(j, tile):
                    ready(act, score_ps, j, 2, tile + 1)
                    ready(act, pt_ps, 2 * (j - 1) + tile, 3)
                    if isinstance(j, int) and 2 * j + tile == 1:
                        values_placed(act, k)
                    act.activation(prob[:, tile].rearrange("p (q n) -> p q n", q=4), S[:, :, 0:QUAD], ACT.Abs)\
                        .then_inc(prob_abs, 1)

                def exponentials(j, tile):
                    ready(act, shift_sb, j, 2, tile + 1)
                    act.activation(prob[:, tile], prob[:, tile], ACT.Exp, scale=DH ** -0.5).then_inc(prob_exp, 1)

                def high_half(m, par, half):
                    hi, lo = halves(m, par)
                    ready(act, w_scaled, 2 * m + par, 2, half + 1)
                    act.activation(hi[:, half * HALF_LAYER:(half + 1) * HALF_LAYER], stage[:, half], ACT.Copy)\
                        .then_inc(w_hi, 1)

                def step(m, par):
                    j, mj, pj = item(m, par, 0)
                    if before_pairs(m, par):
                        absolute_scores(0, 0)
                    elif exists(j) and not before_pairs(m, par - 1):
                        absolute_scores(j, 0)
                    j, mj, pj = item(m, par, -1)
                    if exists(j):
                        ready(act, av_ps, 2 * j)
                        copy_prob_t(j, 1, (0, 1))
                    j, mj, pj = item(m, par, -2)
                    if exists(j):
                        ready(act, factors2, j, FACTOR_OPS[1])
                        ready(act, scat[pj], mj - 1, 64)
                        for tile in range(2):
                            act.activation(row[:, pj, tile, 0:D], x_res[:, pj, tile], ACT.Identity,
                                           scale=rstd[:, 1, tile, 0:1], bias=offset[:, tile, 0:1]).then_inc(norm2, 1)
                    j, mj, pj = item(m, par, 1)
                    if follows(j):
                        ready(act, q_ps, j)
                        ready(act, score_ps, j - 2, 2)
                        for c in range(KC):
                            act.activation(q_hi[:, pj, c], C[:, c * PAIR:(c + 1) * PAIR], ACT.Identity,
                                           bias=k.bias_t[:, n_bias + c:n_bias + c + 1]).then_inc(q_sb, 1)
                    j, mj, pj = item(m, par, -1)
                    if exists(j):
                        copy_prob_t(j, 1, (2,))
                    j, mj, pj = item(m, par, 0)
                    if exists(j):
                        exponentials(j, 0)
                    if converted(m, par):
                        high_half(m, par, 0)
                    j, mj, pj = item(m, par, 0)
                    if exists(j):
                        absolute_scores(j, 1)
                    j, mj, pj = item(m, par, -2)
                    if exists(j):
                        ready(act, x2t_ps, j)
                        ready(act, logit_ps, j - 1)
                        act.activation(x2_t.rearrange("p c n -> p (c n)"), C, ACT.Copy).then_inc(x2t_sb, 1)
                    j, mj, pj = item(m, par, -1)
                    if exists(j):
                        ready(act, ot_ps, j)
                        ready(act, wo_ps, j - 1)
                        for c in range(KC):
                            act.activation(attn_t[:, c], DB[:, c * PAIR:(c + 1) * PAIR], ACT.Identity,
                                           bias=k.bias_t[:, n_bias + 2 * KC + c:n_bias + 2 * KC + c + 1])\
                                .then_inc(ot_sb, 1)
                    j, mj, pj = item(m, par, 0)
                    if exists(j):
                        ready(act, av_ps, 2 * j - 1)
                        copy_prob_t(j, 0, (0, 1))
                    if converted(m, par):
                        high_half(m, par, 1)
                    if exists(j):
                        copy_prob_t(j, 0, (2,))
                    j, mj, pj = item(m, par, -2)
                    if exists(j):
                        ready(act, router, j, ROUTER_OPS, 4)
                        act.activation(l_exp[:], l_shift[:], ACT.Exp).then_inc(router_exp, 1)
                    j, mj, pj = item(m, par, 0)
                    if exists(j):
                        exponentials(j, 1)
                    j, mj, pj = item(m, par, 2)
                    if follows(j):
                        ready(act, xt_ps, j)
                        ready(act, q_ps, j - 1)
                        act.activation(xn_t[:].rearrange("p c n -> p (c n)"), B, ACT.Copy).then_inc(xt_sb, 1)

                pipeline(act, step)
                act.wait_ge(logit_ps, PAIRS)
                act.wait_ge(norm2, 2 * PAIRS)
                for i in range(2):
                    act.wait_ge(x2_st[i], 16 * PAIRS // 2)
                for half in range(2):
                    high_half(E - 1, 1, half)

            @block.vector
            def _(dve):
                def heads_of(tile):
                    return prob[:, tile].rearrange("p (h k) -> p h k", k=KEYS)

                def top_scores(j, tile):
                    ready(dve, prob_abs, j, 2, tile + 1)
                    dve.tensor_reduce(top[:, tile], heads_of(tile), AX.X, ALU.max).then_inc(top_sb, 1)

                def shift_scores(j, tile):
                    ready(dve, top_sb, j, 2, tile + 1)
                    dve.tensor_tensor(heads_of(tile), heads_of(tile),
                                      top[:, tile].unsqueeze(2).to_broadcast([P, HEADS, KEYS]),
                                      ALU.subtract).then_inc(shift_sb, 1)

                values = DB[:, 0:HEADS * VW].rearrange("p (h w) -> p h w", w=VW)

                def inverse_sums(j, tile):
                    ready(dve, av_ps, j, 2, tile + 1)
                    dve.reciprocal(den[:, tile], values[:, :, DH]).then_inc(den_sb, 1)

                def normalise_attn(j, tile):
                    ready(dve, den_sb, j, 2, tile + 1)
                    ready(dve, ot_ps, j - 1)
                    dve.tensor_tensor(attn[:, tile].rearrange("p (h d) -> p h d", d=DH), values[:, :, 0:DH],
                                      den[:, tile].unsqueeze(2).to_broadcast([P, HEADS, DH]), ALU.mult)\
                        .then_inc(attn_sb, 1)

                def statistics(n, stat, x, j, tile):
                    if tile == 0:
                        ready(dve, stat, j - 1, 4)
                    dve.bn_stats(stats[:, n, tile], x[:, tile]).then_inc(stat, 1)

                def aggregate(n, stat, factors, j):
                    ready(dve, factors, j - 1, FACTOR_OPS[n])
                    settled(dve, stat, j, 4, 2)
                    for tile in range(2):
                        dve.bn_aggr(mv[:, n, tile], stats[:, n, tile]).then_inc(stat, 1)

                def scale_weights(layer, half):
                    ready(dve, stage_ld[half], layer, 16)
                    dve.tensor_scalar(stage[:, half], stage[:, half], W_SCALE, None, ALU.mult).then_inc(w_scaled, 1)

                def route(j, part, wait=None):
                    if part == 1:
                        ready(dve, logit_ps, j)
                    if part == 10:
                        ready(dve, router_exp, j)
                    if wait:
                        (settled if part in (2, 5) else ready)(dve, router, j, ROUTER_OPS, wait)
                    if part == 1:
                        dve.tensor_copy(logits[:].rearrange("p t e -> p (t e)"), C[:, 0:2 * E]).then_inc(router, 1)
                    if part == 2:
                        for tile in range(2):
                            dve.max(best[:, tile], logits[:, tile]).then_inc(router, 1)
                    if part == 4:
                        dve.tensor_tensor(l_shift[:], best[:], best[:, :, 0:1].to_broadcast([P, 2, E]), ALU.subtract)\
                            .then_inc(router, 1)
                    if part == 5:
                        for tile in range(2):
                            dve.max_index(best_i[:, tile], best[:, tile], logits[:, tile]).then_inc(router, 1)
                    if part == 7:
                        dve.tensor_copy(best_f[:], best_i[:, :, 0:2]).then_inc(router, 1)
                    if part == 8:
                        ready(dve, row_sb, j - 1, 3)
                        dve.tensor_tensor(mask[:], k.expert_no[:].unsqueeze(1).unsqueeze(1).to_broadcast([P, 2, 2, E]),
                                          best_f[:].unsqueeze(3).to_broadcast([P, 2, 2, E]), ALU.is_equal)\
                            .then_inc(router, 1)
                    if part == 9:
                        dve.tensor_tensor(chosen[:], mask[:, :, 0], mask[:, :, 1], ALU.add).then_inc(router, 1)
                    if part == 10:
                        dve.tensor_reduce(l_sum[:], l_exp[:], AX.X, ALU.add).then_inc(router, 1)
                    if part == 11:
                        dve.reciprocal(l_rec[:], l_sum[:]).then_inc(router, 1)
                    if part == 12:
                        dve.tensor_tensor(share[:], l_exp[:, :, 0:2], l_rec[:].unsqueeze(2).to_broadcast([P, 2, 2]),
                                          ALU.mult).then_inc(router, 1)

                def step(m, par):
                    here, last, before_last, placed_pair = (
                        exists(2 * m + par + shift) for shift in (0, -1, -2, -3))
                    i0, i1, i2, i3, n1, n2 = (item(m, par, shift)[0] for shift in (0, -1, -2, -3, 1, 2))
                    next_pair, coming = follows(n1), follows(n2)
                    x_coming, x_last = x_in[:, par], x_res[:, 1 - par]

                    if staged(m, par):
                        scale_weights(2 * m + par, 0)
                    if placed_pair:
                        ready(dve, rank_ps, i3)
                        dve.tensor_tensor(place[:], C[:, 0:2 * E].rearrange("p (t e) -> p t e", e=E),
                                          k.region_of[:].unsqueeze(1).to_broadcast([P, 2, E]), ALU.add)\
                            .then_inc(places, 1)
                        dve.tensor_tensor(k.seen[:], k.seen[:], chosen[:, 0], ALU.add).then_inc(places, 1)
                        ready(dve, places, i3, PLACE_OPS, 1)
                        dve.tensor_tensor(placed[:], mask[:], place[:].unsqueeze(2).to_broadcast([P, 2, 2, E]),
                                          ALU.mult).then_inc(places, 1)
                        ready(dve, places, i3, PLACE_OPS, 3)
                        with nc.allow_low_precision(reason="whole numbers below 2**24"):
                            dve.tensor_reduce(pos[:, 1 - par], placed[:], AX.X, ALU.add).then_inc(places, 1)
                        dve.tensor_tensor(k.seen[:], k.seen[:], chosen[:, 1], ALU.add).then_inc(places, 1)
                    if here:
                        top_scores(i0, 0)
                        shift_scores(i0, 0)
                    if coming:
                        ready(dve, x_in_ld[par], item(m, par, 2)[1], 16)
                        statistics(0, stats1, x_coming, n2, 0)
                        statistics(0, stats1, x_coming, n2, 1)
                    if last:
                        inverse_sums(i1, 1)
                    if coming:
                        aggregate(0, stats1, factors1, n2)
                    if next_pair:
                        ready(dve, q_sb, n1, KC)
                        for c in range(KC):
                            dve.scalar_tensor_tensor(q_lo[:, 1 - par, c], C[:, c * PAIR:(c + 1) * PAIR],
                                                     k.bias_t[:, n_bias + c:n_bias + c + 1], q_hi[:, 1 - par, c],
                                                     ALU.add, ALU.subtract).then_inc(q_lo_sb, 1)
                    if last:
                        normalise_attn(i1, 1)
                    if coming:
                        ready(dve, factors1, n2, FACTOR_OPS[0])
                        ready(dve, xt_ps, n2 - 1)
                        for tile in range(2):
                            dve.tensor_scalar(x_norm[:, tile], x_coming[:, tile], mv[:, 0, tile, 0:1],
                                              rstd[:, 0, tile, 0:1], ALU.subtract, ALU.mult).then_inc(norm1, 1)
                    if staged(m, par):
                        scale_weights(2 * m + par, 1)
                    if here:
                        top_scores(i0, 1)
                    if before_last:
                        route(i2, 1)
                    if here:
                        shift_scores(i0, 1)
                    if before_last:
                        route(i2, 2, 1)
                    if before_last:
                        route(i2, 4, 3)
                        route(i2, 5)
                    if last:
                        ready(dve, wo_ps, i1)
                        ready(dve, res_bo, i1)
                        dve.scalar_tensor_tensor(x_last.rearrange("p t d -> p (t d)"), C, k.gates[:, 0:1],
                                                 x_last.rearrange("p t d -> p (t d)"), ALU.mult, ALU.add)\
                            .then_inc(x2_sb, 1)
                    if before_last:
                        route(i2, 7, 6)
                    if last:
                        ready(dve, x2_sb, i1)
                        statistics(1, stats2, x_last, i1, 0)
                    if before_last:
                        route(i2, 8, 7)
                    if last:
                        statistics(1, stats2, x_last, i1, 1)
                    if here:
                        inverse_sums(i0, 0)
                    if before_last:
                        route(i2, 9, 8)
                    if here:
                        normalise_attn(i0, 0)
                    if last:
                        aggregate(1, stats2, factors2, i1)
                    if before_last:
                        route(i2, 10)
                        route(i2, 11, 10)
                        route(i2, 12, 11)

                pipeline(dve, step)

                def done(part):
                    dve.wait_ge(plan, part)

                dve.wait_ge(xt_ps, PAIRS)
                dve.tensor_tensor(upto, k.tile_no[:, 0:RUNS].unsqueeze(2).to_broadcast([P, RUNS, RUNS]),
                                  k.tile_no[:, 0:RUNS].unsqueeze(1).to_broadcast([P, RUNS, RUNS]), ALU.is_ge)\
                    .then_inc(plan_consts, 1)
                dve.tensor_scalar(packed_row[:], k.tile_no[:], float(SLOTS), None, ALU.mult).then_inc(plan_consts, 1)
                dve.tensor_copy(run_base[:, 0:E], k.region_of[:]).then_inc(plan_consts, 1)
                dve.memset(run_base[:, RUNS:RUNS + 1], float(E * REGION)).then_inc(plan_consts, 1)
                dve.wait_ge(count_ps, 1)
                dve.tensor_tensor(k.pad_at[:], C[:, 0:E], k.region_of[:], ALU.add).then_inc(plan, 1)
                dve.tensor_copy(count_i[:, 0], C[:, 0:E]).then_inc(plan, 1)
                dve.tensor_scalar(count_i[:, 1], C[:, 0:E], float(SLOTS - 1), None, ALU.add).then_inc(plan, 1)
                done(3)
                dve.tensor_scalar(tiles_i[:], count_i[:], SLOTS.bit_length() - 1, None, ALU.logical_shift_right)\
                    .then_inc(plan, 1)
                done(4)
                dve.tensor_copy(run_length[:], tiles_i[:]).then_inc(plan, 1)
                done(5)
                dve.tensor_tensor(run_length[:, 1], run_length[:, 1], run_length[:, 0], ALU.subtract).then_inc(plan, 1)
                dve.wait_ge(plan_consts, 4)
                dve.scalar_tensor_tensor(run_base[:, E:RUNS], run_length[:, 0], float(SLOTS), k.region_of[:],
                                         ALU.mult, ALU.add).then_inc(plan, 1)
                done(6)
                dve.tensor_tensor(upto_runs, upto, lengths.unsqueeze(1).to_broadcast([P, RUNS, RUNS]), ALU.mult)\
                    .then_inc(plan, 1)
                done(7)
                dve.tensor_tensor(jump[:], run_base[:, 1:RUNS + 1], run_base[:, 0:RUNS], ALU.subtract)\
                    .then_inc(plan, 1)
                done(8)
                dve.tensor_reduce(run_end[:], upto_runs, AX.X, ALU.add).then_inc(plan, 1)
                done(9)
                dve.scalar_tensor_tensor(skip[:], lengths, -float(SLOTS), jump[:], ALU.mult, ALU.add)\
                    .then_inc(plan, 1)
                done(10)
                dve.wait_ge(pt_ps, 3 * 2 * PAIRS)
                dve.tensor_tensor(past, k.tile_no[:].unsqueeze(2).to_broadcast([P, NT, RUNS]),
                                  run_end[:].unsqueeze(1).to_broadcast([P, NT, RUNS]), ALU.is_ge).then_inc(plan, 1)
                done(12)
                dve.tensor_tensor(past_skip, past, skip[:].unsqueeze(1).to_broadcast([P, NT, RUNS]), ALU.mult)\
                    .then_inc(plan, 1)
                dve.tensor_reduce(run_of[:], past, AX.X, ALU.add).then_inc(plan, 1)
                done(13)
                dve.tensor_reduce(skipped[:], past_skip, AX.X, ALU.add).then_inc(plan, 1)
                done(14)
                dve.tensor_scalar(late[:], run_of[:], float(E), -float(E), ALU.is_ge, ALU.mult).then_inc(plan, 1)
                done(15)
                dve.tensor_tensor(row_f[:], packed_row[:], skipped[:], ALU.add).then_inc(plan, 1)
                done(16)
                dve.tensor_tensor(expert_f[:], run_of[:], late[:], ALU.add).then_inc(plan, 1)
                done(17)
                dve.tensor_scalar(k.row_of[:], row_f[:], float(E * REGION), None, ALU.min).then_inc(plan, 1)
                done(18)
                dve.tensor_scalar(k.expert_of[:], expert_f[:], float(E - 1), None, ALU.min).then_inc(plan, 1)
                done(PLAN_OPS)
                hi, lo = halves(E - 1, 1)
                for half in range(2):
                    cols = slice(half * HALF_LAYER, (half + 1) * HALF_LAYER)
                    ready(dve, w_hi, 2 * E - 1, 2, half + 1)
                    dve.tensor_tensor(lo[:, cols], stage[:, half], hi[:, cols], ALU.subtract).then_inc(w_lo, 1)

            @block.tensor
            def _(pe):
                def scores(m, par, tile):
                    j, mj, pj = item(m, par, 0)
                    b = batch_of(m, par, 0)
                    ready(pe, q_lo_sb, j, KC)
                    ready(pe, prob_abs, 2 * j + tile - 1)
                    for q in range(4):
                        c = q // 2
                        for n, (rows, keys) in enumerate(((q_hi, k.keys_hi), (q_hi, k.keys_lo), (q_lo, k.keys_hi))):
                            mm = pe.matmul(S[:, q, 0:QUAD], rows[:, pj, c, tile * P:(tile + 1) * P],
                                           keys[:, bass.ds(b, 1), q * QUAD:(q + 1) * QUAD].rearrange("p a n -> p (a n)"),
                                           start=(n == 0), stop=(n == 2))
                    mm.then_inc(score_ps, 1)

                def turn_probs(j, tile, groups):
                    for g in groups:
                        if g == 2:
                            ready(pe, pt_sb, 2 * j + tile, 4, 1)
                        for i, c in enumerate((range(0, 4), range(4, 8), range(8, PCH))[g]):
                            r = chunk_rows(c)
                            mm = pe.transpose((A, B, A)[g][0:r, i * P:(i + 1) * P], prob[:, tile, c * P:c * P + r],
                                              k.ident[:])
                        mm.then_inc(pt_ps, 1)

                def values(m, par, shift, tile):
                    j, mj, pj = item(m, par, shift)
                    b = batch_of(m, par, shift)
                    if isinstance(j, int) and 2 * j + tile == 0:
                        values_placed(pe, k)
                    for c in range(PCH):
                        ready(pe, pt_sb, 2 * j + tile, 4, (1, 1, 1, 1, 2, 2, 2, 2, 3, 4)[c])
                        first, n = chunk_heads(c)
                        r = chunk_rows(c)
                        mm = pe.matmul(DB[:, first * VW:(first + n) * VW], prob_t[0:r, c, :],
                                       k.v_rows[0:r, bass.ds(b, 1), c, 0:n * VW].rearrange("p a n -> p (a n)"),
                                       start=(c == 0), stop=(c == PCH - 1), skip_group_check=True)
                    mm.then_inc(av_ps, 1)

                def turn_pair(dst, src, done):
                    for c in range(KC):
                        for tile in range(2):
                            mm = pe.transpose(dst[:, c * PAIR + tile * P:c * PAIR + (tile + 1) * P],
                                              src[:, tile, c * P:(c + 1) * P], k.ident[:])
                    mm.then_inc(done, 1)

                def step(m, par):
                    here, last, before_last, placed_pair = (
                        exists(2 * m + par + shift) for shift in (0, -1, -2, -3))
                    i0, i1, i2, i3, n1, n2 = (item(m, par, shift)[0] for shift in (0, -1, -2, -3, 1, 2))
                    next_pair, coming = follows(n1), follows(n2)
                    if before_pairs(m, par):
                        scores(0, 0, 0)
                    elif here and not before_pairs(m, par - 1):
                        scores(m, par, 0)
                    if placed_pair:
                        ready(pe, router, i3, ROUTER_OPS, 9)
                        ready(pe, places, i3 - 1, PLACE_OPS)
                        if exists(i3 + 1):
                            ready(pe, x2_sb, i3 + 1)
                        pe.matmul(C[:, 0:E], k.before[:], chosen[:, 0], start=True, stop=False)
                        pe.matmul(C[:, 0:E], k.ones[:], k.seen[:], start=False, stop=True)
                        pe.matmul(C[:, E:2 * E], k.before[:], chosen[:, 1], start=True, stop=False)
                        pe.matmul(C[:, E:2 * E], k.ones[:], k.seen[:], start=False, stop=False)
                        pe.matmul(C[:, E:2 * E], k.ones[:], chosen[:, 0], start=False, stop=True)\
                            .then_inc(rank_ps, 1)
                    if last:
                        ready(pe, prob_exp, i1, 2, 2)
                        ready(pe, pt_sb, 2 * i1, 4)
                        if exists(i1 + 2):
                            ready(pe, xt_sb, i1 + 2)
                        turn_probs(i1, 1, (0, 1))
                    if next_pair:
                        ready(pe, xt_sb, n1)
                        ready(pe, x2_sb, n1 - 3)
                        ready(pe, places, n1 - 4, PLACE_OPS, 1)
                        for o in range(KC):
                            for c in range(KC):
                                mm = pe.matmul(C[:, o * PAIR:(o + 1) * PAIR], k.wq_t[:, c, o * P:(o + 1) * P],
                                               xn_t[:, c], start=(c == 0), stop=(c == KC - 1))
                        mm.then_inc(q_ps, 1)
                    if last:
                        turn_probs(i1, 1, (2,))
                        ready(pe, attn_sb, i1, 2, 1)
                        values(m, par, -1, 1)
                    if here:
                        scores(m, par, 1)
                    if before_last:
                        ready(pe, norm2, i2, 2)
                        if exists(i2 + 3):
                            ready(pe, q_lo_sb, i2 + 3, KC)
                        ready(pe, places, i2 - 1, PLACE_OPS, 1)
                        turn_pair(C, row[:, par, :, 0:D], x2t_ps)
                    if last:
                        ready(pe, attn_sb, i1, 2)
                        turn_pair(DB, attn, ot_ps)
                    if here:
                        ready(pe, prob_exp, i0, 2, 1)
                        ready(pe, pt_sb, 2 * i0 - 1, 4)
                        ready(pe, xt_sb, n1 if exists(n1) else PAIRS - 1)
                        turn_probs(i0, 0, (0,))
                    if before_last:
                        ready(pe, x2t_sb, i2)
                        for tile in range(2):
                            for c in range(KC):
                                mm = pe.matmul(C[:, tile * E:(tile + 1) * E], x2_t[:, c, tile * P:(tile + 1) * P],
                                               k.w_router[:, c], start=(c == 0), stop=(c == KC - 1))
                        mm.then_inc(logit_ps, 1)
                    if here:
                        turn_probs(i0, 0, (1,))
                    if last:
                        ready(pe, ot_sb, i1, KC)
                        if next_pair:
                            ready(pe, q_lo_sb, n1, KC)
                        ready(pe, router, i2, ROUTER_OPS, 1)
                        for tile in range(2):
                            for c in range(KC):
                                mm = pe.matmul(C[:, tile * D:(tile + 1) * D], attn_t[:, c, tile * P:(tile + 1) * P],
                                               k.wo_t[:, c], start=(c == 0), stop=(c == KC - 1))
                        mm.then_inc(wo_ps, 1)
                    if here:
                        turn_probs(i0, 0, (2,))
                        ready(pe, ot_sb, i0 - 1, KC)
                        values(m, par, 0, 0)
                    if coming:
                        ready(pe, norm1, n2, 2)
                        ready(pe, xt_sb, n2 - 1)
                        ready(pe, pt_sb, 2 * (n2 - 2), 4, 2)
                        turn_pair(B, x_norm, xt_ps)

                pipeline(pe, step)
                pe.wait_ge(places, PLACE_OPS * PAIRS)
                pe.matmul(C[:, 0:E], k.ones[:], k.seen[:], start=True, stop=True).then_inc(count_ps, 1)


LOOP_TILES = range(4, MAX_TILES - 3 - (MAX_TILES - 3) % 2)
FULL_TILES_LOADED = 4
assert FULL_TILES_LOADED <= min(FULL_TILES, LOOP_TILES.start)


def tile_exists(tile):
    return not isinstance(tile, int) or 0 <= tile < MAX_TILES


def tile_pipeline(eng, step):
    for s in range(-2, LOOP_TILES.start):
        step(s // 2, s % 2)
    with eng.Fori(LOOP_TILES.start // 2, LOOP_TILES.stop // 2) as m:
        for par in range(2):
            step(m, par)
    for s in range(LOOP_TILES.stop, MAX_TILES + 2):
        step(s // 2, s % 2)


def expert_phase(nc, t, k, out, routed):
    S, A = k.banks[:, 0:4], k.banks[:, 4]
    Y = [k.banks[:, 6], k.banks[:, 7]]
    BANKS = 4
    PER = HC // BANKS

    with ExitStack() as ctx:
        def sb(name, shape, dt=F32):
            return ctx.enter_context(nc.sbuf_tensor(name, shape, dt))

        def sem(name):
            return ctx.enter_context(nc.semaphore(name))

        meta = sb("meta", [P, 2, SB, E + 1])
        x_hi = sb("x_hi", [P, KC, SLOTS], F16)
        x_lo = sb("x_lo", [P, KC, SLOTS], F16)
        hid = sb("hid", [P, HC, SLOTS])
        h_hi = sb("h_hi", [P, 2, HC, SLOTS], F16)
        h_lo = sb("h_lo", [P, 2, HC, SLOTS], F16)
        y = sb("y", [P, 2, SB, D])
        b2_b = sb("b2_b", [P, E, D])
        b2_ld = sem("b2_ld")
        x_row, row_ld = k.x_row, k.row_ld
        added = [sem(f"added{i}") for i in range(2)]
        xt_done, x_hi_sb, x_lo_sb = sem("xt_done"), sem("x_hi_sb"), sem("x_lo_sb")
        hid_ps, hid_sb, h_hi_sb, h_lo_sb = (sem(n) for n in ("hid_ps", "hid_sb", "h_hi_sb", "h_lo_sb"))
        y_ps, y_bias, y_sb, meta_sb = (sem(n) for n in ("y_ps", "y_bias", "y_sb", "meta_sb"))

        def expert(eng, tile):
            return eng.value_load(k.expert_of[0:1, bass.ds(tile, 1)], min_val=0, max_val=E - 1)

        with nc.Block() as block:
            @block.sync
            def _(sp):
                def step(m, par):
                    j, mj, pj = item(m, par, 2)
                    if isinstance(j, int) and j == FULL_TILES_LOADED:
                        sp.wait_ge(k.pads, 16 * (E + 1))
                    if tile_exists(j) and tile_exists(j - 2):
                        ready(sp, xt_done, j - 2)
                        ready(sp, meta_sb, j - 2)
                        load_rows(sp, k, routed, j, pj)
                    if isinstance(m, int) and 2 * m + par == -1:
                        sp.dma_start(b2_b[:].rearrange("p e d -> p (e d)"),
                                     t["L0_ffn_b2"].rearrange("e d -> (e d)").partition_broadcast(P)).then_inc(b2_ld, 16)
                    if isinstance(m, int) and 2 * m + par == 0:
                        for e in range(E):
                            at = sp.value_load(k.pad_at[0:1, e:e + 1], min_val=0, max_val=E * REGION - SLOTS)
                            sp.dma_start(routed[bass.ds(at, SLOTS), :].rearrange("(t p) r -> p t r", p=P),
                                         k.pad_rows[:]).then_inc(k.pads, 16)

                tile_pipeline(sp, step)

            @block.gpsimd
            def _(pool):
                def step(m, par):
                    j, mj, pj = item(m, par, -2)
                    if tile_exists(j):
                        settled(pool, added[1 - pj], mj - (pj == 0), 16 * SB)
                        for b in range(SB):
                            settled(pool, y_sb, j, SB, b + 1)
                            pool.indirect_dma_start(
                                out[:, :], bass.IndirectOffsetOnAxis(ap=meta[:, pj, b, E:E + 1].bitcast(U32), axis=0),
                                y[:, pj, b], None, compute_op=ALU.add).then_inc(added[pj], 16)
                    j, mj, pj = item(m, par, 0)
                    if tile_exists(j):
                        ready(pool, added[pj], mj - 1, 16 * SB)
                        ready(pool, y_sb, j - 2, SB)
                        settled(pool, row_ld[pj], mj, 16)
                        pool.tensor_copy(meta[:, pj], x_row[:, pj, :, D:ROW]).then_inc(meta_sb, 1)

                tile_pipeline(pool, step)
                for i in range(2):
                    pool.wait_ge(added[i], 16 * SB * ((MAX_TILES + 1 - i) // 2))

            @block.scalar
            def _(act):
                def step(m, par):
                    j, mj, pj = item(m, par, 0)
                    if tile_exists(j):
                        e = expert(act, j)
                        for q in range(BANKS):
                            ready(act, hid_ps, j, BANKS, q + 1)
                            ready(act, h_lo_sb, j - 1, BANKS, q + 1)
                            for c in range(q * PER, (q + 1) * PER):
                                ins = act.activation(hid[:, c], S[:, q, c % PER * SLOTS:(c % PER + 1) * SLOTS],
                                                     ACT.Gelu_apprx_tanh, bias=k.bias_t[:, bass.ds(e * HC + c, 1)],
                                                     scale=1.0 / W_SCALE)
                            ins.then_inc(hid_sb, 1)
                    j, mj, pj = item(m, par, 1)
                    if tile_exists(j):
                        ready(act, xt_done, j)
                        ready(act, hid_ps, j - 1, BANKS)
                        ready(act, x_lo_sb, j - 1)
                        act.activation(x_hi[:].rearrange("p c n -> p (c n)"), A, ACT.Copy).then_inc(x_hi_sb, 1)

                tile_pipeline(act, step)

            @block.vector
            def _(dve):
                def step(m, par):
                    j, mj, pj = item(m, par, 0)
                    if tile_exists(j):
                        for q in range(BANKS):
                            part = slice(q * PER, (q + 1) * PER)
                            ready(dve, hid_sb, j, BANKS, q + 1)
                            ready(dve, y_ps, j - 2)
                            dve.tensor_copy(h_hi[:, pj, part], hid[:, part]).then_inc(h_hi_sb, 1)
                            ready(dve, h_hi_sb, j, BANKS, q + 1)
                            dve.tensor_tensor(h_lo[:, pj, part], hid[:, part], h_hi[:, pj, part], ALU.subtract)\
                                .then_inc(h_lo_sb, 1)
                    j, mj, pj = item(m, par, 1)
                    if tile_exists(j):
                        ready(dve, x_hi_sb, j)
                        dve.tensor_tensor(x_lo[:].rearrange("p c n -> p (c n)"), A,
                                          x_hi[:].rearrange("p c n -> p (c n)"), ALU.subtract).then_inc(x_lo_sb, 1)
                    j, mj, pj = item(m, par, -1)
                    if tile_exists(j):
                        e = expert(dve, j)
                        ready(dve, y_ps, j)
                        if isinstance(j, int) and j == 0:
                            dve.wait_ge(b2_ld, 16)
                        ready(dve, added[pj], mj - 1, 16 * SB)
                        ready(dve, meta_sb, j)
                        for b in range(SB):
                            dve.scalar_tensor_tensor(y[:, pj, b], Y[pj][:, b * D:(b + 1) * D], 1.0 / W_SCALE,
                                                     b2_b[:, bass.ds(e, 1), :].rearrange("p a d -> p (a d)"),
                                                     ALU.mult, ALU.add).then_inc(y_bias, 1)
                            ready(dve, y_bias, j, SB, b + 1)
                            dve.tensor_scalar(y[:, pj, b], y[:, pj, b],
                                              meta[:, pj, b, bass.ds(e, 1)], k.gates[:, 1:2],
                                              ALU.mult, ALU.mult).then_inc(y_sb, 1)

                tile_pipeline(dve, step)

            @block.tensor
            def _(pe):
                def step(m, par):
                    j, mj, pj = item(m, par, 0)
                    if tile_exists(j):
                        e = expert(pe, j)
                        ready(pe, x_lo_sb, j)
                        for q in range(BANKS):
                            ready(pe, hid_sb, j - 1, BANKS, q + 1)
                            for c in range(q * PER, (q + 1) * PER):
                                n = 0
                                for i in range(KC):
                                    for w, x in ((k.w1_hi, x_hi), (k.w1_hi, x_lo), (k.w1_lo, x_hi)):
                                        mm = pe.matmul(
                                            S[:, q, c % PER * SLOTS:(c % PER + 1) * SLOTS],
                                            w[:, bass.ds(e, 1), i, c * P:(c + 1) * P].rearrange("p a n -> p (a n)"),
                                            x[:, i], start=(n == 0), stop=(n == 3 * KC - 1))
                                        n += 1
                            mm.then_inc(hid_ps, 1)
                    j, mj, pj = item(m, par, 1)
                    if tile_exists(j):
                        ready(pe, row_ld[pj], mj, 16)
                        ready(pe, x_lo_sb, j - 1)
                        for i in range(KC):
                            for b in range(SB):
                                mm = pe.transpose(A[:, i * SLOTS + b * P:i * SLOTS + (b + 1) * P],
                                                  x_row[:, pj, b, i * P:(i + 1) * P], k.ident[:])
                        mm.then_inc(xt_done, 1)
                    j, mj, pj = item(m, par, -1)
                    if tile_exists(j):
                        e = expert(pe, j)
                        ready(pe, h_lo_sb, j, BANKS)
                        ready(pe, y_bias, j - 2, SB)
                        for b in range(SB):
                            n = 0
                            for c in range(HC):
                                for h, w in ((h_hi, k.w2_hi), (h_hi, k.w2_lo), (h_lo, k.w2_hi)):
                                    mm = pe.matmul(Y[pj][:, b * D:(b + 1) * D], h[:, pj, c, b * P:(b + 1) * P],
                                                   w[:, bass.ds(e, 1), c, :].rearrange("p a n -> p (a n)"),
                                                   start=(n == 0), stop=(n == 3 * HC - 1))
                                    n += 1
                        mm.then_inc(y_ps, 1)

                tile_pipeline(pe, step)


class Kept:
    pass


def load_rows(sp, k, routed, tile, par):
    at = sp.value_load(k.row_of[0:1, bass.ds(tile, 1)], min_val=0, max_val=E * REGION)
    sp.dma_start(k.x_row[:, par], routed[bass.ds(at, SLOTS), :].rearrange("(t p) r -> p t r", p=P))\
        .then_inc(k.row_ld[par], 16)


def gated_cross_attention_and_experts(nc, t, out):
    k = Kept()
    with ExitStack() as ctx:
        def sb(name, shape, dt=F32):
            return ctx.enter_context(nc.sbuf_tensor(name, shape, dt))

        k.banks = ctx.enter_context(nc.psum_tensor("banks", [P, 8, 512], F32))
        k.w1_hi, k.w1_lo = (sb(n, [P, E, KC, HID], F16) for n in ("w1_hi", "w1_lo"))
        k.w2_hi, k.w2_lo = (sb(n, [P, E, HC, D], F16) for n in ("w2_hi", "w2_lo"))
        k.ident = sb("ident", [P, P])
        k.ones = sb("ones", [P, P], BF16)
        k.before = sb("before", [P, P], BF16)
        k.bias_t = sb("bias_t", [P, E * HC + 3 * KC])
        k.gates = sb("gates", [P, 2])
        k.expert_no = sb("expert_no", [P, E])
        k.tile_no = sb("tile_no", [P, MAX_TILES + 1])
        k.region_of = sb("region_of", [P, E])
        k.seen = sb("seen", [P, E], BF16)
        k.pad_rows = sb("pad_rows", [P, SB, ROW])
        k.row = sb("row", [P, 2, 2, ROW])
        k.pos = sb("pos", [P, 2, 2, 2], U32)
        k.pad_at = sb("pad_at", [P, E], I32)
        k.expert_of = sb("expert_of", [P, MAX_TILES + 1], I32)
        k.row_of = sb("row_of", [P, MAX_TILES + 1], I32)
        k.x_row = sb("x_row", [P, 2, SB, ROW])
        k.row_ld = [ctx.enter_context(nc.semaphore(f"row_ld{i}")) for i in range(2)]
        k.pads = ctx.enter_context(nc.semaphore("pads"))
        k.scat = [ctx.enter_context(nc.semaphore(f"scat{i}")) for i in range(2)]
        k.x_in_ld = [ctx.enter_context(nc.semaphore(f"x_in_ld{i}")) for i in range(2)]
        k.v_placed = [ctx.enter_context(nc.semaphore(f"v_placed{i}")) for i in range(2)]
        routed = nc.dram_tensor("routed", [ROUTED, ROW], F32, kind="Internal").ap()

        with ExitStack() as attn_ctx:
            def sba(name, shape, dt=F32):
                return attn_ctx.enter_context(nc.sbuf_tensor(name, shape, dt))

            k.wq_t, k.wo_t = (k.x_row[:].rearrange("p i b r -> p (i b r)")[:, i * KC * D:(i + 1) * KC * D].rearrange(
                "p (c n) -> p c n", c=KC) for i in range(2))
            k.keys_hi, k.keys_lo = (sba(n, [P, BATCH, SCORES], F16) for n in ("keys_hi", "keys_lo"))
            k.v_rows = sba("v_rows", [P, BATCH, PCH, VCOLS])
            k.w_router = sba("w_router", [P, KC, E])
            k.gated_bo = sba("gated_bo", [P, D])
            k.token_no = sba("token_no", [P, TOKENS // P], I32)
            k.x_in = sba("x_in", [P, 2, 2, D])
            k.prob = sba("prob", [P, 2, SCORES])
            k.minus_half = sba("minus_half", [P, 1])
            k.q_hi, k.q_lo = (sba(n, [P, 2, KC, PAIR], F16) for n in ("q_hi", "q_lo"))
            k.x_norm = sba("x_norm", [P, 2, D])
            k.xn_t = sba("xn_t", [P, KC, PAIR])
            k.stats = sba("stats", [P, 2, 2, 6])
            k.mv = sba("mv", [P, 2, 2, 2])
            k.var_eps = sba("var_eps", [P, 2, 2, 1])
            k.rstd = sba("rstd", [P, 2, 2, 1])
            k.stats1, k.factors1, k.norm1, k.xt_ps, k.xt_sb, k.q_ps, k.q_sb, k.q_lo_sb = (
                attn_ctx.enter_context(nc.semaphore(n))
                for n in ("stats1", "factors1", "norm1", "xt_ps", "xt_sb", "q_ps", "q_sb", "q_lo_sb"))
            setup_phase(nc, t, k)
            attention_phase(nc, t, k, out, routed)
        expert_phase(nc, t, k, out, routed)


_INS = ["x", "ctx_1024", "g_xattn", "g_ffn", "L0_xattn_Wq", "L0_xattn_bq", "L0_xattn_Wk", "L0_xattn_bk",
        "L0_xattn_Wv", "L0_xattn_bv", "L0_xattn_Wo", "L0_xattn_bo", "L0_ffn_w_router", "L0_ffn_w1", "L0_ffn_b1",
        "L0_ffn_w2", "L0_ffn_b2"]


def kernel(**inputs):
    import numpy as _np
    import concourse.bacc as _bacc
    from concourse import mybir as _mybir
    from concourse.bass_utils import run_bass_kernel_spmd as _run

    nc = _bacc.Bacc("TRN2", target_bir_lowering=False, num_devices=1)
    arrays, args = {}, {}
    for name in _INS:
        a = _np.ascontiguousarray(inputs[name])
        arrays[f"in_{name}_dram"] = a
        args[name] = nc.dram_tensor(f"in_{name}_dram", a.shape, _mybir.dt.from_np(a.dtype), kind="ExternalInput").ap()
    out = nc.dram_tensor("out_0_dram", (TOKENS + SLOTS, D), F32, kind="ExternalOutput").ap()
    gated_cross_attention_and_experts(nc, args, out)
    r = _run(nc, [arrays], core_ids=[0])
    return r.results[0]["out_0_dram"][0:TOKENS].reshape(BATCH, SEQ, D)
```
